# Optimizing a Trainium2 kernel written in Bass

```python
import numpy as np
import jax
import jax.numpy as jnp

def _softmax(x, axis=-1):
    return jax.nn.softmax(x, axis=axis)

def _gelu(x):
    return jax.nn.gelu(x, approximate=True)

def _silu(x):
    return jax.nn.silu(x)

def _sigmoid(x):
    return jax.nn.sigmoid(x)

def _layernorm(x, axis=-1, eps=1e-05):
    m = jnp.mean(x, axis=axis, keepdims=True)
    v = jnp.var(x, axis=axis, keepdims=True)
    return (x - m) / jnp.sqrt(v + eps)

def _scatter_add(tgt, idx, src, axis=0):
    return tgt.at[idx].add(src)

def _segment_sum(src, seg, n):
    return jax.ops.segment_sum(src, seg, n)
kernel_name = 'mk_seq_preln_d2_jaxref_r8_a792a7'

def setup_inputs(seed: int=0):
    np.random.seed(seed)
    _w = jnp.asarray

    def _L0_attn_setup():
        import jax, jax.numpy as jnp
        import numpy as np
        from jax import lax
        D_MODEL = 128
        B, T = (4, 256)
        LN_EPS = 1e-05

        def _ln(x, w, b):
            mu = jnp.mean(x, axis=-1, keepdims=True)
            var = jnp.mean((x - mu) ** 2, axis=-1, keepdims=True)
            return (x - mu) * lax.rsqrt(var + LN_EPS) * w + b

        def _wkv(u, k, v):
            Bb, Tt, C = k.shape

            def step(carry, kv):
                aa, bb = carry
                kk, vv = kv
                p = jnp.maximum(bb, u + kk)
                e1 = jnp.exp(bb - p)
                e2 = jnp.exp(u + kk - p)
                out = (e1 * aa + e2 * vv) / (e1 + e2)
                p2 = jnp.maximum(bb, kk)
                e1b = jnp.exp(bb - p2)
                e2b = jnp.exp(kk - p2)
                return ((e1b * aa + e2b * vv, p2 + jnp.log(e1b + e2b)), out)
            init = (jnp.zeros((Bb, C), k.dtype), jnp.zeros((Bb, C), k.dtype))
            _, outs = lax.scan(step, init, (jnp.swapaxes(k, 0, 1), jnp.swapaxes(v, 0, 1)))
            return jnp.swapaxes(outs, 0, 1)
        key = jax.random.key(seed)
        ks = jax.random.split(key, 12)
        C = D_MODEL
        s = 0.02
        return {'x': jax.random.normal(ks[0], (B, T, C), jnp.float32), 'time_decay': jax.random.normal(ks[1], (C,), jnp.float32), 'time_first': jax.random.normal(ks[2], (C,), jnp.float32) * 0.5, 'time_shift': jax.random.normal(ks[3], (1, 1, C), jnp.float32) * 0.1, 'Wk': jax.random.normal(ks[4], (C, C), jnp.float32) * s, 'Wv': jax.random.normal(ks[5], (C, C), jnp.float32) * s, 'Wr': jax.random.normal(ks[6], (C, C), jnp.float32) * s, 'Wck': jax.random.normal(ks[7], (4 * C, C), jnp.float32) * s, 'Wcv': jax.random.normal(ks[8], (C, 4 * C), jnp.float32) * s, 'Wcr': jax.random.normal(ks[9], (C, C), jnp.float32) * s, 'ln1_w': jnp.ones((C,), jnp.float32), 'ln1_b': jnp.zeros((C,), jnp.float32), 'ln2_w': jnp.ones((C,), jnp.float32), 'ln2_b': jnp.zeros((C,), jnp.float32)}
    _L0_attn_in = _L0_attn_setup()

    def _L0_ffn_setup():
        import jax, jax.numpy as jnp
        import numpy as np
        D_IN, D_HID = (128, 512)

        def _ternary(key, shape):
            return jax.random.randint(key, shape, -1, 2).astype(jnp.float32)

        def _tlin(x, w, s):
            return jnp.einsum('bsi,oi->bso', x, w) * s
        key = jax.random.key(seed)
        ks = jax.random.split(key, 12)
        inv = lambda fan: 1.0 / np.sqrt(fan).astype(np.float32)
        return {'x': jax.random.normal(ks[0], (4, 256, D_IN), dtype=jnp.float32), 'w1_w': _ternary(ks[1], (D_HID, D_IN)), 'w1_s': jax.random.uniform(ks[2], (D_HID,), dtype=jnp.float32) * inv(D_IN), 'w2_w': _ternary(ks[3], (D_HID, D_IN)), 'w2_s': jax.random.uniform(ks[4], (D_HID,), dtype=jnp.float32) * inv(D_IN), 'h1_w': _ternary(ks[5], (D_HID, D_HID)), 'h1_s': jax.random.uniform(ks[6], (D_HID,), dtype=jnp.float32) * inv(D_HID), 'h2_w': _ternary(ks[7], (D_HID, D_HID)), 'h2_s': jax.random.uniform(ks[8], (D_HID,), dtype=jnp.float32) * inv(D_HID), 'w3_w': _ternary(ks[9], (D_IN, D_HID)), 'w3_s': jax.random.uniform(ks[10], (D_IN,), dtype=jnp.float32) * inv(D_HID)}
    _L0_ffn_in = _L0_ffn_setup()

    def _L1_attn_setup():
        import jax, jax.numpy as jnp
        import numpy as np
        B, S, D = (2, 256, 128)
        H, DH = (16, 64)
        SCALE = DH ** (-0.5)
        key = jax.random.key(seed)
        ks = jax.random.split(key, 5)

        def w(k, shape):
            return jax.random.normal(k, shape, dtype=jnp.float32) * 0.02
        return {'x': jax.random.normal(ks[0], (B, S, D), dtype=jnp.float32), 'Wq': w(ks[1], (D, H * DH)), 'Wk': w(ks[2], (D, H * DH)), 'Wv': w(ks[3], (D, H * DH)), 'Wo': w(ks[4], (H * DH, D)), 'bo': jnp.zeros((D,), dtype=jnp.float32)}
    _L1_attn_in = _L1_attn_setup()

    def _L1_ffn_setup():
        import jax, jax.numpy as jnp
        import numpy as np
        DIM = 128
        DEPTH = 6
        HEADS = 16
        DIM_HEAD = 64
        WINDOW = 32
        INNER = HEADS * DIM_HEAD
        DIM_INNER = int(DIM * 4 * 2 / 3)
        QK_SCALE = 8.0

        def shift_tokens(t):
            a, s = jnp.split(t, 2, -1)
            s = jnp.pad(s, ((0, 0), (1, 0), (0, 0)))[:, :-1]
            return jnp.concatenate([a, s], -1)

        def l2norm(t):
            return t / jnp.maximum(jnp.linalg.norm(t, axis=-1, keepdims=True), 1e-12)

        def rotate_half(x):
            x1, x2 = jnp.split(x, 2, -1)
            return jnp.concatenate([-x2, x1], -1)

        def rotary_tables(n):
            half = jnp.arange(0, DIM_HEAD, 2, dtype=jnp.float32)
            inv_freq = 1.0 / 10000.0 ** (half / DIM_HEAD)
            t = jnp.arange(n, dtype=jnp.float32)
            freqs = t[:, None] * inv_freq[None, :]
            freqs = jnp.concatenate([freqs, freqs], -1)
            base_scale = (half + 0.4 * DIM_HEAD) / (1.4 * DIM_HEAD)
            power = (t - n // 2) / (WINDOW // 2)
            scale = base_scale[None, :] ** power[:, None]
            scale = jnp.concatenate([scale, scale], -1)
            return (freqs, scale)

        def local_attention(q, k, v):
            b, h, n, d = q.shape
            w = WINDOW
            nw = n // w
            bq = q.reshape(b, h, nw, w, d)
            bk = k.reshape(b, h, nw, w, d)
            bv = v.reshape(b, h, nw, w, d)

            def look(t):
                p = jnp.pad(t, ((0, 0), (0, 0), (1, 0), (0, 0), (0, 0)))
                return jnp.concatenate([p[:, :, :nw], p[:, :, 1:]], axis=3)
            bk2, bv2 = (look(bk), look(bv))
            seq = jnp.arange(n).reshape(nw, w)
            seq_p = jnp.pad(seq, ((1, 0), (0, 0)), constant_values=-1)
            jt = jnp.concatenate([seq_p[:nw], seq_p[1:]], axis=1)
            it = seq[:, :, None]
            jb = jt[:, None, :]
            mask = (it < jb) | (it > jb + w) | (jb == -1)
            sim = jnp.einsum('bhwie,bhwje->bhwij', bq, bk2) * QK_SCALE
            sim = jnp.where(mask, -jnp.finfo(sim.dtype).max, sim)
            attn = jax.nn.softmax(sim, -1)
            out = jnp.einsum('bhwij,bhwje->bhwie', attn, bv2)
            return out.reshape(b, h, n, d)

        def attn_layer(x, Wqkv, qs, ksc, Wo):
            b, n, _ = x.shape
            qkv = x @ Wqkv
            q, k, v = jnp.split(qkv, 3, -1)
            sh = lambda t: t.reshape(b, n, HEADS, DIM_HEAD).transpose(0, 2, 1, 3)
            q, k, v = (sh(q), sh(k), sh(v))
            q = l2norm(q) * qs
            k = l2norm(k) * ksc
            freqs, scale = rotary_tables(n)
            cos, sin = (jnp.cos(freqs), jnp.sin(freqs))
            q = q * cos * scale + rotate_half(q) * sin * scale
            inv = 1.0 / scale
            k = k * cos * inv + rotate_half(k) * sin * inv
            out = local_attention(q, k, v)
            out = out.transpose(0, 2, 1, 3).reshape(b, n, INNER)
            return out @ Wo

        def ffn_layer(x, g, bln, W1, b1, W2, b2):
            mu = x.mean(-1, keepdims=True)
            var = ((x - mu) ** 2).mean(-1, keepdims=True)
            xn = (x - mu) / jnp.sqrt(var + 1e-05) * g + bln
            hg = xn @ W1 + b1
            a, gate = jnp.split(hg, 2, -1)
            return a * jax.nn.gelu(gate, approximate=False) @ W2 + b2
        key = jax.random.key(seed)
        ks = jax.random.split(key, 8)
        B, N = (2, 256)
        init = lambda k, shape: jax.random.normal(k, shape, jnp.float32) * 0.02
        return {'x': jax.random.normal(ks[0], (B, N, DIM), jnp.float32), 'Wqkv': init(ks[1], (DEPTH, DIM, 3 * INNER)), 'q_scale': jnp.ones((DEPTH, DIM_HEAD), jnp.float32), 'k_scale': jnp.ones((DEPTH, DIM_HEAD), jnp.float32), 'Wo': init(ks[2], (DEPTH, INNER, DIM)), 'ln_g': jnp.ones((DEPTH, DIM), jnp.float32), 'ln_b': jnp.zeros((DEPTH, DIM), jnp.float32), 'W1': init(ks[3], (DEPTH, DIM, 2 * DIM_INNER)), 'b1': jnp.zeros((DEPTH, 2 * DIM_INNER), jnp.float32), 'W2': init(ks[4], (DEPTH, DIM_INNER, DIM)), 'b2': jnp.zeros((DEPTH, DIM), jnp.float32)}
    _L1_ffn_in = _L1_ffn_setup()
    _d = {'L0_attn_x': _L0_attn_in['x'], 'L0_attn_time_decay': _L0_attn_in['time_decay'], 'L0_attn_time_first': _L0_attn_in['time_first'], 'L0_attn_time_shift': _L0_attn_in['time_shift'], 'L0_attn_Wk': _L0_attn_in['Wk'], 'L0_attn_Wv': _L0_attn_in['Wv'], 'L0_attn_Wr': _L0_attn_in['Wr'], 'L0_attn_Wck': _L0_attn_in['Wck'], 'L0_attn_Wcv': _L0_attn_in['Wcv'], 'L0_attn_Wcr': _L0_attn_in['Wcr'], 'L0_attn_ln1_w': _L0_attn_in['ln1_w'], 'L0_attn_ln1_b': _L0_attn_in['ln1_b'], 'L0_attn_ln2_w': _L0_attn_in['ln2_w'], 'L0_attn_ln2_b': _L0_attn_in['ln2_b'], 'L0_ffn_w1_w': _L0_ffn_in['w1_w'], 'L0_ffn_w1_s': _L0_ffn_in['w1_s'], 'L0_ffn_w2_w': _L0_ffn_in['w2_w'], 'L0_ffn_w2_s': _L0_ffn_in['w2_s'], 'L0_ffn_h1_w': _L0_ffn_in['h1_w'], 'L0_ffn_h1_s': _L0_ffn_in['h1_s'], 'L0_ffn_h2_w': _L0_ffn_in['h2_w'], 'L0_ffn_h2_s': _L0_ffn_in['h2_s'], 'L0_ffn_w3_w': _L0_ffn_in['w3_w'], 'L0_ffn_w3_s': _L0_ffn_in['w3_s'], 'L1_attn_Wq': _L1_attn_in['Wq'], 'L1_attn_Wk': _L1_attn_in['Wk'], 'L1_attn_Wv': _L1_attn_in['Wv'], 'L1_attn_Wo': _L1_attn_in['Wo'], 'L1_attn_bo': _L1_attn_in['bo'], 'L1_ffn_Wqkv': _L1_ffn_in['Wqkv'], 'L1_ffn_q_scale': _L1_ffn_in['q_scale'], 'L1_ffn_k_scale': _L1_ffn_in['k_scale'], 'L1_ffn_Wo': _L1_ffn_in['Wo'], 'L1_ffn_ln_g': _L1_ffn_in['ln_g'], 'L1_ffn_ln_b': _L1_ffn_in['ln_b'], 'L1_ffn_W1': _L1_ffn_in['W1'], 'L1_ffn_b1': _L1_ffn_in['b1'], 'L1_ffn_W2': _L1_ffn_in['W2'], 'L1_ffn_b2': _L1_ffn_in['b2']}
    _x0 = _d['L0_attn_x']
    _d['L0_attn_x'] = jax.random.normal(jax.random.fold_in(jax.random.key(seed), 1), (16, 256, 128), dtype=_x0.dtype)
    del _x0
    return _d

def reference(L0_attn_x, L0_attn_time_decay, L0_attn_time_first, L0_attn_time_shift, L0_attn_Wk, L0_attn_Wv, L0_attn_Wr, L0_attn_Wck, L0_attn_Wcv, L0_attn_Wcr, L0_attn_ln1_w, L0_attn_ln1_b, L0_attn_ln2_w, L0_attn_ln2_b, L0_ffn_w1_w, L0_ffn_w1_s, L0_ffn_w2_w, L0_ffn_w2_s, L0_ffn_h1_w, L0_ffn_h1_s, L0_ffn_h2_w, L0_ffn_h2_s, L0_ffn_w3_w, L0_ffn_w3_s, L1_attn_Wq, L1_attn_Wk, L1_attn_Wv, L1_attn_Wo, L1_attn_bo, L1_ffn_Wqkv, L1_ffn_q_scale, L1_ffn_k_scale, L1_ffn_Wo, L1_ffn_ln_g, L1_ffn_ln_b, L1_ffn_W1, L1_ffn_b1, L1_ffn_W2, L1_ffn_b2):

    def _L0_attn_ref(x, time_decay, time_first, time_shift, Wk, Wv, Wr, Wck, Wcv, Wcr, ln1_w, ln1_b, ln2_w, ln2_b):
        import jax, jax.numpy as jnp
        import numpy as np
        from jax import lax
        D_MODEL = 128
        B, T = (4, 256)
        LN_EPS = 1e-05

        def _ln(x, w, b):
            mu = jnp.mean(x, axis=-1, keepdims=True)
            var = jnp.mean((x - mu) ** 2, axis=-1, keepdims=True)
            return (x - mu) * lax.rsqrt(var + LN_EPS) * w + b

        def _wkv(u, k, v):
            Bb, Tt, C = k.shape

            def step(carry, kv):
                aa, bb = carry
                kk, vv = kv
                p = jnp.maximum(bb, u + kk)
                e1 = jnp.exp(bb - p)
                e2 = jnp.exp(u + kk - p)
                out = (e1 * aa + e2 * vv) / (e1 + e2)
                p2 = jnp.maximum(bb, kk)
                e1b = jnp.exp(bb - p2)
                e2b = jnp.exp(kk - p2)
                return ((e1b * aa + e2b * vv, p2 + jnp.log(e1b + e2b)), out)
            init = (jnp.zeros((Bb, C), k.dtype), jnp.zeros((Bb, C), k.dtype))
            _, outs = lax.scan(step, init, (jnp.swapaxes(k, 0, 1), jnp.swapaxes(v, 0, 1)))
            return jnp.swapaxes(outs, 0, 1)
        Bb, Tt, C = x.shape
        ts = time_shift
        h = _ln(x, ln1_w, ln1_b)
        x_shifted = jnp.concatenate([jnp.broadcast_to(ts, (Bb, 1, C)), h[:, :-1, :]], axis=1)
        xxx = h + (h - x_shifted) * ts
        k = jnp.einsum('btc,oc->bto', xxx, Wk)
        v = jnp.einsum('btc,oc->bto', xxx, Wv)
        r = jax.nn.sigmoid(jnp.einsum('btc,oc->bto', xxx, Wr))
        wkv = _wkv(time_first, k, v)
        x = x + r * wkv
        h2 = _ln(x, ln2_w, ln2_b)
        xx2 = jnp.concatenate([h2[:, -1:, :], h2[:, :-1, :]], axis=1)
        xxx2 = h2 + (xx2 - h2) * ts
        kc = jnp.einsum('btc,oc->bto', xxx2, Wck)
        rc = jax.nn.sigmoid(jnp.einsum('btc,oc->bto', xxx2, Wcr))
        vv = jnp.einsum('bth,ch->btc', jax.nn.relu(kc) ** 2, Wcv)
        return x + rc * vv

    def _L0_ffn_ref(x, w1_w, w1_s, w2_w, w2_s, h1_w, h1_s, h2_w, h2_s, w3_w, w3_s):
        import jax, jax.numpy as jnp
        import numpy as np
        D_IN, D_HID = (128, 512)

        def _ternary(key, shape):
            return jax.random.randint(key, shape, -1, 2).astype(jnp.float32)

        def _tlin(x, w, s):
            return jnp.einsum('bsi,oi->bso', x, w) * s
        h = jax.nn.silu(_tlin(x, w1_w, w1_s)) * _tlin(x, w2_w, w2_s)
        h = jax.nn.gelu(_tlin(h, h1_w, h1_s), approximate=False)
        h = jax.nn.gelu(_tlin(h, h2_w, h2_s), approximate=False)
        return _tlin(h, w3_w, w3_s)

    def _L1_attn_ref(x, Wq, Wk, Wv, Wo, bo):
        import jax, jax.numpy as jnp
        import numpy as np
        B, S, D = (2, 256, 128)
        H, DH = (16, 64)
        SCALE = DH ** (-0.5)
        b, s, _ = x.shape
        q = (x @ Wq).reshape(b, s, H, DH)
        k = (x @ Wk).reshape(b, s, H, DH)
        v = (x @ Wv).reshape(b, s, H, DH)
        scores = jnp.einsum('bqhd,bkhd->bhqk', q, k) * SCALE
        attn = jax.nn.softmax(scores, axis=-1)
        out = jnp.einsum('bhqk,bkhd->bqhd', attn, v).reshape(b, s, H * DH)
        return out @ Wo + bo

    def _L1_ffn_ref(x, Wqkv, q_scale, k_scale, Wo, ln_g, ln_b, W1, b1, W2, b2):
        import jax, jax.numpy as jnp
        import numpy as np
        DIM = 128
        DEPTH = 6
        HEADS = 16
        DIM_HEAD = 64
        WINDOW = 32
        INNER = HEADS * DIM_HEAD
        DIM_INNER = int(DIM * 4 * 2 / 3)
        QK_SCALE = 8.0

        def shift_tokens(t):
            a, s = jnp.split(t, 2, -1)
            s = jnp.pad(s, ((0, 0), (1, 0), (0, 0)))[:, :-1]
            return jnp.concatenate([a, s], -1)

        def l2norm(t):
            return t / jnp.maximum(jnp.linalg.norm(t, axis=-1, keepdims=True), 1e-12)

        def rotate_half(x):
            x1, x2 = jnp.split(x, 2, -1)
            return jnp.concatenate([-x2, x1], -1)

        def rotary_tables(n):
            half = jnp.arange(0, DIM_HEAD, 2, dtype=jnp.float32)
            inv_freq = 1.0 / 10000.0 ** (half / DIM_HEAD)
            t = jnp.arange(n, dtype=jnp.float32)
            freqs = t[:, None] * inv_freq[None, :]
            freqs = jnp.concatenate([freqs, freqs], -1)
            base_scale = (half + 0.4 * DIM_HEAD) / (1.4 * DIM_HEAD)
            power = (t - n // 2) / (WINDOW // 2)
            scale = base_scale[None, :] ** power[:, None]
            scale = jnp.concatenate([scale, scale], -1)
            return (freqs, scale)

        def local_attention(q, k, v):
            b, h, n, d = q.shape
            w = WINDOW
            nw = n // w
            bq = q.reshape(b, h, nw, w, d)
            bk = k.reshape(b, h, nw, w, d)
            bv = v.reshape(b, h, nw, w, d)

            def look(t):
                p = jnp.pad(t, ((0, 0), (0, 0), (1, 0), (0, 0), (0, 0)))
                return jnp.concatenate([p[:, :, :nw], p[:, :, 1:]], axis=3)
            bk2, bv2 = (look(bk), look(bv))
            seq = jnp.arange(n).reshape(nw, w)
            seq_p = jnp.pad(seq, ((1, 0), (0, 0)), constant_values=-1)
            jt = jnp.concatenate([seq_p[:nw], seq_p[1:]], axis=1)
            it = seq[:, :, None]
            jb = jt[:, None, :]
            mask = (it < jb) | (it > jb + w) | (jb == -1)
            sim = jnp.einsum('bhwie,bhwje->bhwij', bq, bk2) * QK_SCALE
            sim = jnp.where(mask, -jnp.finfo(sim.dtype).max, sim)
            attn = jax.nn.softmax(sim, -1)
            out = jnp.einsum('bhwij,bhwje->bhwie', attn, bv2)
            return out.reshape(b, h, n, d)

        def attn_layer(x, Wqkv, qs, ksc, Wo):
            b, n, _ = x.shape
            qkv = x @ Wqkv
            q, k, v = jnp.split(qkv, 3, -1)
            sh = lambda t: t.reshape(b, n, HEADS, DIM_HEAD).transpose(0, 2, 1, 3)
            q, k, v = (sh(q), sh(k), sh(v))
            q = l2norm(q) * qs
            k = l2norm(k) * ksc
            freqs, scale = rotary_tables(n)
            cos, sin = (jnp.cos(freqs), jnp.sin(freqs))
            q = q * cos * scale + rotate_half(q) * sin * scale
            inv = 1.0 / scale
            k = k * cos * inv + rotate_half(k) * sin * inv
            out = local_attention(q, k, v)
            out = out.transpose(0, 2, 1, 3).reshape(b, n, INNER)
            return out @ Wo

        def ffn_layer(x, g, bln, W1, b1, W2, b2):
            mu = x.mean(-1, keepdims=True)
            var = ((x - mu) ** 2).mean(-1, keepdims=True)
            xn = (x - mu) / jnp.sqrt(var + 1e-05) * g + bln
            hg = xn @ W1 + b1
            a, gate = jnp.split(hg, 2, -1)
            return a * jax.nn.gelu(gate, approximate=False) @ W2 + b2
        for i in range(DEPTH):
            x = attn_layer(shift_tokens(x), Wqkv[i], q_scale[i], k_scale[i], Wo[i]) + x
            x = ffn_layer(shift_tokens(x), ln_g[i], ln_b[i], W1[i], b1[i], W2[i], b2[i]) + x
        return x
    x = L0_attn_x
    x = x + _L0_attn_ref(_layernorm(x, axis=-1), L0_attn_time_decay, L0_attn_time_first, L0_attn_time_shift, L0_attn_Wk, L0_attn_Wv, L0_attn_Wr, L0_attn_Wck, L0_attn_Wcv, L0_attn_Wcr, L0_attn_ln1_w, L0_attn_ln1_b, L0_attn_ln2_w, L0_attn_ln2_b)
    x = x + _L0_ffn_ref(_layernorm(x, axis=-1), L0_ffn_w1_w, L0_ffn_w1_s, L0_ffn_w2_w, L0_ffn_w2_s, L0_ffn_h1_w, L0_ffn_h1_s, L0_ffn_h2_w, L0_ffn_h2_s, L0_ffn_w3_w, L0_ffn_w3_s)
    x = x + _L1_attn_ref(_layernorm(x, axis=-1), L1_attn_Wq, L1_attn_Wk, L1_attn_Wv, L1_attn_Wo, L1_attn_bo)
    x = x + _L1_ffn_ref(_layernorm(x, axis=-1), L1_ffn_Wqkv, L1_ffn_q_scale, L1_ffn_k_scale, L1_ffn_Wo, L1_ffn_ln_g, L1_ffn_ln_b, L1_ffn_W1, L1_ffn_b1, L1_ffn_W2, L1_ffn_b2)
    return x

_drawn_inputs = setup_inputs


def setup_inputs(seed=0):
    import zlib

    import numpy as np

    out = dict(_drawn_inputs(seed))
    spreads = {'L0_attn_ln1_w': (1.0, 0.2),
     'L0_attn_ln1_b': (0.0, 0.1),
     'L0_attn_ln2_w': (1.0, 0.2),
     'L0_attn_ln2_b': (0.0, 0.1),
     'L1_attn_bo': (0.0, 0.1),
     'L1_ffn_q_scale': (1.0, 0.2),
     'L1_ffn_k_scale': (1.0, 0.2),
     'L1_ffn_ln_g': (1.0, 0.2),
     'L1_ffn_ln_b': (0.0, 0.1),
     'L1_ffn_b1': (0.0, 0.1),
     'L1_ffn_b2': (0.0, 0.1)}
    factors = {}
    for name, (base, spread) in spreads.items():
        noise = np.random.default_rng([zlib.crc32(name.encode()), seed]).standard_normal(out[name].shape)
        drawn = base * np.exp(spread * noise) if base else spread * noise
        out[name] = jnp.asarray(drawn.astype(out[name].dtype))
    for name, factor in factors.items():
        out[name] = (out[name] * factor).astype(out[name].dtype)
    return out
```

```python
import concourse.bass as bass
from concourse import mybir
from contextlib import ExitStack

F32 = mybir.dt.float32
F32R = mybir.dt.float32r
BF16 = mybir.dt.bfloat16
ACT = mybir.ActivationFunctionType
ALU = mybir.AluOpType
AXX = mybir.AxisListType.X

P = 128
C = 128
SEQS, T = 16, 256
NT = SEQS * T // P
TPS = T // P
H, DH = 16, 64
PAIRS = H // 2
INNER = H * DH
HID = 512
HB = HID // P
LAYERS = 6
WIN = 32
NW = T // WIN
WPT = P // WIN
FF = int(C * 4 * 2 / 3)
FBLK = [min(P, FF - c * P) for c in range(-(-FF // P))]
EPS = 1e-5
MASKED = -1.0e30
EXP_SET = "natural_log_exp_and_others"


class Chain:

    def __init__(self, eng, sem, per_step, step):
        self.eng, self.sem, self.base, self.per_step, self.n = eng, sem, step * per_step, per_step, 0

    def __call__(self, ins):
        self.n += 1
        ins.then_inc(self.sem, 1)
        self.eng.wait_ge(self.sem, self.base + self.n)

    def end(self):
        assert self.n == self.per_step, (self.n, self.per_step)
LOADS_A, LOADS_B, LOADS_C, LOADS_CONST, CONSTS = 3, 4, 4, 6, 5
PHASES = 4


def build(nc, dram, out):
    ctx = ExitStack()
    with ctx:
        def sb(name, shape, dt=F32):
            return ctx.enter_context(nc.sbuf_tensor(name, shape, dt))

        def sem(name):
            return ctx.enter_context(nc.semaphore(name))

        bank = [ctx.enter_context(nc.psum_tensor(f"bank{i}", [P, 512], F32)) for i in range(8)]

        x_all = sb("x_all", [P, NT, C])
        ident = sb("ident", [P, P])
        ident_bf = sb("ident_bf", [P, P], BF16)
        mask_bf = sb("mask_bf", [P, TPS, 8, 2 * WIN], BF16)
        ones_row = sb("ones_row", [1, P])
        mean_mat = sb("mean_mat", [P, P])
        rope = sb("rope", [P, TPS, 4, DH])
        rope_d = sb("rope_d", [P, 2, TPS, 4, DH])
        m_vo = sb("m_vo", [P, 2, H, C])
        wvt = sb("wvt", [P, PAIRS, C])
        wo = sb("wo", [P, PAIRS, C])
        wqk_stage = sb("wqk_stage", [P, 2 * INNER])
        wqk_split = sb("wqk_split", [P, 2, 2, 2 * INNER], F32R)
        x_split = sb("x_split", [P, 2, T], F32R)
        w1 = sb("w1", [P, 2 * FF])
        w2 = sb("w2", [P, len(FBLK), C])
        cols_d = sb("cols_d", [P, 2 + 2 * len(FBLK)])
        b2 = sb("b2", [1, C])
        bo = sb("bo", [1, C])
        qk_scale = sb("qk_scale", [P, 2 * DH])

        ARENA = 27500
        arena = sb("arena", [P, ARENA])

        class Local:
            def __init__(self):
                self.at = 0

            def __call__(self, *shape):
                n = 1
                for s in shape:
                    n *= s
                v = arena[:, self.at:self.at + n]
                self.at += n
                assert self.at <= ARENA, self.at
                names = " ".join("abcd"[i] for i in range(len(shape)))
                if len(shape) > 1:
                    v = v.rearrange(f"p ({names}) -> p {names}", **{"abcd"[i]: s for i, s in enumerate(shape)})
                return v

        weights = Local()
        wa = weights(8 * C)
        wcv = weights(HB, C)
        cols_a = weights(6)
        wb1 = weights(2 * HID)
        wbh = weights(2, HB, HID)
        wb3 = weights(HB, C)
        cols_b = weights(4 * HB + 1)
        wqk_c = weights(2 * INNER)

        phase_end = sem("phase_end")

        def end_phase(eng, k):
            eng.drain().then_inc(phase_end, 1)
            eng.wait_ge(phase_end, 4 * k)

        loaded_x = sem("loaded_x")
        loaded_const = sem("loaded_const")
        loaded_a = sem("loaded_a")
        loaded_b = sem("loaded_b")
        loaded_c = sem("loaded_c")
        stored = sem("stored")
        const_ready = sem("const_ready")
        mask_stage = wqk_stage[:, 0:TPS * 2 * WIN].rearrange("p (t k) -> p t k", t=TPS)

        def rsqrt_step(link, v, y, w):
            link(nc.vector.tensor_tensor(w, y, y, ALU.mult))
            link(nc.vector.scalar_tensor_tensor(w, w, -0.5, v, ALU.mult, ALU.mult))
            link(nc.vector.scalar_tensor_tensor(y, w, 1.5, y, ALU.add, ALU.mult))

        LANES, UT = 2, 4
        UN = UT * P
        SA = NT // (UT * LANES)
        la = Local()
        la.at = weights.at

        def lanes(*shape):
            return [la(*shape) for _ in range(LANES)]

        a_st, a_mv, a_var, a_y, a_w = lanes(UT, 6), lanes(UT, 2), lanes(UT), lanes(UT), lanes(UT)
        a_x1, a_hn = lanes(UT, C), lanes(UT, C)
        a_x1t = lanes(2, T)
        a_h = lanes(2, T + 1)
        a_d, a_xxx = lanes(2, T), lanes(2, T)
        a_k, a_v, a_er = lanes(2, T), lanes(2, T), lanes(2, T)
        a_m, a_bs, a_aa = lanes(2, T + 1), lanes(2, T + 1), lanes(2, T + 1)
        a_g = [v.rearrange("p a c -> p (a c)").rearrange("p (s t) -> p s t", s=2) for v in a_x1]
        a_ek = [v.rearrange("p a c -> p (a c)").rearrange("p (s t) -> p s t", s=2) for v in a_hn]
        a_e1b, a_e2b, a_e1, a_e2 = lanes(2, T), lanes(2, T), lanes(2, T), lanes(2, T)
        a_rk = [[v.rearrange("p s t -> p (s t)") for v in (a_k[i], a_v[i], a_e1b[i], a_e2b[i])] for i in range(LANES)]
        TS, TF, G1, B1, G2, B2 = (cols_a[:, i:i + 1] for i in range(6))

        def flat(v):
            return v.rearrange("p a b -> p (a b)")

        def seqs(v):
            return v.rearrange("p (s t) -> p s t", s=2)

        bT0, bT1, bK, bV = ([bank[4 * i + j] for i in range(LANES)] for j in range(4))
        (a_var1, a_y1, a_var2, a_y2, a_hn_ready, a_tr1, a_h_ready, a_xxx_ready, a_kvr, a_kv_ready, a_ge_in,
         a_ge, a_bs_ready, a_bb, a_e_in, a_e, a_er_plus, a_den, a_xr, a_tr2, a_var3, a_y3, a_h2n, a_tr3, a_h2_ready,
         a_xxx2, a_cr, a_ck, a_relu, a_rk_ready, a_cv, a_er2, a_out, a_tr4, a_x_done) = (sem("a_" + s) for s in (
             "var1 rstd1 var2 rstd2 hn transposed1 h xxx kvr kv ge_in ge cum lncum e_in e er_plus den xr transposed2 var3 rstd3 "
             "h2n transposed3 h2 xxx2 cr ck relu relu2 cv er2 out transposed4 x_done").split())
        a_fixed = sem("a_fixed")
        a_chain = sem("a_chain")
        a_act_chain = sem("a_act_chain")
        a_pool_chain = sem("a_pool_chain")

        def phase_a_vector_start(dve):
            dve.wait_ge(loaded_a, LOADS_A * 16)
            for i in range(LANES):
                nc.vector.tensor_copy(a_h[i][:, :, 0], cols_a[:, 0:1].to_broadcast([P, 2])).then_inc(a_fixed, 1)
                nc.vector.memset(a_m[i][:, :, 0], 0.0).then_inc(a_fixed, 1)
                nc.vector.memset(a_bs[i][:, :, 0], 1.0).then_inc(a_fixed, 1)
                nc.vector.memset(a_aa[i][:, :, 0], 0.0).then_inc(a_fixed, 1)
                nc.vector.memset(a_w[i], 0.0).then_inc(a_x_done, 1)
            dve.wait_ge(a_fixed, 4 * LANES)
            dve.wait_ge(a_x_done, LANES)

        def phase_a_vector_steps(dve, step):
            link = Chain(dve, a_chain, LANES * A_LINKS, step)
            n = LANES * step + 1

            def tiles(i, t):
                return x_all[:, bass.ds((LANES * step + i) * UT + t, 1), :].rearrange("p a c -> p (a c)")

            def stats(src, i):
                for t in range(UT):
                    ins = nc.vector.bn_stats(a_st[i][:, t, :], src(t))
                link(ins)
                nc.vector.memset(a_w[i], 0.0)
                for t in range(UT):
                    ins = nc.vector.bn_aggr(a_mv[i][:, t, :], a_st[i][:, t, :])
                link(ins)

            def normalise(dst, src, i):
                rsqrt_step(link, a_var[i], a_y[i], a_w[i])
                for t in range(UT):
                    last = nc.vector.tensor_scalar(dst[:, t, :], src(t), a_mv[i][:, t, 0:1], a_y[i][:, t:t + 1],
                                                   ALU.subtract, ALU.mult)
                return last

            for i in range(LANES):
                stats(lambda t: tiles(i, t), i)
                nc.vector.tensor_scalar(a_var[i], a_mv[i][:, :, 1], EPS, None, ALU.add).then_inc(a_var1, 1)
            for i in range(LANES):
                dve.wait_ge(a_y1, n + i)
                link(normalise(a_x1[i], lambda t: tiles(i, t), i))
                stats(lambda t: a_x1[i][:, t, :], i)
                nc.vector.tensor_scalar(a_var[i], a_mv[i][:, :, 1], EPS, None, ALU.add).then_inc(a_var2, 1)
            for i in range(LANES):
                dve.wait_ge(a_y2, n + i)
                normalise(a_hn[i], lambda t: a_x1[i][:, t, :], i).then_inc(a_hn_ready, 1)
            for i in range(LANES):
                dve.wait_ge(a_h_ready, n + i)
                link(nc.vector.tensor_tensor(a_d[i], a_h[i][:, :, 1:], a_h[i][:, :, :T], ALU.subtract))
                nc.vector.scalar_tensor_tensor(a_xxx[i], a_d[i], TS, a_h[i][:, :, 1:], ALU.mult, ALU.add)\
                    .then_inc(a_xxx_ready, 1)
            for i in range(LANES):
                dve.wait_ge(a_kv_ready, n + i)
                for s in range(2):
                    link(nc.vector.tensor_tensor_scan(a_m[i][:, s, 1:], a_k[i][:, s, :], a_k[i][:, s, :], 0.0,
                                                      ALU.max, ALU.max))
                nc.vector.tensor_tensor(a_g[i], a_m[i][:, :, :T], a_m[i][:, :, 1:], ALU.subtract).then_inc(a_ge_in, 1)
                nc.vector.tensor_tensor(a_ek[i], a_k[i], a_m[i][:, :, 1:], ALU.subtract).then_inc(a_ge_in, 1)
            for i in range(LANES):
                dve.wait_ge(a_ge, n + i)
                for s in range(2):
                    nc.vector.tensor_tensor_scan(a_bs[i][:, s, 1:], a_g[i][:, s, :], a_ek[i][:, s, :], 1.0,
                                                 ALU.mult, ALU.add).then_inc(a_bs_ready, 1)
            for i in range(LANES):
                dve.wait_ge(a_bb, n + i)
                link(nc.vector.tensor_tensor(a_d[i], a_d[i], a_m[i][:, :, :T], ALU.add))
                link(nc.vector.tensor_tensor(a_d[i], a_d[i], a_k[i], ALU.subtract))
                nc.vector.tensor_scalar(a_e1b[i], a_d[i], 0.0, None, ALU.min).then_inc(a_e_in, 1)
                nc.vector.tensor_scalar(a_e2b[i], a_d[i], 0.0, None, ALU.max).then_inc(a_e_in, 1)
                nc.vector.tensor_scalar(a_e1[i], a_d[i], TF, 0.0, ALU.subtract, ALU.min).then_inc(a_e_in, 1)
                nc.vector.tensor_scalar(a_e2[i], a_d[i], TF, 0.0, ALU.subtract, ALU.max).then_inc(a_e_in, 1)
            for i in range(LANES):
                dve.wait_ge(a_e, n + i)
                link(nc.vector.tensor_tensor(a_e2b[i], a_e2b[i], a_v[i], ALU.mult))
                for s in range(2):
                    link(nc.vector.tensor_tensor_scan(a_aa[i][:, s, 1:], a_e1b[i][:, s, :], a_e2b[i][:, s, :], 0.0,
                                                      ALU.mult, ALU.add))
                dve.wait_ge(a_den, n + i)
                link(nc.vector.tensor_tensor(a_d[i], a_e1[i], a_aa[i][:, :, :T], ALU.mult))
                link(nc.vector.tensor_tensor(a_d[i], a_d[i], a_e2[i], ALU.add))
                link(nc.vector.reciprocal(a_er[i], a_er[i]))
                link(nc.vector.tensor_tensor(a_d[i], a_d[i], a_er[i], ALU.mult))
                nc.vector.tensor_tensor(a_x1t[i], a_d[i], a_x1t[i], ALU.add).then_inc(a_xr, 1)
            for i in range(LANES):
                dve.wait_ge(a_tr2, n + i)
                stats(lambda t: bT1[i][:, t * C:(t + 1) * C], i)
                nc.vector.tensor_scalar(a_var[i], a_mv[i][:, :, 1], EPS, None, ALU.add).then_inc(a_var3, 1)
            for i in range(LANES):
                dve.wait_ge(a_y3, n + i)
                normalise(a_hn[i], lambda t: bT1[i][:, t * C:(t + 1) * C], i).then_inc(a_h2n, 1)
            for i in range(LANES):
                dve.wait_ge(a_h2_ready, n + i)
                link(nc.vector.tensor_tensor(a_d[i], a_h[i][:, :, :T], a_h[i][:, :, 1:], ALU.subtract))
                link(nc.vector.scalar_tensor_tensor(a_xxx[i], a_d[i], TS, a_h[i][:, :, 1:], ALU.mult, ALU.add))
                nc.vector.tensor_copy(a_h[i][:, :, 0], cols_a[:, 0:1].to_broadcast([P, 2])).then_inc(a_xxx2, 1)
            for i in range(LANES):
                dve.wait_ge(a_er2, n + i)
                link(nc.vector.reciprocal(a_er[i], a_er[i]))
                dve.wait_ge(a_cv, n + i)
                link(nc.vector.tensor_tensor(flat(a_d[i]), flat(a_er[i]), bK[i][:, :], ALU.mult))
                nc.vector.tensor_tensor(a_x1t[i], a_x1t[i], a_d[i], ALU.add).then_inc(a_out, 1)
            for i in range(LANES):
                dve.wait_ge(a_tr4, n + i)
                xs = x_all[:, bass.ds((LANES * step + i) * UT, UT), :]
                nc.vector.tensor_tensor(xs, xs, bT0[i][:, :].rearrange("p (t c) -> p t c", t=UT), ALU.add)\
                    .then_inc(a_x_done, 1)
            dve.wait_ge(a_x_done, n + 2 * LANES - 1)
            link.end()

        A_LINKS = 32

        def phase_a_scalar_steps(act, step):
            n = LANES * step + 1
            link = Chain(act, a_act_chain, 9 * LANES, step)

            def rstd(i):
                link(nc.scalar.activation(a_y[i], a_var[i], ACT.Ln))
                return nc.scalar.activation(a_y[i], a_y[i], ACT.Exp, scale=-0.5)

            for i in range(LANES):
                act.wait_ge(a_var1, n + i)
                rstd(i).then_inc(a_y1, 1)
            for i in range(LANES):
                act.wait_ge(a_var2, n + i)
                rstd(i).then_inc(a_y2, 1)
            for i in range(LANES):
                act.wait_ge(a_tr1, n + i)
                nc.scalar.activation(flat(a_x1t[i]), bT0[i][:, :], ACT.Copy)
                nc.scalar.activation(a_h[i][:, :, 1:], seqs(bT1[i][:, :]), ACT.Identity, bias=B1, scale=G1)\
                    .then_inc(a_h_ready, 1)
            for i in range(LANES):
                act.wait_ge(a_kvr, n + i)
                nc.scalar.activation(flat(a_k[i]), bK[i][:, :], ACT.Copy)
                nc.scalar.activation(flat(a_v[i]), bV[i][:, :], ACT.Copy)
                nc.scalar.activation(flat(a_er[i]), bT0[i][:, :], ACT.Exp, scale=-1.0).then_inc(a_kv_ready, 1)
            for i in range(LANES):
                act.wait_ge(a_ge_in, 2 * (n + i))
                nc.scalar.activation(a_g[i], a_g[i], ACT.Exp)
                nc.scalar.activation(a_ek[i], a_ek[i], ACT.Exp).then_inc(a_ge, 1)
                act.wait_ge(a_kv_ready, n + i)
                nc.scalar.activation(a_er[i], a_er[i], ACT.Identity, bias=1.0).then_inc(a_er_plus, 1)
            for i in range(LANES):
                act.wait_ge(a_bs_ready, 2 * (n + i))
                nc.scalar.activation(a_d[i], a_bs[i][:, :, :T], ACT.Ln).then_inc(a_bb, 1)
            for i in range(LANES):
                act.wait_ge(a_e_in, 4 * (n + i))
                nc.scalar.activation(a_e1[i], a_e1[i], ACT.Exp)
                nc.scalar.activation(a_e2[i], a_e2[i], ACT.Exp, scale=-1.0)
                nc.scalar.activation(a_e1b[i], a_e1b[i], ACT.Exp)
                nc.scalar.activation(a_e2b[i], a_e2b[i], ACT.Exp, scale=-1.0).then_inc(a_e, 1)
            for i in range(LANES):
                act.wait_ge(a_var3, n + i)
                rstd(i).then_inc(a_y3, 1)
            for i in range(LANES):
                act.wait_ge(a_tr3, n + i)
                link(nc.scalar.activation(a_h[i][:, :, 1:], seqs(bT1[i][:, :]), ACT.Identity, bias=B2, scale=G2))
                nc.scalar.activation(a_h[i][:, :, 0], a_h[i][:, :, T], ACT.Copy).then_inc(a_h2_ready, 1)
            for i in range(LANES):
                act.wait_ge(a_cr, n + i)
                link(nc.scalar.activation(flat(a_er[i]), bT0[i][:, :], ACT.Exp, scale=-1.0))
                nc.scalar.activation(a_er[i], a_er[i], ACT.Identity, bias=1.0).then_inc(a_er2, 1)
            for c in range(HB):
                for i in range(LANES):
                    act.wait_ge(a_ck, HB * LANES * step + c * LANES + i + 1)
                    src = (bV, bT1)[c % 2][i]
                    link(nc.scalar.activation(a_rk[i][c], src[:, :], ACT.Relu))
                    nc.scalar.activation(a_rk[i][c], a_rk[i][c], ACT.Square).then_inc(a_rk_ready, 1)
            link.end()

        def phase_a_gpsimd_steps(pool, step):
            n = LANES * step + 1
            link = Chain(pool, a_pool_chain, 2 * LANES, step)
            for i in range(LANES):
                pool.wait_ge(a_er_plus, n + i)
                pool.wait_ge(a_e, n + i)
                link(nc.gpsimd.tensor_tensor(a_g[i], a_e1[i], a_e2[i], ALU.add))
                link(nc.gpsimd.tensor_tensor(a_er[i], a_er[i], a_g[i], ALU.mult))
                nc.gpsimd.tensor_tensor(a_e2[i], a_e2[i], a_v[i], ALU.mult).then_inc(a_den, 1)
            link.end()

        def phase_a_tensor_steps(pe, step):
            n = LANES * step + 1

            def transposes(dst, src):
                for t in range(UT):
                    last = nc.tensor.transpose(dst[:, t * P:(t + 1) * P], src(t), ident[:, :])
                return last

            for i in range(LANES):
                pe.wait_ge(a_hn_ready, n + i)
                pe.wait_ge(a_x_done, n + i)
                transposes(bT0[i], lambda t: a_x1[i][:, t, :])
                transposes(bT1[i], lambda t: a_hn[i][:, t, :]).then_inc(a_tr1, 1)
            for i in range(LANES):
                pe.wait_ge(a_xxx_ready, n + i)
                for j, dst in enumerate((bK, bV, bT0)):
                    last = nc.tensor.matmul(dst[i][:, :], wa[:, j * C:(j + 1) * C], flat(a_xxx[i]), start=True, stop=True)
                last.then_inc(a_kvr, 1)
            for i in range(LANES):
                pe.wait_ge(a_xr, n + i)
                transposes(bT1[i], lambda t: flat(a_x1t[i])[:, t * P:(t + 1) * P]).then_inc(a_tr2, 1)
            for i in range(LANES):
                pe.wait_ge(a_h2n, n + i)
                transposes(bT1[i], lambda t: a_hn[i][:, t, :]).then_inc(a_tr3, 1)
            for i in range(LANES):
                pe.wait_ge(a_xxx2, n + i)
                nc.tensor.matmul(bT0[i][:, :], wa[:, 3 * C:4 * C], flat(a_xxx[i]), start=True, stop=True).then_inc(a_cr, 1)
            for c in range(HB):
                for i in range(LANES):
                    if c >= 2:
                        pe.wait_ge(a_rk_ready, HB * LANES * step + (c - 2) * LANES + i + 1)
                    dst = (bV, bT1)[c % 2][i]
                    nc.tensor.matmul(dst[:, :], wa[:, (4 + c) * C:(5 + c) * C], flat(a_xxx[i]), start=True, stop=True)\
                        .then_inc(a_ck, 1)
            for c in range(HB):
                for i in range(LANES):
                    pe.wait_ge(a_rk_ready, HB * LANES * step + c * LANES + i + 1)
                    last = nc.tensor.matmul(bK[i][:, :], wcv[:, c, :], a_rk[i][c], start=(c == 0), stop=(c == HB - 1))
                    if c == HB - 1:
                        last.then_inc(a_cv, 1)
            for i in range(LANES):
                pe.wait_ge(a_out, n + i)
                transposes(bT0[i], lambda t: flat(a_x1t[i])[:, t * P:(t + 1) * P]).then_inc(a_tr4, 1)

        SB_ = NT // UT
        lb = Local()
        lb.at = weights.at
        b_st, b_mv = lb(NT, 6), lb(NT, 2)
        b_var, b_y, b_w = lb(NT), lb(NT), lb(NT)
        b_xn = lb(UT, C)
        b_xt = lb(UN)
        b_sl = lb(2, UN)
        b_h = lb(HB, UN)
        b_g = lb(2, HB, UN)
        b_o = lb(UN)
        b_fixed, b_chain, b_rstd, b_xn_ready, b_xtp, b_xt_ready = (sem("b_" + s) for s in "fixed chain rstd xn xtp xt".split())
        b_up, b_silu, b_h_ready, b_hid, b_gelu, b_down, b_o_ready, b_ot, b_x_done = (
            sem("b_" + s) for s in "up silu h hid gelu down o ot x_done".split())

        def scale_b(layer, c):
            return cols_b[:, layer * HB + c:layer * HB + c + 1]

        def normalise_b(u):
            for t in range(UT):
                last = nc.vector.tensor_scalar(
                    b_xn[:, t, :], x_all[:, bass.ds(u * UT + t, 1), :].rearrange("p a c -> p (a c)"),
                    b_mv[:, bass.ds(u * UT + t, 1), 0], b_y[:, bass.ds(u * UT + t, 1)], ALU.subtract, ALU.mult)
            last.then_inc(b_xn_ready, 1)

        def phase_b_vector(dve):
            link = Chain(dve, b_chain, 5, 0)
            for t in range(NT):
                ins = nc.vector.bn_stats(b_st[:, t, :], x_all[:, t, :])
            link(ins)
            for t in range(NT):
                ins = nc.vector.bn_aggr(b_mv[:, t, :], b_st[:, t, :])
            link(ins)
            nc.vector.tensor_scalar(b_var, b_mv[:, :, 1], EPS, None, ALU.add).then_inc(b_fixed, 1)
            dve.wait_ge(b_rstd, 1)
            rsqrt_step(link, b_var, b_y, b_w)
            link.end()
            dve.wait_ge(loaded_b, LOADS_B * 16)
            normalise_b(0)
            with dve.Fori(0, SB_) as u:
                for c in range(HB):
                    dve.wait_ge(b_silu, HB * u + c + 1)
                    if c == 0:
                        dve.wait_ge(b_down, u + 1)
                    nc.vector.scalar_tensor_tensor(b_h[:, c, :], bank[2 + c % 2][:, :], scale_b(1, c), b_sl[:, c % 2, :],
                                                   ALU.mult, ALU.mult).then_inc(b_h_ready, 1)
                dve.wait_ge(b_xtp, u + 1)
                normalise_b((u + 1) & (SB_ - 1))
                dve.wait_ge(b_ot, u + 1)
                xs = x_all[:, bass.ds(u * UT, UT), :]
                nc.vector.tensor_tensor(xs, xs, bank[5][:, :].rearrange("p (t c) -> p t c", t=UT), ALU.add)\
                    .then_inc(b_x_done, 1)
            dve.wait_ge(b_x_done, SB_ + 1)

        def phase_b_scalar(act):
            act.wait_ge(b_fixed, 1)
            nc.scalar.activation(b_y, b_var, ACT.Ln).then_inc(b_fixed, 1)
            act.wait_ge(b_fixed, 2)
            nc.scalar.activation(b_y, b_y, ACT.Exp, scale=-0.5).then_inc(b_rstd, 1)
            act.wait_ge(loaded_b, LOADS_B * 16)
            act.wait_ge(b_xtp, 1)
            nc.scalar.activation(b_xt, bank[6][:, :], ACT.Copy).then_inc(b_xt_ready, 1)
            with act.Fori(0, SB_) as u:
                for c in range(HB):
                    act.wait_ge(b_up, HB * u + c + 1)
                    if c >= 2:
                        act.wait_ge(b_h_ready, HB * u + c - 1)
                    nc.scalar.activation(b_sl[:, c % 2, :], bank[c % 2][:, :], ACT.Silu, scale=scale_b(0, c))\
                        .then_inc(b_silu, 1)
                for layer in range(2):
                    for c in range(HB):
                        act.wait_ge(b_hid, 2 * HB * u + HB * layer + c + 1)
                        nc.scalar.activation(b_g[:, layer, c, :], bank[(4 if layer == 0 else 0) + c][:, :], ACT.Gelu,
                                             scale=scale_b(2 + layer, c)).then_inc(b_gelu, 1)
                act.wait_ge(b_xtp, u + 2)
                nc.scalar.activation(b_xt, bank[6][:, :], ACT.Copy).then_inc(b_xt_ready, 1)
                act.wait_ge(b_down, u + 2)
                nc.scalar.activation(b_o, bank[4][:, :], ACT.Copy, scale=scale_b(4, 0)).then_inc(b_o_ready, 1)

        def phase_b_tensor(pe):
            def transpose_tokens():
                for t in range(UT):
                    last = nc.tensor.transpose(bank[6][:, t * P:(t + 1) * P], b_xn[:, t, :], ident[:, :])
                last.then_inc(b_xtp, 1)

            pe.wait_ge(loaded_b, LOADS_B * 16)
            pe.wait_ge(b_xn_ready, 1)
            transpose_tokens()
            with pe.Fori(0, SB_) as u:
                pe.wait_ge(b_xt_ready, u + 1)
                for c in range(HB):
                    if c >= 2:
                        pe.wait_ge(b_h_ready, HB * u + c - 1)
                    nc.tensor.matmul(bank[c % 2][:, :], wb1[:, c * P:(c + 1) * P], b_xt, start=True, stop=True)
                    nc.tensor.matmul(bank[2 + c % 2][:, :], wb1[:, HID + c * P:HID + (c + 1) * P], b_xt,
                                     start=True, stop=True).then_inc(b_up, 1)
                for layer in range(2):
                    if layer == 0:
                        pe.wait_ge(b_x_done, u + 1)
                    for c in range(HB):
                        for k in range(HB):
                            if c == 0 and layer == 0:
                                pe.wait_ge(b_h_ready, HB * u + k + 1)
                            if c == 0 and layer == 1:
                                pe.wait_ge(b_gelu, 2 * HB * u + k + 1)
                            src = b_h[:, k, :] if layer == 0 else b_g[:, 0, k, :]
                            last = nc.tensor.matmul(bank[(4 if layer == 0 else 0) + c][:, :],
                                                    wbh[:, layer, k, c * P:(c + 1) * P], src,
                                                    start=(k == 0), stop=(k == HB - 1))
                        last.then_inc(b_hid, 1)
                pe.wait_ge(b_xn_ready, u + 2)
                transpose_tokens()
                for k in range(HB):
                    pe.wait_ge(b_gelu, 2 * HB * u + HB + k + 1)
                    last = nc.tensor.matmul(bank[4][:, :], wb3[:, k, :], b_g[:, 1, k, :], start=(k == 0), stop=(k == HB - 1))
                last.then_inc(b_down, 1)
                pe.wait_ge(b_o_ready, u + 1)
                for t in range(UT):
                    last = nc.tensor.transpose(bank[5][:, t * P:(t + 1) * P], b_o[:, t * P:(t + 1) * P], ident[:, :])
                last.then_inc(b_ot, 1)

        TURNS = TPS * PAIRS
        GROUPS = TURNS // 2
        lc = Local()
        lc.at = weights.at
        c_st, c_mv = lc(NT, 6), lc(NT, 2)
        c_var, c_y, c_w = lc(NT), lc(NT), lc(NT)
        c_xn, c_xv = lc(TPS, C), lc(TPS, C)
        c_xt = lc(T)
        c_q = lc(PAIRS, T)
        c_k = lc(PAIRS, 2, T)
        c_e = lc(3, 2, T)
        c_pt = lc(2, TPS, 4, P)
        c_yt = lc(H, P)
        c_nm, c_sum, c_inv = lc(3, 2), lc(3, 2), lc(3, 2)
        (c_fixed, c_chain, c_rstd, c_xn_ready, c_xv_ready, c_xtp, c_xt_ready, c_proj, c_q_ready, c_k_ready, c_s, c_max,
         c_exp, c_prob, c_ptp, c_pt_ready, c_py, c_yt_ready, c_acc, c_x_done, c_m, c_m_ready, c_recip) = (
            sem("c_" + s) for s in ("fixed chain rstd xn xv xtp xt proj q k s max exp prob ptp pt py yt acc x_done m m_ready "
                                    "recip").split())
        QSCALE = float(DH) ** -0.5

        def head_slot(h):
            return h % 2 * PAIRS + h // 2

        def wv_wo(pe, ready, done, base, first_bank=5):
            for g in range(4):
                if g >= 2:
                    pe.wait_ge(done, base + g - 1)
                d = g % 2 * DH
                for j in range(4):
                    a = 4 * (g // 2) + j
                    last = nc.tensor.matmul(bank[first_bank + g % 2][:, j * P:(j + 1) * P], wvt[d:d + DH, a, :], wo[d:d + DH, a, :],
                                            start=True, stop=True)
                last.then_inc(ready, 1)

        def wv_wo_slots(slot, g):
            first = g % 2 * PAIRS + 4 * (g // 2)
            return m_vo[:, slot, first:first + 4, :]

        def normalise_c(n):
            for t in range(TPS):
                last = nc.vector.tensor_scalar(
                    c_xn[:, t, :], x_all[:, bass.ds(n * TPS + t, 1), :].rearrange("p a c -> p (a c)"),
                    c_mv[:, bass.ds(n * TPS + t, 1), 0], c_y[:, bass.ds(n * TPS + t, 1)], ALU.subtract, ALU.mult)
            last.then_inc(c_xn_ready, 1)

        def phase_c_vector(dve):
            nc.vector.memset(c_k, 0.0).then_inc(c_fixed, 1)
            nc.vector.memset(c_nm, 0.0).then_inc(c_x_done, 1)
            nc.vector.memset(c_sum, 0.0).then_inc(c_py, 1)
            nc.vector.memset(c_inv, 0.0).then_inc(c_acc, 1)
            link = Chain(dve, c_chain, 5, 0)
            for t in range(NT):
                ins = nc.vector.bn_stats(c_st[:, t, :], x_all[:, t, :])
            link(ins)
            for t in range(NT):
                ins = nc.vector.bn_aggr(c_mv[:, t, :], c_st[:, t, :])
            link(ins)
            nc.vector.tensor_scalar(c_var, c_mv[:, :, 1], EPS, None, ALU.add).then_inc(c_fixed, 1)
            dve.wait_ge(c_rstd, 1)
            rsqrt_step(link, c_var, c_y, c_w)
            link.end()
            normalise_c(0)

            def keys(n):
                for g in range(4):
                    dve.wait_ge(c_proj, 8 * n + 4 + g + 1)
                    src = bank[5 + (g + 1) % 2][:, :].rearrange("p (a t) -> p a t", a=2)
                    nc.vector.tensor_copy(c_k[0:DH, 2 * g:2 * g + 2, 0, :], src[0:DH])
                    nc.vector.tensor_copy(c_k[DH:P, 2 * g:2 * g + 2, 1, :], src[DH:P]).then_inc(c_k_ready, 1)

            dve.wait_ge(c_fixed, 2)
            keys(0)
            with dve.Fori(0, SEQS) as n:
                dve.wait_ge(c_py, GROUPS * n + 1)
                dve.wait_ge(c_xn_ready, n + 1)
                nc.vector.tensor_copy(c_xv, c_xn).then_inc(c_xv_ready, 1)
                dve.wait_ge(c_xv_ready, n + 1)
                dve.wait_ge(c_xtp, n + 1)
                normalise_c((n + 1) & (SEQS - 1))
                for t in range(TURNS + 6):
                    if t < TURNS:
                        dve.wait_ge(c_s, TURNS * n + t + 1)
                        nc.vector.tensor_reduce(out=c_nm[:, t % 3, :], in_=bank[t % 3][:, :].rearrange("p (h k) -> p h k", h=2),
                                                op=ALU.max, axis=AXX, negate=True).then_inc(c_max, 1)
                    if 1 <= t <= TURNS:
                        r = (t - 1) % 3
                        dve.wait_ge(c_exp, 2 * (TURNS * n + t - 1) + 2)
                        nc.vector.reciprocal(c_inv[:, r, :], c_sum[:, r, :]).then_inc(c_recip, 1)
                        dve.wait_ge(c_recip, TURNS * n + t)
                        for hd in range(2):
                            last = nc.vector.tensor_scalar(c_e[:, r, hd, :], c_e[:, r, hd, :], c_inv[:, r, hd:hd + 1], None,
                                                           ALU.mult)
                        last.then_inc(c_prob, 1)
                    if t == TURNS:
                        keys(n + 1)
                    if t >= 5 and t % 2 == 1 and (t - 5) // 2 < GROUPS:
                        g = (t - 5) // 2
                        if g % 4 == 0:
                            dve.wait_ge(c_acc, TPS * n + g // 4 + 1)
                        dve.wait_ge(c_py, GROUPS * n + g + 2)
                        nc.vector.tensor_copy(c_yt[:, 4 * (g % 4):4 * (g % 4) + 4, :],
                                              bank[5][:, :].rearrange("p (h q) -> p h q", h=4)).then_inc(c_yt_ready, 1)
                    if t in (13, TURNS + 5):
                        j = 0 if t == 13 else 1
                        dve.wait_ge(c_acc, TPS * n + j + 2)
                        xs = x_all[:, bass.ds(n * TPS + j, 1), :].rearrange("p a c -> p (a c)")
                        nc.vector.tensor_tensor(xs, xs, bank[7][:, 0:C], ALU.add).then_inc(c_x_done, 1)
            dve.wait_ge(c_x_done, TPS * SEQS + 1)

        def phase_c_scalar(act):
            for g in range(H // 4):
                act.wait_ge(c_m, g + 1)
                nc.scalar.activation(wv_wo_slots(1, g), bank[5 + g % 2][:, :].rearrange("p (h c) -> p h c", h=4),
                                     ACT.Copy).then_inc(c_m_ready, 1)
            act.wait_ge(c_fixed, 2)
            nc.scalar.activation(c_y, c_var, ACT.Ln).then_inc(c_fixed, 1)
            act.wait_ge(c_fixed, 3)
            nc.scalar.activation(c_y, c_y, ACT.Exp, scale=-0.5).then_inc(c_rstd, 1)

            def queries(n):
                act.wait_ge(c_xtp, n + 1)
                nc.scalar.activation(c_xt, bank[7][:, 0:T], ACT.Copy).then_inc(c_xt_ready, 1)
                for g in range(4):
                    act.wait_ge(c_proj, 8 * n + g + 1)
                    nc.scalar.activation(c_q[:, 2 * g:2 * g + 2, :], bank[5 + (g + 1) % 2][:, :].rearrange("p (a t) -> p a t", a=2),
                                         ACT.Copy, scale=QSCALE).then_inc(c_q_ready, 1)

            queries(0)
            with act.Fori(0, SEQS) as n:
                for t in range(TURNS + 2):
                    if t < TURNS:
                        act.wait_ge(c_max, TURNS * n + t + 1)
                        if t >= 3:
                            act.wait_ge(c_ptp, TURNS * n + t - 2)
                        for hd in range(2):
                            nc.scalar.activation(c_e[:, t % 3, hd, :], bank[t % 3][:, hd * T:(hd + 1) * T], ACT.Exp,
                                                 bias=c_nm[:, t % 3, hd:hd + 1], accum_out=c_sum[:, t % 3, hd:hd + 1])\
                                .then_inc(c_exp, 1)
                    if t == TURNS:
                        queries(n + 1)
                    if t >= 2:
                        u = t - 2
                        g = u // 2
                        act.wait_ge(c_ptp, TURNS * n + u + 1)
                        if u % 2 == 0:
                            act.wait_ge(c_py, (GROUPS * n + g) if g >= 1 else GROUPS * n + 1)
                        nc.scalar.activation(c_pt[:, g % 2, :, 2 * (u % 2):2 * (u % 2) + 2, :],
                                             bank[3 + u % 2][:, :].rearrange("p (h k q) -> p k h q", h=2, k=TPS), ACT.Copy)\
                            .then_inc(c_pt_ready, 1)

        def phase_c_tensor(pe):
            pe.wait_ge(loaded_c, LOADS_C * 16)
            wv_wo(pe, c_m, c_m_ready, 0)
            pe.wait_ge(c_m_ready, H // 4)

            def projections(n):
                pe.wait_ge(c_xn_ready, n + 1)
                for t in range(TPS):
                    last = nc.tensor.transpose(bank[7][:, t * P:(t + 1) * P], c_xn[:, t, :], ident[:, :])
                last.then_inc(c_xtp, 1)
                pe.wait_ge(c_xt_ready, n + 1)
                for g in range(8):
                    if 2 <= g < 6:
                        pe.wait_ge(c_q_ready, 4 * n + g - 1)
                    elif g >= 6:
                        pe.wait_ge(c_k_ready, 4 * n + g - 5)
                    for a in range(2):
                        w = wqk_c[:, (2 * g + a) * P:(2 * g + a + 1) * P]
                        last = nc.tensor.matmul(bank[5 + (g + 1) % 2][:, a * T:(a + 1) * T], w, c_xt, start=True, stop=True)
                    last.then_inc(c_proj, 1)

            def sum_heads():
                for h in range(H):
                    nc.tensor.matmul(bank[7][:, 0:C], c_yt[:, h, :], m_vo[:, 1, head_slot(h), :], start=(h == 0), stop=False)
                nc.tensor.matmul(bank[7][:, 0:C], ones_row[:, :], bo[:, :], start=False, stop=True).then_inc(c_acc, 1)

            projections(0)
            with pe.Fori(0, SEQS) as n:
                pe.wait_ge(c_k_ready, 4 * n + 4)
                pe.wait_ge(c_q_ready, 4 * n + 4)
                pe.wait_ge(c_xv_ready, n + 1)
                for t in range(TURNS + 5):
                    if t < TURNS:
                        j, a = t // PAIRS, t % PAIRS
                        if t >= 3:
                            pe.wait_ge(c_exp, 2 * (TURNS * n + t - 3) + 2)
                        nc.tensor.matmul(bank[t % 3][:, :], c_q[:, a, j * P:(j + 1) * P],
                                         c_k[:, a, :, :].rearrange("p h k -> p (h k)"), start=True, stop=True).then_inc(c_s, 1)
                    if t == TURNS:
                        pe.wait_ge(c_x_done, TPS * n + 2)
                        pe.wait_ge(c_yt_ready, GROUPS * n + 6)
                        projections(n + 1)
                    if 2 <= t < TURNS + 2:
                        u = t - 2
                        pe.wait_ge(c_prob, TURNS * n + u + 1)
                        if u >= 2:
                            pe.wait_ge(c_pt_ready, TURNS * n + u - 1)
                        for hd in range(2):
                            for k in range(TPS):
                                last = nc.tensor.transpose(bank[3 + u % 2][:, (hd * TPS + k) * P:(hd * TPS + k + 1) * P],
                                                           c_e[:, u % 3, hd, k * P:(k + 1) * P], ident[:, :])
                        last.then_inc(c_ptp, 1)
                    if t in (12, TURNS + 4):
                        j = 0 if t == 12 else 1
                        pe.wait_ge(c_yt_ready, GROUPS * n + 4 * (j + 1))
                        pe.wait_ge(c_x_done, TPS * n + j + 1)
                        sum_heads()
                    if t >= 4 and t % 2 == 0 and (t - 4) // 2 < GROUPS:
                        g = (t - 4) // 2
                        pe.wait_ge(c_pt_ready, TURNS * n + 2 * g + 2)
                        if g == 6:
                            pe.wait_ge(c_k_ready, 4 * n + 8)
                        elif g >= 1:
                            pe.wait_ge(c_yt_ready, GROUPS * n + g)
                        for k in range(TPS):
                            last = nc.tensor.matmul(bank[5][:, :], c_xv[:, k, :],
                                                    c_pt[:, g % 2, k, :, :].rearrange("p h q -> p (h q)"),
                                                    start=(k == 0), stop=(k == TPS - 1))
                        last.then_inc(c_py, 1)

        ld = Local()
        XT0 = 3 * WIN
        d_xs = ld(TPS, C)
        d_xt = ld(XT0 + T)
        d_raw, d_sq, d_nrm = ld(2 * H, DH), ld(2 * H, DH), ld(2 * H, DH)
        d_rot = [ld(2 * H, DH) for _ in range(TPS)]
        d_t2 = d_sq
        d_ss, d_y, d_w = ld(2 * H), ld(2 * H), ld(2 * H)
        d_q = ld(PAIRS, T)
        d_k = ld(PAIRS, 2, WIN + T)
        d_e = ld(H, 2 * WIN)
        d_mx, d_sum, d_inv = ld(H), ld(H), ld(H)
        d_pt = ld(PAIRS, P)
        d_xw = [ld(NW, C) for _ in range(2)]
        d_yt = ld(H, P)
        d_x2 = ld(TPS, C)
        d_xf, d_xc, d_v, d_r, d_wf, d_xn = ld(T), ld(T), ld(T), ld(T), ld(T), ld(T)
        d_gl = ld(2, T)
        d_h = ld(len(FBLK), T)
        d_st, d_mv = ld(NT, 6), ld(NT, 2)
        d_var, d_rstd, d_wn = ld(NT), ld(NT), ld(NT)
        NF = len(FBLK)
        SLOTS, SLOTS0 = 16, 9
        (s_xs, s_split, s_ss, s_y, s_norm, s_t1, s_rope, s_tab, s_wsplit, s_proj, s_raw, s_sq, s_tp, s_tev,
         s_s, s_sub, s_exp, s_prob, s_py, s_yev, s_acc, s_x2, s_mean, s_xsq, s_varp, s_var, s_ln, s_y2, s_xn, s_up, s_gl, s_h,
         s_ffo, s_x_done, s_m, s_m_ready, d_zero, d_chain, d_pool_chain, d_act_chain,
         kept, d_stats, loaded_qk, loaded_sc, loaded_vo, loaded_ff) = (
            sem("d_" + s) for s in (
                "xs split ss rsq norm t1 rope tab wsplit proj raw sq tp tev s sub exp prob py yev acc x2 mean xsq varp "
                "var ln rsq2 xn up gl h ffo x_done m m_ready zero chain pool_chain act_chain "
                "kept stats loaded_qk loaded_sc loaded_vo loaded_ff").split())
        LOADS_FF = 5
        back = [sem(f"d_back{g}") for g in range(4)]
        KEEP = NT // len(back)

        x_kept = Local()(NT, C)

        def front_split(dve, f, link, first):
            dve.wait_ge(s_tev, xt_slot(f, first) + 1)
            if not first:
                dve.wait_ge(s_proj, 8 * f)
            link(nc.vector.tensor_copy(x_split[:, 0, :], d_xt[:, XT0:]))
            nc.vector.tensor_tensor(x_split[:, 1, :], d_xt[:, XT0:], x_split[:, 0, :].bitcast(F32), ALU.subtract)\
                .then_inc(s_split, 1)

        def front_norm(dve, f, j, link, first):
            i = TPS * f + j
            par = (f >> 4) & 1 if not first else 0
            dve.wait_ge(s_sq, i + 1)
            link(nc.vector.tensor_reduce(out=d_ss, in_=d_sq, op=ALU.add, axis=AXX))
            nc.vector.tensor_scalar(d_ss, d_ss, 1e-24, None, ALU.max).then_inc(s_ss, 1)
            dve.wait_ge(s_y, i + 1)
            rsqrt_step(link, d_ss, d_y, d_w)
            if not (first and j == 0):
                dve.wait_ge(s_rope, i)
            nc.vector.tensor_tensor(d_nrm, d_raw, d_y.unsqueeze(2).to_broadcast([P, 2 * H, DH]), ALU.mult).then_inc(s_norm, 1)
            dve.wait_ge(s_norm, i + 1)
            dve.wait_ge(s_tab, ((f >> 4) if not first else 0) + 1)
            if not first:
                dve.wait_ge(s_tev, slot_of(f - 1, 0))
            for m in range(2):
                tab = rope_d[:, bass.ds(par, 1), j, m, :].to_broadcast([P, H, DH])
                nc.vector.tensor_tensor(d_rot[j][:, m * H:(m + 1) * H, :], d_nrm[:, m * H:(m + 1) * H, :], tab, ALU.mult)\
                    .then_inc(s_t1, 1)

        def softmax_max(dve, n, j, link):
            i = TPS * n + j
            dve.wait_ge(s_s, i + 1)
            for b in range(2):
                last = nc.vector.tensor_reduce(out=d_mx[:, 8 * b:8 * b + 8],
                                               in_=bank[2 + b][:, :].rearrange("p (h k) -> p h k", h=8), op=ALU.max, axis=AXX)
            link(last)
            dve.wait_ge(s_tp, slot_of(n, 5 * j))
            for b in range(2):
                last = nc.vector.tensor_tensor(d_e[:, 8 * b:8 * b + 8, :], bank[2 + b][:, :].rearrange("p (h k) -> p h k", h=8),
                                               d_mx[:, 8 * b:8 * b + 8].unsqueeze(2).to_broadcast([P, 8, 2 * WIN]), ALU.subtract)
            last.then_inc(s_sub, 1)

        def softmax_prob(dve, n, j, link):
            dve.wait_ge(s_exp, TPS * n + j + 1)
            link(nc.vector.tensor_reduce(out=d_sum, in_=d_e, op=ALU.add, axis=AXX))
            link(nc.vector.reciprocal(d_inv, d_sum))
            nc.vector.tensor_tensor(d_e, d_e, d_inv.unsqueeze(2).to_broadcast([P, H, 2 * WIN]), ALU.mult).then_inc(s_prob, 1)

        def split_weights(dve, layer_next, link):
            par = layer_next & 1
            dve.wait_ge(loaded_qk, 16 * (layer_next + 1))
            hi = wqk_split[:, bass.ds(par, 1), 0, :].rearrange("p a n -> p (a n)")
            lo = wqk_split[:, bass.ds(par, 1), 1, :].rearrange("p a n -> p (a n)")
            link(nc.vector.tensor_copy(hi, wqk_stage[:, :]))
            nc.vector.tensor_tensor(lo, wqk_stage[:, :], hi.bitcast(F32), ALU.subtract).then_inc(s_wsplit, 1)

        D_LINKS = 20

        def phase_d_vector(dve):
            for v in (d_xt, d_k, d_xw[0], d_xw[1], d_xf):
                nc.vector.memset(v, 0.0).then_inc(d_zero, 1)
            for q, s in enumerate((s_sub, s_py, s_yev, s_yev, s_acc, s_x_done)):
                nc.vector.memset(d_w[:, q:q + 1], 0.0).then_inc(s, 1)
            link = Chain(dve, d_chain, 0, 0)
            split_weights(dve, 0, link)
            for t in range(NT):
                ins = nc.vector.bn_stats(d_st[:, t, :], x_all[:, t, :])
            link(ins)
            for t in range(NT):
                ins = nc.vector.bn_aggr(d_mv[:, t, :], d_st[:, t, :])
            link(ins)
            nc.vector.tensor_scalar(d_var, d_mv[:, :, 1], EPS, None, ALU.add).then_inc(d_stats, 1)
            dve.wait_ge(d_stats, 3)
            rsqrt_step(link, d_var, d_rstd, d_wn)
            dve.wait_ge(kept, 16 * (NT // KEEP))
            for t in range(NT):
                ins = nc.vector.tensor_scalar(x_all[:, t, :], x_all[:, t, :], d_mv[:, t, 0:1], d_rstd[:, t:t + 1],
                                              ALU.subtract, ALU.mult)
            link(ins)
            nc.vector.tensor_copy(d_xs, x_all[:, 0:TPS, :]).then_inc(s_xs, 1)
            front_split(dve, 0, link, True)
            for j in range(TPS):
                front_norm(dve, 0, j, link, True)
            before = link.n
            with dve.Fori(0, LAYERS) as layer:
                link = Chain(dve, d_chain, 1 + SEQS * D_LINKS, layer)
                link.base = link.base + before
                split_weights(dve, layer + 1, link)
                with dve.Fori(0, SEQS) as b:
                    n = layer * SEQS + b
                    f = n + 1
                    link = Chain(dve, d_chain, D_LINKS, n)
                    link.base = link.base + (layer + 1 + before)
                    dve.wait_ge(s_tp, slot_of(n, 0))
                    dve.wait_ge(s_x_done, n + 1)
                    nc.vector.tensor_copy(d_xs, x_all[:, bass.ds((f & (SEQS - 1)) * TPS, TPS), :]).then_inc(s_xs, 1)
                    softmax_max(dve, n, 0, link)
                    front_split(dve, f, link, False)
                    front_norm(dve, f, 0, link, False)
                    softmax_prob(dve, n, 0, link)
                    softmax_max(dve, n, 1, link)
                    front_norm(dve, f, 1, link, False)
                    softmax_prob(dve, n, 1, link)
                    for j in range(TPS):
                        dve.wait_ge(s_acc, TPS * n + j + 2)
                        xs = x_all[:, bass.ds(b * TPS + j, 1), :].rearrange("p a c -> p (a c)")
                        nc.vector.tensor_tensor(d_x2[:, j, :], xs, bank[j][:, 0:C], ALU.add).then_inc(s_x2, 1)
                    dve.wait_ge(s_mean, n + 1)
                    link(nc.vector.tensor_tensor(d_xc, d_xf, bank[7][:, 0:T], ALU.subtract))
                    nc.vector.tensor_tensor(d_v, d_xc, d_xc, ALU.mult).then_inc(s_xsq, 1)
                    dve.wait_ge(s_varp, n + 1)
                    nc.vector.tensor_scalar(d_v, bank[6][:, 0:T], EPS, None, ALU.add).then_inc(s_var, 1)
                    dve.wait_ge(s_y2, n + 1)
                    rsqrt_step(link, d_v, d_r, d_wf)
                    link(nc.vector.tensor_tensor(d_xc, d_xc, d_r, ALU.mult))
                    dve.wait_ge(loaded_ff, 16 * LOADS_FF * (layer + 1))
                    nc.vector.tensor_scalar(d_xn, d_xc, cols_d[:, 0:1], cols_d[:, 1:2], ALU.mult, ALU.add).then_inc(s_xn, 1)
                    for c, m in enumerate(FBLK):
                        dve.wait_ge(s_gl, NF * n + c + 1)
                        nc.vector.scalar_tensor_tensor(d_h[0:m, c, :], bank[7 - c % 2][0:m, T:2 * T], cols_d[0:m, 2 + c:3 + c],
                                                       d_gl[0:m, c % 2, :], ALU.add, ALU.mult).then_inc(s_h, 1)
                    dve.wait_ge(s_ffo, n + 1)
                    nc.vector.tensor_tensor(x_all[:, bass.ds(b * TPS, TPS), :], d_x2,
                                            bank[0][:, 0:T].rearrange("p (t c) -> p t c", t=TPS), ALU.add).then_inc(s_x_done, 1)
                    link.end()
            dve.wait_ge(s_x_done, LAYERS * SEQS + 1)

        def add_kept(dve):
            for g in range(NT // KEEP):
                dve.wait_ge(back[g], 16)
                s = slice(g * KEEP, (g + 1) * KEEP)
                nc.vector.tensor_tensor(x_all[:, s, :], x_all[:, s, :], x_kept[:, s, :], ALU.add).then_inc(s_x_done, 1)


        def slot_of(n, s):
            return SLOTS0 + SLOTS * n + s

        def xt_slot(f, first):
            return 0 if first else slot_of(f - 1, 2)

        def slot_bank(s):
            return bank[4 + s % 2]

        def phase_d_scalar(act):
            def front_xt(slot, s, f, first):
                act.wait_ge(s_tp, slot + 1)
                if not first:
                    act.wait_ge(s_split, f)
                src = slot_bank(s)
                nc.scalar.activation(d_xt[0:C // 2, XT0:], src[0:C // 2, 0:T], ACT.Copy)
                nc.scalar.activation(d_xt[C // 2:C, XT0 + 1:], src[C // 2:C, 0:T - 1], ACT.Copy).then_inc(s_tev, 1)

            def front_raw(f, j, first):
                i = TPS * f + j
                for c in range(4):
                    act.wait_ge(s_proj, 4 * i + c + 1)
                    if c == 0 and not (first and j == 0):
                        act.wait_ge(s_norm, i)
                    nc.scalar.activation(d_raw[:, 8 * c:8 * c + 8, :], bank[c % 2][:, :].rearrange("p (h d) -> p h d", h=8),
                                         ACT.Copy).then_inc(s_raw, 1)

            def front_sq(f, j, first):
                i = TPS * f + j
                act.wait_ge(s_raw, 4 * i + 4)
                if not (first and j == 0):
                    act.wait_ge(s_rope, i)
                nc.scalar.activation(d_sq, d_raw, ACT.Square).then_inc(s_sq, 1)
                act.wait_ge(s_ss, i + 1)
                nc.scalar.activation(d_y, d_ss, ACT.Ln).then_inc(d_act_chain, 1)
                act.wait_ge(d_act_chain, i + 1)
                nc.scalar.activation(d_y, d_y, ACT.Exp, scale=-0.5).then_inc(s_y, 1)

            def front_qk(slot0, s0, j):
                for q in range(4):
                    act.wait_ge(s_tp, slot0 + q + 1)
                    src = slot_bank(s0 + q)[:, :].rearrange("p (a t) -> p a t", a=4)
                    a = 4 * (q % 2)
                    if q < 2:
                        nc.scalar.activation(d_q[:, a:a + 4, j * P:(j + 1) * P], src, ACT.Copy).then_inc(s_tev, 1)
                    else:
                        at = WIN + j * P
                        nc.scalar.activation(d_k[0:DH, a:a + 4, 0, at:at + P], src[0:DH], ACT.Copy)
                        nc.scalar.activation(d_k[DH:P, a:a + 4, 1, at:at + P], src[DH:P], ACT.Copy).then_inc(s_tev, 1)

            def softmax_exp(n, j):
                i = TPS * n + j
                act.wait_ge(s_sub, i + 2)
                nc.scalar.activation(d_e, d_e, ACT.Exp, scale=8.0).then_inc(s_exp, 1)

            act.wait_ge(d_zero, 5)
            act.wait_ge(d_stats, 1)
            nc.scalar.activation(d_rstd, d_var, ACT.Ln).then_inc(d_stats, 1)
            act.wait_ge(d_stats, 2)
            nc.scalar.activation(d_rstd, d_rstd, ACT.Exp, scale=-0.5).then_inc(d_stats, 1)
            front_xt(0, 1, 0, True)
            for j in range(TPS):
                front_raw(0, j, True)
                front_sq(0, j, True)
            for j in range(TPS):
                front_qk(1 + 4 * j, 2 + 4 * j, j)
            with act.Fori(0, LAYERS) as layer:
                for g in range(4):
                    act.wait_ge(s_m, 4 * layer + g + 1)
                    nc.scalar.activation(wv_wo_slots(0, g), bank[6 + g % 2][:, :].rearrange("p (h c) -> p h c", h=4),
                                         ACT.Copy).then_inc(s_m_ready, 1)
                with act.Fori(0, SEQS) as b:
                    n = layer * SEQS + b
                    f = n + 1
                    nc.scalar.preload_act_table_set(EXP_SET)
                    act.wait_ge(s_py, NW * n + 1)
                    for s, hd, first, lo, hi in ((0, 0, 2, 0, 2), (0, 1, 0, 0, 4), (1, 0, 0, 2, 6), (1, 1, 0, 4, 8), (2, 0, 2, 6, 8)):
                        if hd == 0:
                            act.wait_ge(s_tp, slot_of(n, s) + 1)
                        rows = slice(hd * DH, (hd + 1) * DH)
                        last = nc.scalar.activation(
                            d_xw[hd][rows, lo:hi, :],
                            slot_bank(s)[rows, first * P:(first + hi - lo) * P].rearrange("p (w c) -> p w c", c=P), ACT.Copy)
                        if hd == 1:
                            last.then_inc(s_tev, 1)
                    front_xt(slot_of(n, 2), 2, f, False)
                    for j in range(TPS):
                        front_raw(f, j, False)
                        softmax_exp(n, j)
                        front_sq(f, j, False)
                    for j in range(TPS):
                        for s in range(3 + 2 * j, 5 + 2 * j):
                            act.wait_ge(s_tp, slot_of(n, s) + 1)
                            act.wait_ge(s_py, NW * n + WPT * j + 1)
                            a = 4 * ((s - 3) % 2)
                            nc.scalar.activation(d_pt[:, a:a + 4, :], slot_bank(s)[:, :].rearrange("p (a q) -> p a q", a=4),
                                                 ACT.Copy).then_inc(s_tev, 1)
                        act.wait_ge(s_acc, TPS * n + j + 1)
                        for w in range(WPT):
                            act.wait_ge(s_py, NW * n + WPT * j + w + 2)
                            nc.scalar.activation(d_yt[:, :, w * WIN:(w + 1) * WIN],
                                                 bank[6 + w % 2][:, :].rearrange("p (h q) -> p h q", h=H), ACT.Copy)\
                                .then_inc(s_yev, 1)
                    for j in range(TPS):
                        front_qk(slot_of(n, 7 + 4 * j), 7 + 4 * j, j)
                    act.wait_ge(s_tp, slot_of(n, 15) + 1)
                    src = slot_bank(15)
                    nc.scalar.activation(d_xf[0:C // 2, :], src[0:C // 2, 0:T], ACT.Copy)
                    nc.scalar.activation(d_xf[C // 2:C, 1:], src[C // 2:C, 0:T - 1], ACT.Copy).then_inc(s_tev, 1)
                    act.wait_ge(s_var, n + 1)
                    nc.scalar.activation(d_r, d_v, ACT.Ln).then_inc(s_ln, 1)
                    act.wait_ge(s_ln, n + 1)
                    nc.scalar.activation(d_r, d_r, ACT.Exp, scale=-0.5).then_inc(s_y2, 1)
                    nc.scalar.preload_act_table(ACT.Gelu)
                    for c, m in enumerate(FBLK):
                        act.wait_ge(s_up, NF * n + c + 1)
                        if c >= 2:
                            act.wait_ge(s_h, NF * n + c - 1)
                        nc.scalar.activation(d_gl[0:m, c % 2, :], bank[7 - c % 2][0:m, 0:T], ACT.Gelu,
                                             bias=cols_d[0:m, 2 + NF + c:3 + NF + c]).then_inc(s_gl, 1)

        def phase_d_gpsimd(pool):
            def tables(layer_next):
                par = layer_next & 1
                pool.wait_ge(loaded_sc, 16 * (layer_next + 1))
                for m in range(2):
                    sc = qk_scale[:, m * DH:(m + 1) * DH]
                    half = DH // 2
                    nc.gpsimd.tensor_tensor(rope_d[:, bass.ds(par, 1), :, m, :].rearrange("p a t d -> p (a t) d"),
                                            rope[:, :, m, :], sc.unsqueeze(1).to_broadcast([P, TPS, DH]), ALU.mult)
                    for a, z in ((0, half), (half, 0)):
                        last = nc.gpsimd.tensor_tensor(
                            rope_d[:, bass.ds(par, 1), :, 2 + m, a:a + half].rearrange("p a t d -> p (a t) d"),
                            rope[:, :, 2 + m, a:a + half], sc[:, z:z + half].unsqueeze(1).to_broadcast([P, TPS, half]), ALU.mult)
                last.then_inc(s_tab, 1)

            def rotate(f, j, first):
                i = TPS * f + j
                par = (f >> 4) & 1 if not first else 0
                half = DH // 2
                pool.wait_ge(s_tab, ((f >> 4) if not first else 0) + 1)
                pool.wait_ge(s_norm, i + 1)
                for m in range(2):
                    for a, z in ((0, half), (half, 0)):
                        last = nc.gpsimd.tensor_tensor(
                            d_t2[:, m * H:(m + 1) * H, a:a + half], d_nrm[:, m * H:(m + 1) * H, z:z + half],
                            rope_d[:, bass.ds(par, 1), j, 2 + m, a:a + half].to_broadcast([P, H, half]), ALU.mult)
                last.then_inc(d_pool_chain, 1)
                pool.wait_ge(d_pool_chain, i + 1)
                pool.wait_ge(s_t1, 2 * i + 2)
                nc.gpsimd.tensor_tensor(d_rot[j], d_rot[j], d_t2, ALU.add).then_inc(s_rope, 1)

            pool.wait_ge(loaded_const, LOADS_CONST * 16)
            tables(0)
            for j in range(TPS):
                rotate(0, j, True)
            with pool.Fori(0, LAYERS) as layer:
                tables(layer + 1)
                with pool.Fori(0, SEQS) as b:
                    for j in range(TPS):
                        rotate(layer * SEQS + b + 1, j, False)

        def phase_d_tensor(pe):
            def slot_free(slot):
                if not (isinstance(slot, int) and slot < 2):
                    pe.wait_ge(s_tev, slot - 1)

            def front_xt(slot, s, f, first):
                pe.wait_ge(s_xs, f + 1)
                slot_free(slot)
                for t in range(TPS):
                    last = nc.tensor.transpose(slot_bank(s)[:, t * P:(t + 1) * P], d_xs[:, t, :], ident[:, :])
                if not first:
                    for q in range(2):
                        at = (NW + q) * WIN
                        last = nc.tensor.transpose(slot_bank(s)[0:DH, T + q * P:T + (q + 1) * P], d_xt[:, at:at + 2 * WIN],
                                                   ident[:, :])
                last.then_inc(s_tp, 1)

            def front_project(f, j, n, first):
                i = TPS * f + j
                par = (f >> 4) & 1 if not first else 0
                pe.wait_ge(s_split, f + 1)
                pe.wait_ge(s_wsplit, ((f >> 4) if not first else 0) + 1)
                if not first and j == 0:
                    pe.wait_ge(s_x_done, n + 1)
                for c in range(4):
                    if not (first and j == 0 and c < 2):
                        pe.wait_ge(s_raw, 4 * i + c - 1)
                    for q, (xp, wp) in enumerate(((0, 0), (1, 0), (0, 1))):
                        w = wqk_split[:, bass.ds(par, 1), wp, c * 512:(c + 1) * 512].rearrange("p a n -> p (a n)")
                        last = nc.tensor.matmul(bank[c % 2][:, :], x_split[:, xp, j * P:(j + 1) * P], w,
                                                start=(q == 0), stop=(q == 2))
                    last.then_inc(s_proj, 1)

            def front_transpose(slot0, s0, f, j):
                pe.wait_ge(s_rope, TPS * f + j + 1)
                for q in range(4):
                    slot_free(slot0 + q)
                    for a in range(4):
                        h = 2 * (4 * q + a)
                        last = nc.tensor.transpose(slot_bank(s0 + q)[:, a * P:(a + 1) * P],
                                                   d_rot[j][:, h:h + 2, :].rearrange("p h d -> p (h d)"), ident[:, :])
                    last.then_inc(s_tp, 1)

            def scores(n, j):
                pe.wait_ge(s_sub, TPS * n + j + 1)
                for b in range(2):
                    nc.tensor.matmul(bank[2 + b][:, :], ident_bf[:, :], mask_bf[:, j, :, :].rearrange("p h k -> p (h k)"),
                                     start=True, stop=True)
                for a in range(PAIRS):
                    for w in range(WPT):
                        at = j * P + w * WIN
                        last = nc.tensor.matmul(bank[2 + a // 4][w * WIN:(w + 1) * WIN, (a % 4) * P:(a % 4 + 1) * P],
                                                d_q[:, a, at:at + WIN], d_k[:, a, :, at:at + 2 * WIN], start=False, stop=True, skip_group_check=True,
                                                tile_position=(0, w * WIN))
                last.then_inc(s_s, 1)

            def window_tokens(n):
                for s in range(2):
                    slot_free(slot_of(n, s))
                    for q in range(4):
                        at = (4 * s + q) * WIN
                        last = nc.tensor.transpose(slot_bank(s)[:, q * P:(q + 1) * P], d_xt[:, at:at + P], ident[:, :])
                    last.then_inc(s_tp, 1)

            def attend(n, j):
                i = TPS * n + j
                pe.wait_ge(s_prob, i + 1)
                for q in range(2):
                    s = 3 + 2 * j + q
                    slot_free(slot_of(n, s))
                    for a in range(4):
                        h = 2 * (4 * q + a)
                        last = nc.tensor.transpose(slot_bank(s)[:, a * P:(a + 1) * P],
                                                   d_e[:, h:h + 2, :].rearrange("p h k -> p (h k)"), ident[:, :])
                    last.then_inc(s_tp, 1)
                pe.wait_ge(s_tev, slot_of(n, 5 + 2 * j))
                for w in range(WPT):
                    pe.wait_ge(s_yev, NW * n + WPT * j + w + 1)
                    for hd in range(2):
                        last = nc.tensor.matmul(bank[6 + w % 2][:, hd * T:(hd + 1) * T], d_xw[hd][:, WPT * j + w, :],
                                                d_pt[:, :, w * WIN:(w + 1) * WIN], start=True, stop=True)
                    last.then_inc(s_py, 1)
                pe.wait_ge(s_yev, NW * n + WPT * (j + 1) + 2)
                for r in range(H):
                    last = nc.tensor.matmul(bank[j][:, 0:C], d_yt[:, r, :], m_vo[:, 0, r, :], start=(r == 0), stop=(r == H - 1))
                last.then_inc(s_acc, 1)

            def ffn(n, layer):
                pe.wait_ge(s_x2, TPS * n + 2)
                slot_free(slot_of(n, 15))
                for t in range(TPS):
                    last = nc.tensor.transpose(slot_bank(15)[:, t * P:(t + 1) * P], d_x2[:, t, :], ident[:, :])
                last.then_inc(s_tp, 1)
                pe.wait_ge(s_tev, slot_of(n, 16))
                nc.tensor.matmul(bank[7][:, 0:T], mean_mat[:, :], d_xf, start=True, stop=True).then_inc(s_mean, 1)
                pe.wait_ge(s_xsq, n + 1)
                nc.tensor.matmul(bank[6][:, 0:T], mean_mat[:, :], d_v, start=True, stop=True).then_inc(s_varp, 1)
                pe.wait_ge(s_xn, n + 1)
                pe.wait_ge(loaded_ff, 16 * LOADS_FF * (layer + 1))
                for c, m in enumerate(FBLK):
                    if c >= 2:
                        pe.wait_ge(s_h, NF * n + c - 1)
                    for half, first in ((0, FF), (1, 0)):
                        last = nc.tensor.matmul(bank[7 - c % 2][0:m, half * T:(half + 1) * T],
                                                w1[:, first + c * P:first + c * P + m], d_xn, start=True, stop=True)
                    last.then_inc(s_up, 1)
                for t in range(TPS):
                    for c, m in enumerate(FBLK):
                        if t == 0:
                            pe.wait_ge(s_h, NF * n + c + 1)
                        nc.tensor.matmul(bank[0][:, t * C:(t + 1) * C], d_h[0:m, c, t * P:(t + 1) * P], w2[0:m, c, :],
                                         start=(c == 0), stop=False)
                    last = nc.tensor.matmul(bank[0][:, t * C:(t + 1) * C], ones_row[:, :], b2[:, :], start=False, stop=True)
                last.then_inc(s_ffo, 1)

            pe.wait_ge(d_zero, 5)
            front_xt(0, 1, 0, True)
            for j in range(TPS):
                front_project(0, j, None, True)
            for j in range(TPS):
                front_transpose(1 + 4 * j, 2 + 4 * j, 0, j)
            with pe.Fori(0, LAYERS) as layer:
                pe.wait_ge(loaded_vo, 32 * (layer + 1))
                wv_wo(pe, s_m, s_m_ready, 4 * layer, 6)
                with pe.Fori(0, SEQS) as b:
                    n = layer * SEQS + b
                    pe.wait_ge(s_m_ready, 4 * layer + 4)
                    pe.wait_ge(s_tev, slot_of(n, 0))
                    scores(n, 0)
                    window_tokens(n)
                    front_xt(slot_of(n, 2), 2, n + 1, False)
                    front_project(n + 1, 0, n, False)
                    scores(n, 1)
                    front_project(n + 1, 1, n, False)
                    for j in range(TPS):
                        attend(n, j)
                    for j in range(TPS):
                        front_transpose(slot_of(n, 7 + 4 * j), 7 + 4 * j, n + 1, j)
                    ffn(n, layer)

        def load_layer(sp, layer, qk, rest):
            at = (layer if isinstance(layer, int) else layer % LAYERS)

            def of(name):
                return dram[name][bass.ds(at, 1)].rearrange("a p n -> (a p) n")

            if qk:
                if qk != "first":
                    sp.wait_ge(s_wsplit, layer)
                sp.dma_start(wqk_stage[:, :], of("wqk")).then_inc(loaded_qk, 16)
                if qk != "first":
                    sp.wait_ge(s_tab, layer)
                sp.dma_start(qk_scale[:, :], of("qk_scale").to_broadcast([P, 2 * DH])).then_inc(loaded_sc, 16)
            if rest:
                if rest != "first":
                    sp.wait_ge(s_m, 4 * layer)
                sp.dma_start(wvt[:, :, :], of("wvt").rearrange("(a p) c -> p a c", p=P)).then_inc(loaded_vo, 16)
                sp.dma_start(wo[:, :, :], of("wo").rearrange("(a p) c -> p a c", p=P)).then_inc(loaded_vo, 16)
                if rest != "first":
                    sp.wait_ge(s_ffo, SEQS * layer)
                sp.dma_start(w1[:, :], of("w1")).then_inc(loaded_ff, 16)
                full = FF // P
                sp.dma_start(w2[:, 0:full, :], of("w2")[0:full * P, :].rearrange("(b p) c -> p b c", p=P)).then_inc(loaded_ff, 16)
                sp.dma_start(w2[0:FBLK[-1], full, :], of("w2")[full * P:FF, :]).then_inc(loaded_ff, 16)
                sp.dma_start(cols_d[:, :], of("cols_d")).then_inc(loaded_ff, 16)
                sp.dma_start(b2[:, :], of("b2")).then_inc(loaded_ff, 16)

        block = ctx.enter_context(nc.Block())

        @block.sync
        def _(sp):
            sp.dma_start(x_all[:, :, :], dram["x"].rearrange("n p c -> p n c")).then_inc(loaded_x, 16)
            sp.dma_start(cols_a, dram["cols_a"]).then_inc(loaded_a, 16)
            sp.dma_start(ident[:, :], dram["ident"]).then_inc(loaded_const, 16)
            sp.dma_start(wa, dram["wa"]).then_inc(loaded_a, 16)
            sp.dma_start(wcv, dram["wcv"].rearrange("(b p) c -> p b c", p=P)).then_inc(loaded_a, 16)
            sp.dma_start(mask_stage, dram["mask"].rearrange("t p k -> p t k")).then_inc(loaded_const, 16)
            for k in range(4):
                sp.dma_start(rope[:, :, k, :], dram["rope"][k].rearrange("(t p) d -> p t d", p=P)).then_inc(loaded_const, 16)
            sp.dma_start(cols_b, dram["cols_b"]).then_inc(loaded_b, 16)
            sp.dma_start(wb1, dram["wb1"]).then_inc(loaded_b, 16)
            sp.dma_start(wbh, dram["wbh"].rearrange("l (b p) n -> p l b n", p=P)).then_inc(loaded_b, 16)
            sp.dma_start(wb3, dram["wb3"].rearrange("(b p) c -> p b c", p=P)).then_inc(loaded_b, 16)
            sp.dma_start(wqk_c, dram["wqk_c"]).then_inc(loaded_c, 16)
            sp.dma_start(wvt[:, :, :], dram["wvt_c"].rearrange("(a p) c -> p a c", p=P)).then_inc(loaded_c, 16)
            sp.dma_start(wo[:, :, :], dram["wo_c"].rearrange("(a p) c -> p a c", p=P)).then_inc(loaded_c, 16)
            sp.dma_start(bo[:, :], dram["bo"]).then_inc(loaded_c, 16)
            sp.wait_ge(const_ready, CONSTS)
            sp.wait_ge(loaded_c, LOADS_C * 16)
            sp.wait_ge(c_m, H // 4)
            load_layer(sp, 0, "first", "first")
            sp.wait_ge(phase_end, 4 * 3)
            for g in range(NT // KEEP):
                s = slice(g * KEEP, (g + 1) * KEEP)
                sp.dma_start(out[s].rearrange("n p c -> p n c"), x_all[:, s, :]).then_inc(kept, 16)
            with sp.Fori(0, LAYERS) as layer:
                load_layer(sp, layer + 1, True, True)
            sp.wait_ge(loaded_x, 16)
            sp.wait_ge(loaded_qk, 16 * (LAYERS + 1))
            sp.wait_ge(loaded_sc, 16 * (LAYERS + 1))
            sp.wait_ge(loaded_vo, 32 * (LAYERS + 1))
            sp.wait_ge(loaded_ff, 16 * LOADS_FF * (LAYERS + 1))
            sp.wait_ge(phase_end, 4 * PHASES)
            sp.wait_ge(kept, 16 * (NT // KEEP))
            for g in range(NT // KEEP):
                s = slice(g * KEEP, (g + 1) * KEEP)
                sp.dma_start(x_kept[:, s, :], out[s].rearrange("n p c -> p n c")).then_inc(back[g], 16)
            for g in range(NT // KEEP):
                s = slice(g * KEEP, (g + 1) * KEEP)
                sp.wait_ge(s_x_done, LAYERS * SEQS + 2 + g)
                sp.dma_start(out[s].rearrange("n p c -> p n c"), x_all[:, s, :]).then_inc(stored, 16)
            sp.wait_ge(stored, 16 * (NT // KEEP))
            sp.wait_ge(loaded_a, LOADS_A * 16)
            sp.wait_ge(loaded_b, LOADS_B * 16)
            sp.wait_ge(loaded_c, LOADS_C * 16)

        @block.vector
        def _(dve):
            dve.wait_ge(loaded_const, LOADS_CONST * 16)
            nc.vector.tensor_copy(ident_bf[:, :], ident[:, :]).then_inc(const_ready, 1)
            for t in range(TPS):
                nc.vector.tensor_copy(mask_bf[:, t, :, :], mask_stage[:, t, :].unsqueeze(1).to_broadcast([P, 8, 2 * WIN]))\
                    .then_inc(const_ready, 1)
            nc.vector.memset(ones_row[:, :], 1.0).then_inc(const_ready, 1)
            nc.vector.memset(mean_mat[:, :], 1.0 / C).then_inc(const_ready, 1)
            dve.wait_ge(loaded_x, 16)
            phase_a_vector_start(dve)
            with dve.Fori(0, SA) as step:
                phase_a_vector_steps(dve, step)
            end_phase(dve, 1)
            nc.vector.memset(b_w[:, :NT // 2], 0.0).then_inc(b_x_done, 1)
            nc.vector.memset(b_w[:, NT // 2:], 0.0).then_inc(b_down, 1)
            phase_b_vector(dve)
            end_phase(dve, 2)
            phase_c_vector(dve)
            end_phase(dve, 3)
            phase_d_vector(dve)
            end_phase(dve, 4)
            add_kept(dve)

        @block.scalar
        def _(act):
            nc.scalar.preload_act_table_set(EXP_SET)
            act.wait_ge(const_ready, CONSTS)
            act.wait_ge(loaded_a, LOADS_A * 16)
            with act.Fori(0, SA) as step:
                phase_a_scalar_steps(act, step)
            end_phase(act, 1)
            phase_b_scalar(act)
            end_phase(act, 2)
            nc.scalar.preload_act_table_set(EXP_SET)
            phase_c_scalar(act)
            end_phase(act, 3)
            nc.scalar.preload_act_table_set(EXP_SET)
            phase_d_scalar(act)
            end_phase(act, 4)

        @block.gpsimd
        def _(pool):
            with pool.Fori(0, SA) as step:
                phase_a_gpsimd_steps(pool, step)
            end_phase(pool, 1)
            end_phase(pool, 2)
            end_phase(pool, 3)
            phase_d_gpsimd(pool)
            end_phase(pool, 4)

        @block.tensor
        def _(pe):
            pe.wait_ge(const_ready, CONSTS)
            pe.wait_ge(loaded_const, LOADS_CONST * 16)
            pe.wait_ge(loaded_a, LOADS_A * 16)
            with pe.Fori(0, SA) as step:
                phase_a_tensor_steps(pe, step)
            end_phase(pe, 1)
            phase_b_tensor(pe)
            end_phase(pe, 2)
            phase_c_tensor(pe)
            end_phase(pe, 3)
            phase_d_tensor(pe)
            end_phase(pe, 4)


def rope_tables():
    import numpy as np

    half = np.arange(0, DH, 2, dtype=np.float32)
    inv_freq = (np.float32(1.0) / np.float32(10000.0) ** (half / np.float32(DH))).astype(np.float32)
    t = np.arange(T, dtype=np.float32)
    freqs = (t[:, None] * inv_freq[None, :]).astype(np.float32)
    freqs = np.concatenate([freqs, freqs], -1)
    base = ((half + np.float32(0.4 * DH)) / np.float32(1.4 * DH)).astype(np.float32)
    power = ((t - T // 2) / np.float32(WIN // 2)).astype(np.float32)
    scale = (base[None, :] ** power[:, None]).astype(np.float32)
    scale = np.concatenate([scale, scale], -1)
    sign = np.concatenate([-np.ones(DH // 2), np.ones(DH // 2)]).astype(np.float32)
    cos, sin = np.cos(freqs), np.sin(freqs) * sign
    inv = np.float32(1.0) / scale
    return np.stack([cos * scale, cos * inv, sin * scale, sin * inv]).astype(np.float32)


def window_masks():
    import numpy as np

    out = np.zeros((TPS, P, 2 * WIN), np.float32)
    r, k = np.arange(P) % WIN, np.arange(2 * WIN)
    banned = (k[None, :] - WIN > r[:, None]) | (r[:, None] > k[None, :])
    out[:] = np.where(banned, np.float32(MASKED), np.float32(0.0))
    out[0, :WIN, :WIN] = np.float32(MASKED)
    return out


def laid_out(inp):
    import numpy as np

    a = {k: np.asarray(v) for k, v in inp.items()}
    f = np.float32

    def block_cols(v):
        n = -(-v.shape[-1] // P)
        z = np.zeros(v.shape[:-1] + (n * P,), f)
        z[..., : v.shape[-1]] = v
        return np.swapaxes(z.reshape(v.shape[:-1] + (n, P)), -1, -2)

    d = {}
    d["x"] = a["L0_attn_x"].reshape(NT, P, C)
    d["ident"] = np.eye(P, dtype=f)
    d["mask"] = window_masks()
    d["rope"] = rope_tables()
    d["wa"] = np.concatenate([a["L0_attn_" + n].T for n in ("Wk", "Wv", "Wr", "Wcr", "Wck")], 1)
    d["wcv"] = a["L0_attn_Wcv"].T
    d["cols_a"] = np.stack([a["L0_attn_" + n].reshape(C) for n in
                            ("time_shift", "time_first", "ln1_w", "ln1_b", "ln2_w", "ln2_b")], 1)
    d["wb1"] = np.concatenate([a["L0_ffn_w1_w"].T, a["L0_ffn_w2_w"].T], 1)
    d["wbh"] = np.stack([a["L0_ffn_h1_w"].T, a["L0_ffn_h2_w"].T])
    d["wb3"] = a["L0_ffn_w3_w"].T
    d["cols_b"] = np.concatenate([block_cols(a["L0_ffn_" + n]) for n in ("w1_s", "w2_s", "h1_s", "h2_s", "w3_s")], 1)
    d["wqk_c"] = np.concatenate([a["L1_attn_Wq"], a["L1_attn_Wk"]], 1)
    d["wvt_c"] = a["L1_attn_Wv"].T
    d["wo_c"] = a["L1_attn_Wo"]
    d["bo"] = a["L1_attn_bo"].reshape(1, C)
    w = a["L1_ffn_Wqkv"]
    d["wqk"] = w[:, :, : 2 * INNER]
    d["wvt"] = np.swapaxes(w[:, :, 2 * INNER:], 1, 2)
    d["wo"] = a["L1_ffn_Wo"]
    d["qk_scale"] = np.concatenate([a["L1_ffn_q_scale"], a["L1_ffn_k_scale"]], 1).reshape(LAYERS, 1, 2 * DH)
    d["w1"] = a["L1_ffn_W1"]
    d["w2"] = a["L1_ffn_W2"]
    b1 = a["L1_ffn_b1"]
    d["cols_d"] = np.concatenate([a["L1_ffn_ln_g"][..., None], a["L1_ffn_ln_b"][..., None],
                                  block_cols(b1[:, :FF]), block_cols(b1[:, FF:])], 2)
    d["b2"] = a["L1_ffn_b2"].reshape(LAYERS, 1, C)
    return {k: np.ascontiguousarray(v) for k, v in d.items()}


def kernel(**inputs):
    import concourse.bacc as bacc
    from concourse.bass_utils import run_bass_kernel_spmd

    nc = bacc.Bacc("TRN2", target_bir_lowering=False, num_devices=1)
    arrays, dram = {}, {}
    for name, a in laid_out(inputs).items():
        arrays[f"in_{name}"] = a
        dram[name] = nc.dram_tensor(f"in_{name}", a.shape, mybir.dt.from_np(a.dtype), kind="ExternalInput").ap()
    out = nc.dram_tensor("out_x", (NT, P, C), F32, kind="ExternalOutput").ap()
    build(nc, dram, out)
    r = run_bass_kernel_spmd(nc, [arrays], core_ids=[0])
    return r.results[0]["out_x"].reshape(SEQS, T, C)
```

```python
import concourse.bass as bass
from concourse import mybir
from contextlib import ExitStack

F32 = mybir.dt.float32
F32R = mybir.dt.float32r
BF16 = mybir.dt.bfloat16
ACT = mybir.ActivationFunctionType
ALU = mybir.AluOpType
AXX = mybir.AxisListType.X

P = 128
C = 128
SEQS, T = 16, 256
NT = SEQS * T // P
TPS = T // P
H, DH = 16, 64
PAIRS = H // 2
INNER = H * DH
HID = 512
HB = HID // P
LAYERS = 6
WIN = 32
NW = T // WIN
WPT = P // WIN
FF = int(C * 4 * 2 / 3)
FBLK = [min(P, FF - c * P) for c in range(-(-FF // P))]
EPS = 1e-5
MASKED = -1.0e30
EXP_SET = "natural_log_exp_and_others"


class Chain:

    def __init__(self, eng, sem, per_step, step):
        self.eng, self.sem, self.base, self.per_step, self.n = eng, sem, step * per_step, per_step, 0

    def __call__(self, ins):
        self.n += 1
        ins.then_inc(self.sem, 1)
        self.eng.wait_ge(self.sem, self.base + self.n)

    def end(self):
        assert self.n == self.per_step, (self.n, self.per_step)
LOADS_A, LOADS_B, LOADS_C, LOADS_CONST, CONSTS = 3, 4, 4, 6, 5
PHASES = 4


def build(nc, dram, out):
    ctx = ExitStack()
    with ctx:
        def sb(name, shape, dt=F32):
            return ctx.enter_context(nc.sbuf_tensor(name, shape, dt))

        def sem(name):
            return ctx.enter_context(nc.semaphore(name))

        bank = [ctx.enter_context(nc.psum_tensor(f"bank{i}", [P, 512], F32)) for i in range(8)]

        x_all = sb("x_all", [P, NT + TPS, C])
        ident = sb("ident", [P, P])
        ident_bf = sb("ident_bf", [P, P], BF16)
        mask_bf = sb("mask_bf", [P, TPS, 8, 2 * WIN], BF16)
        ones_row = sb("ones_row", [1, P])
        mean_mat = sb("mean_mat", [P, P])
        rope = sb("rope", [P, TPS, 4, DH])
        rope_d = sb("rope_d", [P, 2, TPS, 4, DH])
        m_vo = sb("m_vo", [P, H, C])
        wvt = sb("wvt", [P, PAIRS, C])
        wo = sb("wo", [P, PAIRS, C])
        wqk_stage = sb("wqk_stage", [P, 2 * INNER])
        wqk_split = sb("wqk_split", [P, 2, 2, 2 * INNER], F32R)
        x_split = sb("x_split", [P, 2, T], F32R)
        w1 = sb("w1", [P, 2 * FF])
        w2 = sb("w2", [P, len(FBLK), C])
        cols_d = sb("cols_d", [P, 2 + 2 * len(FBLK)])
        b2 = sb("b2", [1, C])
        bo = sb("bo", [1, C])
        qk_scale = sb("qk_scale", [P, 2 * DH])

        ARENA = 29952
        arena = sb("arena", [P, ARENA])

        class Local:
            def __init__(self):
                self.at = 0

            def __call__(self, *shape):
                n = 1
                for s in shape:
                    n *= s
                v = arena[:, self.at:self.at + n]
                self.at += n
                assert self.at <= ARENA, self.at
                names = " ".join("abcd"[i] for i in range(len(shape)))
                if len(shape) > 1:
                    v = v.rearrange(f"p ({names}) -> p {names}", **{"abcd"[i]: s for i, s in enumerate(shape)})
                return v

        weights = Local()
        wa = weights(8 * C)
        wcv = weights(HB, C)
        cols_a = weights(6)
        wb1 = weights(2 * HID)
        wbh = weights(2, HB, HID)
        wb3 = weights(HB, C)
        cols_b = weights(4 * HB + 1)
        wqk_c = weights(2 * INNER)

        phase_end = sem("phase_end")

        def end_phase(eng, k):
            eng.drain().then_inc(phase_end, 1)
            eng.wait_ge(phase_end, 4 * k)

        loaded_x = sem("loaded_x")
        loaded_const = sem("loaded_const")
        loaded_a = sem("loaded_a")
        loaded_b = sem("loaded_b")
        loaded_c = sem("loaded_c")
        stored = sem("stored")
        const_ready = sem("const_ready")
        mask_stage = wqk_stage[:, 0:TPS * 2 * WIN].rearrange("p (t k) -> p t k", t=TPS)

        def rsqrt_step(link, v, y, w):
            link(nc.vector.tensor_tensor(w, y, y, ALU.mult))
            link(nc.vector.scalar_tensor_tensor(w, w, -0.5, v, ALU.mult, ALU.mult))
            link(nc.vector.scalar_tensor_tensor(y, w, 1.5, y, ALU.add, ALU.mult))

        LANES, UT = 2, 4
        UN = UT * P
        SA = NT // (UT * LANES)
        la = Local()
        la.at = weights.at

        def lanes(*shape):
            return [la(*shape) for _ in range(LANES)]

        a_st, a_mv, a_var, a_y, a_w = lanes(UT, 6), lanes(UT, 2), lanes(UT), lanes(UT), lanes(UT)
        a_x1, a_hn = lanes(UT, C), lanes(UT, C)
        a_x1t = lanes(2, T)
        a_h = lanes(2, T + 1)
        a_d, a_xxx = lanes(2, T), lanes(2, T)
        a_k, a_v, a_er = lanes(2, T), lanes(2, T), lanes(2, T)
        a_m, a_bs, a_aa = lanes(2, T + 1), lanes(2, T + 1), lanes(2, T + 1)
        a_g = [v.rearrange("p a c -> p (a c)").rearrange("p (s t) -> p s t", s=2) for v in a_x1]
        a_ek = [v.rearrange("p a c -> p (a c)").rearrange("p (s t) -> p s t", s=2) for v in a_hn]
        a_e1b, a_e2b, a_e1, a_e2 = lanes(2, T), lanes(2, T), lanes(2, T), lanes(2, T)
        a_rk = [[v.rearrange("p s t -> p (s t)") for v in (a_k[i], a_v[i], a_e1b[i], a_e2b[i])] for i in range(LANES)]
        TS, TF, G1, B1, G2, B2 = (cols_a[:, i:i + 1] for i in range(6))

        def flat(v):
            return v.rearrange("p a b -> p (a b)")

        def seqs(v):
            return v.rearrange("p (s t) -> p s t", s=2)

        bT0, bT1, bK, bV = ([bank[4 * i + j] for i in range(LANES)] for j in range(4))
        (a_var1, a_y1, a_var2, a_y2, a_hn_ready, a_tr1, a_h_ready, a_xxx_ready, a_kvr, a_kv_ready, a_ge_in,
         a_ge, a_bs_ready, a_bb, a_e_in, a_e, a_er_plus, a_den, a_xr, a_tr2, a_var3, a_y3, a_h2n, a_tr3, a_h2_ready,
         a_xxx2, a_cr, a_ck, a_relu, a_rk_ready, a_cv, a_er2, a_out, a_tr4, a_x_done) = (sem("a_" + s) for s in (
             "var1 rstd1 var2 rstd2 hn transposed1 h xxx kvr kv ge_in ge cum lncum e_in e er_plus den xr transposed2 var3 rstd3 "
             "h2n transposed3 h2 xxx2 cr ck relu relu2 cv er2 out transposed4 x_done").split())
        a_fixed = sem("a_fixed")
        a_chain = sem("a_chain")
        a_act_chain = sem("a_act_chain")
        a_pool_chain = sem("a_pool_chain")

        def phase_a_vector_start(dve):
            dve.wait_ge(loaded_a, LOADS_A * 16)
            for i in range(LANES):
                nc.vector.tensor_copy(a_h[i][:, :, 0], cols_a[:, 0:1].to_broadcast([P, 2])).then_inc(a_fixed, 1)
                nc.vector.memset(a_m[i][:, :, 0], 0.0).then_inc(a_fixed, 1)
                nc.vector.memset(a_bs[i][:, :, 0], 1.0).then_inc(a_fixed, 1)
                nc.vector.memset(a_aa[i][:, :, 0], 0.0).then_inc(a_fixed, 1)
                nc.vector.memset(a_w[i], 0.0).then_inc(a_x_done, 1)
            dve.wait_ge(a_fixed, 4 * LANES)
            dve.wait_ge(a_x_done, LANES)

        def phase_a_vector_steps(dve, step):
            link = Chain(dve, a_chain, LANES * A_LINKS, step)
            n = LANES * step + 1

            def tiles(i, t):
                return x_all[:, bass.ds((LANES * step + i) * UT + t, 1), :].rearrange("p a c -> p (a c)")

            def stats(src, i):
                for t in range(UT):
                    ins = nc.vector.bn_stats(a_st[i][:, t, :], src(t))
                link(ins)
                nc.vector.memset(a_w[i], 0.0)
                for t in range(UT):
                    ins = nc.vector.bn_aggr(a_mv[i][:, t, :], a_st[i][:, t, :])
                link(ins)

            def normalise(dst, src, i):
                rsqrt_step(link, a_var[i], a_y[i], a_w[i])
                for t in range(UT):
                    last = nc.vector.tensor_scalar(dst[:, t, :], src(t), a_mv[i][:, t, 0:1], a_y[i][:, t:t + 1],
                                                   ALU.subtract, ALU.mult)
                return last

            for i in range(LANES):
                stats(lambda t: tiles(i, t), i)
                nc.vector.tensor_scalar(a_var[i], a_mv[i][:, :, 1], EPS, None, ALU.add).then_inc(a_var1, 1)
            for i in range(LANES):
                dve.wait_ge(a_y1, n + i)
                link(normalise(a_x1[i], lambda t: tiles(i, t), i))
                stats(lambda t: a_x1[i][:, t, :], i)
                nc.vector.tensor_scalar(a_var[i], a_mv[i][:, :, 1], EPS, None, ALU.add).then_inc(a_var2, 1)
            for i in range(LANES):
                dve.wait_ge(a_y2, n + i)
                normalise(a_hn[i], lambda t: a_x1[i][:, t, :], i).then_inc(a_hn_ready, 1)
            for i in range(LANES):
                dve.wait_ge(a_h_ready, n + i)
                link(nc.vector.tensor_tensor(a_d[i], a_h[i][:, :, 1:], a_h[i][:, :, :T], ALU.subtract))
                nc.vector.scalar_tensor_tensor(a_xxx[i], a_d[i], TS, a_h[i][:, :, 1:], ALU.mult, ALU.add)\
                    .then_inc(a_xxx_ready, 1)
            for i in range(LANES):
                dve.wait_ge(a_kv_ready, n + i)
                for s in range(2):
                    link(nc.vector.tensor_tensor_scan(a_m[i][:, s, 1:], a_k[i][:, s, :], a_k[i][:, s, :], 0.0,
                                                      ALU.max, ALU.max))
                nc.vector.tensor_tensor(a_g[i], a_m[i][:, :, :T], a_m[i][:, :, 1:], ALU.subtract).then_inc(a_ge_in, 1)
                nc.vector.tensor_tensor(a_ek[i], a_k[i], a_m[i][:, :, 1:], ALU.subtract).then_inc(a_ge_in, 1)
            for i in range(LANES):
                dve.wait_ge(a_ge, n + i)
                for s in range(2):
                    nc.vector.tensor_tensor_scan(a_bs[i][:, s, 1:], a_g[i][:, s, :], a_ek[i][:, s, :], 1.0,
                                                 ALU.mult, ALU.add).then_inc(a_bs_ready, 1)
            for i in range(LANES):
                dve.wait_ge(a_bb, n + i)
                link(nc.vector.tensor_tensor(a_d[i], a_d[i], a_m[i][:, :, :T], ALU.add))
                link(nc.vector.tensor_tensor(a_d[i], a_d[i], a_k[i], ALU.subtract))
                nc.vector.tensor_scalar(a_e1b[i], a_d[i], 0.0, None, ALU.min).then_inc(a_e_in, 1)
                nc.vector.tensor_scalar(a_e2b[i], a_d[i], 0.0, None, ALU.max).then_inc(a_e_in, 1)
                nc.vector.tensor_scalar(a_e1[i], a_d[i], TF, 0.0, ALU.subtract, ALU.min).then_inc(a_e_in, 1)
                nc.vector.tensor_scalar(a_e2[i], a_d[i], TF, 0.0, ALU.subtract, ALU.max).then_inc(a_e_in, 1)
            for i in range(LANES):
                dve.wait_ge(a_e, n + i)
                link(nc.vector.tensor_tensor(a_e2b[i], a_e2b[i], a_v[i], ALU.mult))
                for s in range(2):
                    link(nc.vector.tensor_tensor_scan(a_aa[i][:, s, 1:], a_e1b[i][:, s, :], a_e2b[i][:, s, :], 0.0,
                                                      ALU.mult, ALU.add))
                dve.wait_ge(a_den, n + i)
                link(nc.vector.tensor_tensor(a_d[i], a_e1[i], a_aa[i][:, :, :T], ALU.mult))
                link(nc.vector.tensor_tensor(a_d[i], a_d[i], a_e2[i], ALU.add))
                link(nc.vector.reciprocal(a_er[i], a_er[i]))
                link(nc.vector.tensor_tensor(a_d[i], a_d[i], a_er[i], ALU.mult))
                nc.vector.tensor_tensor(a_x1t[i], a_d[i], a_x1t[i], ALU.add).then_inc(a_xr, 1)
            for i in range(LANES):
                dve.wait_ge(a_tr2, n + i)
                stats(lambda t: bT1[i][:, t * C:(t + 1) * C], i)
                nc.vector.tensor_scalar(a_var[i], a_mv[i][:, :, 1], EPS, None, ALU.add).then_inc(a_var3, 1)
            for i in range(LANES):
                dve.wait_ge(a_y3, n + i)
                normalise(a_hn[i], lambda t: bT1[i][:, t * C:(t + 1) * C], i).then_inc(a_h2n, 1)
            for i in range(LANES):
                dve.wait_ge(a_h2_ready, n + i)
                link(nc.vector.tensor_tensor(a_d[i], a_h[i][:, :, :T], a_h[i][:, :, 1:], ALU.subtract))
                link(nc.vector.scalar_tensor_tensor(a_xxx[i], a_d[i], TS, a_h[i][:, :, 1:], ALU.mult, ALU.add))
                nc.vector.tensor_copy(a_h[i][:, :, 0], cols_a[:, 0:1].to_broadcast([P, 2])).then_inc(a_xxx2, 1)
            for i in range(LANES):
                dve.wait_ge(a_er2, n + i)
                link(nc.vector.reciprocal(a_er[i], a_er[i]))
                dve.wait_ge(a_cv, n + i)
                link(nc.vector.tensor_tensor(flat(a_d[i]), flat(a_er[i]), bK[i][:, :], ALU.mult))
                nc.vector.tensor_tensor(a_x1t[i], a_x1t[i], a_d[i], ALU.add).then_inc(a_out, 1)
            for i in range(LANES):
                dve.wait_ge(a_tr4, n + i)
                xs = x_all[:, bass.ds((LANES * step + i) * UT, UT), :]
                nc.vector.tensor_tensor(xs, xs, bT0[i][:, :].rearrange("p (t c) -> p t c", t=UT), ALU.add)\
                    .then_inc(a_x_done, 1)
            dve.wait_ge(a_x_done, n + 2 * LANES - 1)
            link.end()

        A_LINKS = 32

        def phase_a_scalar_steps(act, step):
            n = LANES * step + 1
            link = Chain(act, a_act_chain, 9 * LANES, step)

            def rstd(i):
                link(nc.scalar.activation(a_y[i], a_var[i], ACT.Ln))
                return nc.scalar.activation(a_y[i], a_y[i], ACT.Exp, scale=-0.5)

            for i in range(LANES):
                act.wait_ge(a_var1, n + i)
                rstd(i).then_inc(a_y1, 1)
            for i in range(LANES):
                act.wait_ge(a_var2, n + i)
                rstd(i).then_inc(a_y2, 1)
            for i in range(LANES):
                act.wait_ge(a_tr1, n + i)
                nc.scalar.activation(flat(a_x1t[i]), bT0[i][:, :], ACT.Copy)
                nc.scalar.activation(a_h[i][:, :, 1:], seqs(bT1[i][:, :]), ACT.Identity, bias=B1, scale=G1)\
                    .then_inc(a_h_ready, 1)
            for i in range(LANES):
                act.wait_ge(a_kvr, n + i)
                nc.scalar.activation(flat(a_k[i]), bK[i][:, :], ACT.Copy)
                nc.scalar.activation(flat(a_v[i]), bV[i][:, :], ACT.Copy)
                nc.scalar.activation(flat(a_er[i]), bT0[i][:, :], ACT.Exp, scale=-1.0).then_inc(a_kv_ready, 1)
            for i in range(LANES):
                act.wait_ge(a_ge_in, 2 * (n + i))
                nc.scalar.activation(a_g[i], a_g[i], ACT.Exp)
                nc.scalar.activation(a_ek[i], a_ek[i], ACT.Exp).then_inc(a_ge, 1)
                act.wait_ge(a_kv_ready, n + i)
                nc.scalar.activation(a_er[i], a_er[i], ACT.Identity, bias=1.0).then_inc(a_er_plus, 1)
            for i in range(LANES):
                act.wait_ge(a_bs_ready, 2 * (n + i))
                nc.scalar.activation(a_d[i], a_bs[i][:, :, :T], ACT.Ln).then_inc(a_bb, 1)
            for i in range(LANES):
                act.wait_ge(a_e_in, 4 * (n + i))
                nc.scalar.activation(a_e1[i], a_e1[i], ACT.Exp)
                nc.scalar.activation(a_e2[i], a_e2[i], ACT.Exp, scale=-1.0)
                nc.scalar.activation(a_e1b[i], a_e1b[i], ACT.Exp)
                nc.scalar.activation(a_e2b[i], a_e2b[i], ACT.Exp, scale=-1.0).then_inc(a_e, 1)
            for i in range(LANES):
                act.wait_ge(a_var3, n + i)
                rstd(i).then_inc(a_y3, 1)
            for i in range(LANES):
                act.wait_ge(a_tr3, n + i)
                link(nc.scalar.activation(a_h[i][:, :, 1:], seqs(bT1[i][:, :]), ACT.Identity, bias=B2, scale=G2))
                nc.scalar.activation(a_h[i][:, :, 0], a_h[i][:, :, T], ACT.Copy).then_inc(a_h2_ready, 1)
            for i in range(LANES):
                act.wait_ge(a_cr, n + i)
                link(nc.scalar.activation(flat(a_er[i]), bT0[i][:, :], ACT.Exp, scale=-1.0))
                nc.scalar.activation(a_er[i], a_er[i], ACT.Identity, bias=1.0).then_inc(a_er2, 1)
            for c in range(HB):
                for i in range(LANES):
                    act.wait_ge(a_ck, HB * LANES * step + c * LANES + i + 1)
                    src = (bV, bT1)[c % 2][i]
                    link(nc.scalar.activation(a_rk[i][c], src[:, :], ACT.Relu))
                    nc.scalar.activation(a_rk[i][c], a_rk[i][c], ACT.Square).then_inc(a_rk_ready, 1)
            link.end()

        def phase_a_gpsimd_steps(pool, step):
            n = LANES * step + 1
            link = Chain(pool, a_pool_chain, 2 * LANES, step)
            for i in range(LANES):
                pool.wait_ge(a_er_plus, n + i)
                pool.wait_ge(a_e, n + i)
                link(nc.gpsimd.tensor_tensor(a_g[i], a_e1[i], a_e2[i], ALU.add))
                link(nc.gpsimd.tensor_tensor(a_er[i], a_er[i], a_g[i], ALU.mult))
                nc.gpsimd.tensor_tensor(a_e2[i], a_e2[i], a_v[i], ALU.mult).then_inc(a_den, 1)
            link.end()

        def phase_a_tensor_steps(pe, step):
            n = LANES * step + 1

            def transposes(dst, src):
                for t in range(UT):
                    last = nc.tensor.transpose(dst[:, t * P:(t + 1) * P], src(t), ident[:, :])
                return last

            for i in range(LANES):
                pe.wait_ge(a_hn_ready, n + i)
                pe.wait_ge(a_x_done, n + i)
                transposes(bT0[i], lambda t: a_x1[i][:, t, :])
                transposes(bT1[i], lambda t: a_hn[i][:, t, :]).then_inc(a_tr1, 1)
            for i in range(LANES):
                pe.wait_ge(a_xxx_ready, n + i)
                for j, dst in enumerate((bK, bV, bT0)):
                    last = nc.tensor.matmul(dst[i][:, :], wa[:, j * C:(j + 1) * C], flat(a_xxx[i]), start=True, stop=True)
                last.then_inc(a_kvr, 1)
            for i in range(LANES):
                pe.wait_ge(a_xr, n + i)
                transposes(bT1[i], lambda t: flat(a_x1t[i])[:, t * P:(t + 1) * P]).then_inc(a_tr2, 1)
            for i in range(LANES):
                pe.wait_ge(a_h2n, n + i)
                transposes(bT1[i], lambda t: a_hn[i][:, t, :]).then_inc(a_tr3, 1)
            for i in range(LANES):
                pe.wait_ge(a_xxx2, n + i)
                nc.tensor.matmul(bT0[i][:, :], wa[:, 3 * C:4 * C], flat(a_xxx[i]), start=True, stop=True).then_inc(a_cr, 1)
            for c in range(HB):
                for i in range(LANES):
                    if c >= 2:
                        pe.wait_ge(a_rk_ready, HB * LANES * step + (c - 2) * LANES + i + 1)
                    dst = (bV, bT1)[c % 2][i]
                    nc.tensor.matmul(dst[:, :], wa[:, (4 + c) * C:(5 + c) * C], flat(a_xxx[i]), start=True, stop=True)\
                        .then_inc(a_ck, 1)
            for c in range(HB):
                for i in range(LANES):
                    pe.wait_ge(a_rk_ready, HB * LANES * step + c * LANES + i + 1)
                    last = nc.tensor.matmul(bK[i][:, :], wcv[:, c, :], a_rk[i][c], start=(c == 0), stop=(c == HB - 1))
                    if c == HB - 1:
                        last.then_inc(a_cv, 1)
            for i in range(LANES):
                pe.wait_ge(a_out, n + i)
                transposes(bT0[i], lambda t: flat(a_x1t[i])[:, t * P:(t + 1) * P]).then_inc(a_tr4, 1)

        SB_ = NT // UT
        lb = Local()
        lb.at = weights.at
        b_st, b_mv = lb(NT, 6), lb(NT, 2)
        b_var, b_y, b_w = lb(NT), lb(NT), lb(NT)
        b_xn = lb(UT, C)
        b_xt = lb(UN)
        b_sl = lb(2, UN)
        b_h = lb(HB, UN)
        b_g = lb(2, HB, UN)
        b_o = lb(UN)
        b_fixed, b_chain, b_rstd, b_xn_ready, b_xtp, b_xt_ready = (sem("b_" + s) for s in "fixed chain rstd xn xtp xt".split())
        b_up, b_silu, b_h_ready, b_hid, b_gelu, b_down, b_o_ready, b_ot, b_x_done = (
            sem("b_" + s) for s in "up silu h hid gelu down o ot x_done".split())

        def scale_b(layer, c):
            return cols_b[:, layer * HB + c:layer * HB + c + 1]

        def normalise_b(u):
            for t in range(UT):
                last = nc.vector.tensor_scalar(
                    b_xn[:, t, :], x_all[:, bass.ds(u * UT + t, 1), :].rearrange("p a c -> p (a c)"),
                    b_mv[:, bass.ds(u * UT + t, 1), 0], b_y[:, bass.ds(u * UT + t, 1)], ALU.subtract, ALU.mult)
            last.then_inc(b_xn_ready, 1)

        def phase_b_vector(dve):
            link = Chain(dve, b_chain, 5, 0)
            for t in range(NT):
                ins = nc.vector.bn_stats(b_st[:, t, :], x_all[:, t, :])
            link(ins)
            for t in range(NT):
                ins = nc.vector.bn_aggr(b_mv[:, t, :], b_st[:, t, :])
            link(ins)
            nc.vector.tensor_scalar(b_var, b_mv[:, :, 1], EPS, None, ALU.add).then_inc(b_fixed, 1)
            dve.wait_ge(b_rstd, 1)
            rsqrt_step(link, b_var, b_y, b_w)
            link.end()
            dve.wait_ge(loaded_b, LOADS_B * 16)
            normalise_b(0)
            with dve.Fori(0, SB_) as u:
                for c in range(HB):
                    dve.wait_ge(b_silu, HB * u + c + 1)
                    if c == 0:
                        dve.wait_ge(b_down, u + 1)
                    nc.vector.scalar_tensor_tensor(b_h[:, c, :], bank[2 + c % 2][:, :], scale_b(1, c), b_sl[:, c % 2, :],
                                                   ALU.mult, ALU.mult).then_inc(b_h_ready, 1)
                dve.wait_ge(b_xtp, u + 1)
                normalise_b((u + 1) & (SB_ - 1))
                dve.wait_ge(b_ot, u + 1)
                xs = x_all[:, bass.ds(u * UT, UT), :]
                nc.vector.tensor_tensor(xs, xs, bank[5][:, :].rearrange("p (t c) -> p t c", t=UT), ALU.add)\
                    .then_inc(b_x_done, 1)
            dve.wait_ge(b_x_done, SB_ + 1)

        def phase_b_scalar(act):
            act.wait_ge(b_fixed, 1)
            nc.scalar.activation(b_y, b_var, ACT.Ln).then_inc(b_fixed, 1)
            act.wait_ge(b_fixed, 2)
            nc.scalar.activation(b_y, b_y, ACT.Exp, scale=-0.5).then_inc(b_rstd, 1)
            act.wait_ge(loaded_b, LOADS_B * 16)
            act.wait_ge(b_xtp, 1)
            nc.scalar.activation(b_xt, bank[6][:, :], ACT.Copy).then_inc(b_xt_ready, 1)
            with act.Fori(0, SB_) as u:
                for c in range(HB):
                    act.wait_ge(b_up, HB * u + c + 1)
                    if c >= 2:
                        act.wait_ge(b_h_ready, HB * u + c - 1)
                    nc.scalar.activation(b_sl[:, c % 2, :], bank[c % 2][:, :], ACT.Silu, scale=scale_b(0, c))\
                        .then_inc(b_silu, 1)
                for layer in range(2):
                    for c in range(HB):
                        act.wait_ge(b_hid, 2 * HB * u + HB * layer + c + 1)
                        nc.scalar.activation(b_g[:, layer, c, :], bank[(4 if layer == 0 else 0) + c][:, :], ACT.Gelu,
                                             scale=scale_b(2 + layer, c)).then_inc(b_gelu, 1)
                act.wait_ge(b_xtp, u + 2)
                nc.scalar.activation(b_xt, bank[6][:, :], ACT.Copy).then_inc(b_xt_ready, 1)
                act.wait_ge(b_down, u + 2)
                nc.scalar.activation(b_o, bank[4][:, :], ACT.Copy, scale=scale_b(4, 0)).then_inc(b_o_ready, 1)

        def phase_b_tensor(pe):
            def transpose_tokens():
                for t in range(UT):
                    last = nc.tensor.transpose(bank[6][:, t * P:(t + 1) * P], b_xn[:, t, :], ident[:, :])
                last.then_inc(b_xtp, 1)

            pe.wait_ge(loaded_b, LOADS_B * 16)
            pe.wait_ge(b_xn_ready, 1)
            transpose_tokens()
            with pe.Fori(0, SB_) as u:
                pe.wait_ge(b_xt_ready, u + 1)
                for c in range(HB):
                    if c >= 2:
                        pe.wait_ge(b_h_ready, HB * u + c - 1)
                    nc.tensor.matmul(bank[c % 2][:, :], wb1[:, c * P:(c + 1) * P], b_xt, start=True, stop=True)
                    nc.tensor.matmul(bank[2 + c % 2][:, :], wb1[:, HID + c * P:HID + (c + 1) * P], b_xt,
                                     start=True, stop=True).then_inc(b_up, 1)
                for layer in range(2):
                    if layer == 0:
                        pe.wait_ge(b_x_done, u + 1)
                    for c in range(HB):
                        for k in range(HB):
                            if c == 0 and layer == 0:
                                pe.wait_ge(b_h_ready, HB * u + k + 1)
                            if c == 0 and layer == 1:
                                pe.wait_ge(b_gelu, 2 * HB * u + k + 1)
                            src = b_h[:, k, :] if layer == 0 else b_g[:, 0, k, :]
                            last = nc.tensor.matmul(bank[(4 if layer == 0 else 0) + c][:, :],
                                                    wbh[:, layer, k, c * P:(c + 1) * P], src,
                                                    start=(k == 0), stop=(k == HB - 1))
                        last.then_inc(b_hid, 1)
                pe.wait_ge(b_xn_ready, u + 2)
                transpose_tokens()
                for k in range(HB):
                    pe.wait_ge(b_gelu, 2 * HB * u + HB + k + 1)
                    last = nc.tensor.matmul(bank[4][:, :], wb3[:, k, :], b_g[:, 1, k, :], start=(k == 0), stop=(k == HB - 1))
                last.then_inc(b_down, 1)
                pe.wait_ge(b_o_ready, u + 1)
                for t in range(UT):
                    last = nc.tensor.transpose(bank[5][:, t * P:(t + 1) * P], b_o[:, t * P:(t + 1) * P], ident[:, :])
                last.then_inc(b_ot, 1)

        TURNS = TPS * PAIRS
        GROUPS = TURNS // 2
        lc = Local()
        lc.at = weights.at
        c_st, c_mv = lc(NT, 6), lc(NT, 2)
        c_var, c_y, c_w = lc(NT), lc(NT), lc(NT)
        c_xn, c_xv = lc(TPS, C), lc(TPS, C)
        c_xt = lc(T)
        c_q = lc(PAIRS, T)
        c_k = lc(PAIRS, 2, T)
        c_e = lc(3, 2, T)
        c_pt = lc(2, TPS, 4, P)
        c_yt = lc(H, P)
        c_nm, c_sum, c_inv = lc(3, 2), lc(3, 2), lc(3, 2)
        (c_fixed, c_chain, c_rstd, c_xn_ready, c_xv_ready, c_xtp, c_xt_ready, c_proj, c_q_ready, c_k_ready, c_s, c_max,
         c_exp, c_prob, c_ptp, c_pt_ready, c_py, c_yt_ready, c_acc, c_x_done, c_m, c_m_ready, c_recip) = (
            sem("c_" + s) for s in ("fixed chain rstd xn xv xtp xt proj q k s max exp prob ptp pt py yt acc x_done m m_ready "
                                    "recip").split())
        QSCALE = float(DH) ** -0.5

        def head_slot(h):
            return h % 2 * PAIRS + h // 2

        def wv_wo(pe, ready, done, base, first_bank=5):
            for g in range(4):
                if g >= 2:
                    pe.wait_ge(done, base + g - 1)
                d = g % 2 * DH
                for j in range(4):
                    a = 4 * (g // 2) + j
                    last = nc.tensor.matmul(bank[first_bank + g % 2][:, j * P:(j + 1) * P], wvt[d:d + DH, a, :], wo[d:d + DH, a, :],
                                            start=True, stop=True)
                last.then_inc(ready, 1)

        def wv_wo_slots(g):
            first = g % 2 * PAIRS + 4 * (g // 2)
            return m_vo[:, first:first + 4, :]

        def normalise_c(n):
            for t in range(TPS):
                last = nc.vector.tensor_scalar(
                    c_xn[:, t, :], x_all[:, bass.ds(n * TPS + t, 1), :].rearrange("p a c -> p (a c)"),
                    c_mv[:, bass.ds(n * TPS + t, 1), 0], c_y[:, bass.ds(n * TPS + t, 1)], ALU.subtract, ALU.mult)
            last.then_inc(c_xn_ready, 1)

        def phase_c_vector(dve):
            nc.vector.memset(c_k, 0.0).then_inc(c_fixed, 1)
            nc.vector.memset(c_nm, 0.0).then_inc(c_x_done, 1)
            nc.vector.memset(c_sum, 0.0).then_inc(c_py, 1)
            nc.vector.memset(c_inv, 0.0).then_inc(c_acc, 1)
            link = Chain(dve, c_chain, 5, 0)
            for t in range(NT):
                ins = nc.vector.bn_stats(c_st[:, t, :], x_all[:, t, :])
            link(ins)
            for t in range(NT):
                ins = nc.vector.bn_aggr(c_mv[:, t, :], c_st[:, t, :])
            link(ins)
            nc.vector.tensor_scalar(c_var, c_mv[:, :, 1], EPS, None, ALU.add).then_inc(c_fixed, 1)
            dve.wait_ge(c_rstd, 1)
            rsqrt_step(link, c_var, c_y, c_w)
            link.end()
            normalise_c(0)

            def keys(n):
                for g in range(4):
                    dve.wait_ge(c_proj, 8 * n + 4 + g + 1)
                    src = bank[5 + (g + 1) % 2][:, :].rearrange("p (a t) -> p a t", a=2)
                    nc.vector.tensor_copy(c_k[0:DH, 2 * g:2 * g + 2, 0, :], src[0:DH])
                    nc.vector.tensor_copy(c_k[DH:P, 2 * g:2 * g + 2, 1, :], src[DH:P]).then_inc(c_k_ready, 1)

            dve.wait_ge(c_fixed, 2)
            keys(0)
            with dve.Fori(0, SEQS) as n:
                dve.wait_ge(c_py, GROUPS * n + 1)
                dve.wait_ge(c_xn_ready, n + 1)
                nc.vector.tensor_copy(c_xv, c_xn).then_inc(c_xv_ready, 1)
                dve.wait_ge(c_xv_ready, n + 1)
                dve.wait_ge(c_xtp, n + 1)
                normalise_c((n + 1) & (SEQS - 1))
                for t in range(TURNS + 6):
                    if t < TURNS:
                        dve.wait_ge(c_s, TURNS * n + t + 1)
                        nc.vector.tensor_reduce(out=c_nm[:, t % 3, :], in_=bank[t % 3][:, :].rearrange("p (h k) -> p h k", h=2),
                                                op=ALU.max, axis=AXX, negate=True).then_inc(c_max, 1)
                    if 1 <= t <= TURNS:
                        r = (t - 1) % 3
                        dve.wait_ge(c_exp, 2 * (TURNS * n + t - 1) + 2)
                        nc.vector.reciprocal(c_inv[:, r, :], c_sum[:, r, :]).then_inc(c_recip, 1)
                        dve.wait_ge(c_recip, TURNS * n + t)
                        for hd in range(2):
                            last = nc.vector.tensor_scalar(c_e[:, r, hd, :], c_e[:, r, hd, :], c_inv[:, r, hd:hd + 1], None,
                                                           ALU.mult)
                        last.then_inc(c_prob, 1)
                    if t == TURNS:
                        keys(n + 1)
                    if t >= 5 and t % 2 == 1 and (t - 5) // 2 < GROUPS:
                        g = (t - 5) // 2
                        if g % 4 == 0:
                            dve.wait_ge(c_acc, TPS * n + g // 4 + 1)
                        dve.wait_ge(c_py, GROUPS * n + g + 2)
                        nc.vector.tensor_copy(c_yt[:, 4 * (g % 4):4 * (g % 4) + 4, :],
                                              bank[5][:, :].rearrange("p (h q) -> p h q", h=4)).then_inc(c_yt_ready, 1)
                    if t in (13, TURNS + 5):
                        j = 0 if t == 13 else 1
                        dve.wait_ge(c_acc, TPS * n + j + 2)
                        xs = x_all[:, bass.ds(n * TPS + j, 1), :].rearrange("p a c -> p (a c)")
                        nc.vector.tensor_tensor(xs, xs, bank[7][:, 0:C], ALU.add).then_inc(c_x_done, 1)
            dve.wait_ge(c_x_done, TPS * SEQS + 1)

        def phase_c_scalar(act):
            for g in range(H // 4):
                act.wait_ge(c_m, g + 1)
                nc.scalar.activation(wv_wo_slots(g), bank[5 + g % 2][:, :].rearrange("p (h c) -> p h c", h=4),
                                     ACT.Copy).then_inc(c_m_ready, 1)
            act.wait_ge(c_fixed, 2)
            nc.scalar.activation(c_y, c_var, ACT.Ln).then_inc(c_fixed, 1)
            act.wait_ge(c_fixed, 3)
            nc.scalar.activation(c_y, c_y, ACT.Exp, scale=-0.5).then_inc(c_rstd, 1)

            def queries(n):
                act.wait_ge(c_xtp, n + 1)
                nc.scalar.activation(c_xt, bank[7][:, 0:T], ACT.Copy).then_inc(c_xt_ready, 1)
                for g in range(4):
                    act.wait_ge(c_proj, 8 * n + g + 1)
                    nc.scalar.activation(c_q[:, 2 * g:2 * g + 2, :], bank[5 + (g + 1) % 2][:, :].rearrange("p (a t) -> p a t", a=2),
                                         ACT.Copy, scale=QSCALE).then_inc(c_q_ready, 1)

            queries(0)
            with act.Fori(0, SEQS) as n:
                for t in range(TURNS + 2):
                    if t < TURNS:
                        act.wait_ge(c_max, TURNS * n + t + 1)
                        if t >= 3:
                            act.wait_ge(c_ptp, TURNS * n + t - 2)
                        for hd in range(2):
                            nc.scalar.activation(c_e[:, t % 3, hd, :], bank[t % 3][:, hd * T:(hd + 1) * T], ACT.Exp,
                                                 bias=c_nm[:, t % 3, hd:hd + 1], accum_out=c_sum[:, t % 3, hd:hd + 1])\
                                .then_inc(c_exp, 1)
                    if t == TURNS:
                        queries(n + 1)
                    if t >= 2:
                        u = t - 2
                        g = u // 2
                        act.wait_ge(c_ptp, TURNS * n + u + 1)
                        if u % 2 == 0:
                            act.wait_ge(c_py, (GROUPS * n + g) if g >= 1 else GROUPS * n + 1)
                        nc.scalar.activation(c_pt[:, g % 2, :, 2 * (u % 2):2 * (u % 2) + 2, :],
                                             bank[3 + u % 2][:, :].rearrange("p (h k q) -> p k h q", h=2, k=TPS), ACT.Copy)\
                            .then_inc(c_pt_ready, 1)

        def phase_c_tensor(pe):
            pe.wait_ge(loaded_c, LOADS_C * 16)
            wv_wo(pe, c_m, c_m_ready, 0)
            pe.wait_ge(c_m_ready, H // 4)

            def projections(n):
                pe.wait_ge(c_xn_ready, n + 1)
                for t in range(TPS):
                    last = nc.tensor.transpose(bank[7][:, t * P:(t + 1) * P], c_xn[:, t, :], ident[:, :])
                last.then_inc(c_xtp, 1)
                pe.wait_ge(c_xt_ready, n + 1)
                for g in range(8):
                    if 2 <= g < 6:
                        pe.wait_ge(c_q_ready, 4 * n + g - 1)
                    elif g >= 6:
                        pe.wait_ge(c_k_ready, 4 * n + g - 5)
                    for a in range(2):
                        w = wqk_c[:, (2 * g + a) * P:(2 * g + a + 1) * P]
                        last = nc.tensor.matmul(bank[5 + (g + 1) % 2][:, a * T:(a + 1) * T], w, c_xt, start=True, stop=True)
                    last.then_inc(c_proj, 1)

            def sum_heads():
                for h in range(H):
                    nc.tensor.matmul(bank[7][:, 0:C], c_yt[:, h, :], m_vo[:, head_slot(h), :], start=(h == 0), stop=False)
                nc.tensor.matmul(bank[7][:, 0:C], ones_row[:, :], bo[:, :], start=False, stop=True).then_inc(c_acc, 1)

            projections(0)
            with pe.Fori(0, SEQS) as n:
                pe.wait_ge(c_k_ready, 4 * n + 4)
                pe.wait_ge(c_q_ready, 4 * n + 4)
                pe.wait_ge(c_xv_ready, n + 1)
                for t in range(TURNS + 5):
                    if t < TURNS:
                        j, a = t // PAIRS, t % PAIRS
                        if t >= 3:
                            pe.wait_ge(c_exp, 2 * (TURNS * n + t - 3) + 2)
                        nc.tensor.matmul(bank[t % 3][:, :], c_q[:, a, j * P:(j + 1) * P],
                                         c_k[:, a, :, :].rearrange("p h k -> p (h k)"), start=True, stop=True).then_inc(c_s, 1)
                    if t == TURNS:
                        pe.wait_ge(c_x_done, TPS * n + 2)
                        pe.wait_ge(c_yt_ready, GROUPS * n + 6)
                        projections(n + 1)
                    if 2 <= t < TURNS + 2:
                        u = t - 2
                        pe.wait_ge(c_prob, TURNS * n + u + 1)
                        if u >= 2:
                            pe.wait_ge(c_pt_ready, TURNS * n + u - 1)
                        for hd in range(2):
                            for k in range(TPS):
                                last = nc.tensor.transpose(bank[3 + u % 2][:, (hd * TPS + k) * P:(hd * TPS + k + 1) * P],
                                                           c_e[:, u % 3, hd, k * P:(k + 1) * P], ident[:, :])
                        last.then_inc(c_ptp, 1)
                    if t in (12, TURNS + 4):
                        j = 0 if t == 12 else 1
                        pe.wait_ge(c_yt_ready, GROUPS * n + 4 * (j + 1))
                        pe.wait_ge(c_x_done, TPS * n + j + 1)
                        sum_heads()
                    if t >= 4 and t % 2 == 0 and (t - 4) // 2 < GROUPS:
                        g = (t - 4) // 2
                        pe.wait_ge(c_pt_ready, TURNS * n + 2 * g + 2)
                        if g == 6:
                            pe.wait_ge(c_k_ready, 4 * n + 8)
                        elif g >= 1:
                            pe.wait_ge(c_yt_ready, GROUPS * n + g)
                        for k in range(TPS):
                            last = nc.tensor.matmul(bank[5][:, :], c_xv[:, k, :],
                                                    c_pt[:, g % 2, k, :, :].rearrange("p h q -> p (h q)"),
                                                    start=(k == 0), stop=(k == TPS - 1))
                        last.then_inc(c_py, 1)

        ld = Local()
        XT0 = 3 * WIN
        LAST = LAYERS * SEQS - 1
        d_xs = ld(TPS, C)
        d_xt = ld(XT0 + T)
        d_raw = [ld(2 * H, DH) for _ in range(TPS)]
        d_rot = [ld(2 * H, DH) for _ in range(TPS)]
        d_sq, d_t2 = ld(2 * H, DH), ld(2 * H, DH)
        d_ss, d_y, d_w = ld(2 * H), ld(2 * H), ld(2 * H)
        d_q = ld(PAIRS, T)
        d_k = ld(PAIRS, 2, WIN + T)
        d_e = [ld(H, 2 * WIN) for _ in range(TPS)]
        d_mx, d_sum, d_inv = ld(H), ld(H), ld(H)
        d_pt = ld(PAIRS, P)
        d_xw = [ld(NW, C) for _ in range(2)]
        d_yt = ld(H, P)
        d_x2 = ld(TPS, C)
        d_xf, d_xc, d_v, d_r, d_wf, d_xn = ld(T), ld(T), ld(T), ld(T), ld(T), ld(T)
        d_gl = ld(2, T)
        stats = Local()
        stats.at = ld.at
        d_h = ld(len(FBLK), T)
        d_st, d_mv = stats(NT, 6), stats(NT, 2)
        d_var, d_rstd, d_wn = stats(NT), stats(NT), stats(NT)
        NF = len(FBLK)
        SLOTS, SLOTS0 = 16, 12
        KEY_SLOTS = (10, 11, 14, 15)
        KEYS = len(KEY_SLOTS)
        (s_xs, s_split, s_ss, s_y, s_norm, s_t1, s_rope, s_tab, s_wsplit, s_proj, s_raw, s_sq, s_tp, s_tev, s_kev,
         s_s, s_sub, s_exp, s_prob, s_py, s_yev, s_acc, s_x2, s_mean, s_xsq, s_varp, s_var, s_ln, s_y2, s_xn, s_up, s_gl, s_h,
         s_ffo, s_x_done, s_m, s_m_ready, d_zero, d_chain, d_pool_chain, d_act_chain,
         kept, d_stats, loaded_qk, loaded_sc, loaded_vo, loaded_ff) = (
            sem("d_" + s) for s in (
                "xs split ss rsq norm t1 rope tab wsplit proj raw sq tp tev kev s sub exp prob py yev acc x2 mean xsq varp "
                "var ln rsq2 xn up gl h ffo x_done m m_ready zero chain pool_chain act_chain "
                "kept stats loaded_qk loaded_sc loaded_vo loaded_ff").split())
        LOADS_FF = 5
        back = [sem(f"d_back{g}") for g in range(4)]
        KEEP = NT // len(back)
        x_kept = Local()(NT, C)
        ZEROS = 7

        def at_least(eng, s, count):
            if not (isinstance(count, int) and count < 1):
                eng.wait_ge(s, count)

        def slot_of(n, s):
            return SLOTS0 + SLOTS * n + s

        def read(eng, n, s):
            if s in KEY_SLOTS:
                eng.wait_ge(s_kev, KEYS * (n + 1) + KEY_SLOTS.index(s) + 1)
            else:
                done = s - sum(k < s for k in KEY_SLOTS)
                eng.wait_ge(s_tev, (SLOTS - KEYS) * n + SLOTS0 - KEYS + done + 1)

        PT, X2, WINDOWS, XT, QK = (0, 3), 2, 5, 7, (8, 12)

        def x2_slot(n):
            return 0 if isinstance(n, int) else X2

        def slot_xt(f):
            return slot_of(f - 2, XT) if not (isinstance(f, int) and f == 0) else 0

        def slot_bank(s):
            return bank[4 + s % 2]

        def layer_of(f):
            return f >> 4

        def sequence(n):
            return n & (SEQS - 1)

        def before_first(n):
            return (LAST - n) // LAST

        def front_tokens(dve, f):
            at_least(dve, s_tp, slot_xt(f - 1) + 1 if not (isinstance(f, int) and f == 0) else 0)
            if not isinstance(f, int):
                dve.wait_ge(s_x_done, f - 1)
            nc.vector.tensor_copy(d_xs, x_all[:, bass.ds(sequence(f) * TPS, TPS), :]).then_inc(s_xs, 1)

        def front_split(dve, f, link):
            if isinstance(f, int) and f == 0:
                dve.wait_ge(s_tev, 1)
            else:
                read(dve, f - 2, XT)
            at_least(dve, s_proj, 8 * f)
            link(nc.vector.tensor_copy(x_split[:, 0, :], d_xt[:, XT0:]))
            nc.vector.tensor_tensor(x_split[:, 1, :], d_xt[:, XT0:], x_split[:, 0, :].bitcast(F32), ALU.subtract)\
                .then_inc(s_split, 1)

        def front_sums(dve, f, j, link, halves=(0, 1)):
            dve.wait_ge(s_sq, TPS * f + j + 1)
            for m in halves:
                last = nc.vector.tensor_reduce(out=d_ss[:, m * H:(m + 1) * H], in_=d_sq[:, m * H:(m + 1) * H, :], op=ALU.add, axis=AXX)
            if 1 not in halves:
                return
            link(last)
            nc.vector.tensor_scalar(d_ss, d_ss, 1e-24, None, ALU.max).then_inc(s_ss, 1)

        def front_norm(dve, f, j, link):
            dve.wait_ge(s_y, TPS * f + j + 1)
            rsqrt_step(link, d_ss, d_y, d_w)
            nc.vector.tensor_tensor(d_raw[j], d_raw[j], d_y.unsqueeze(2).to_broadcast([P, 2 * H, DH]), ALU.mult)\
                .then_inc(s_norm, 1)

        def front_cos(dve, f, j, halves=(0, 1)):
            par = layer_of(f) & 1
            dve.wait_ge(s_norm, TPS * f + j + 1)
            dve.wait_ge(s_tab, layer_of(f) + 1)
            if not (isinstance(f, int) and f == 0):
                dve.wait_ge(s_tp, slot_of(f - 2, QK[j]) + 4)
            for m in halves:
                tab = rope_d[:, bass.ds(par, 1), j, m, :].to_broadcast([P, H, DH])
                nc.vector.tensor_tensor(d_rot[j][:, m * H:(m + 1) * H, :], d_raw[j][:, m * H:(m + 1) * H, :], tab, ALU.mult)\
                    .then_inc(s_t1, 1)

        def front_keys(dve, f, j, slots=(0, 1)):
            at = WIN + j * P
            for q in slots:
                dve.wait_ge(s_tp, slot_of(f - 1, QK[j] + 2 + q) + 1)
                at_least(dve, s_s, 2 * TPS * f)
                src = slot_bank(QK[j] + 2 + q)[:, :].rearrange("p (a t) -> p a t", a=4)
                nc.vector.tensor_copy(d_k[0:DH, 4 * q:4 * q + 4, 0, at:at + P], src[0:DH])
                nc.vector.tensor_copy(d_k[DH:P, 4 * q:4 * q + 4, 1, at:at + P], src[DH:P]).then_inc(s_kev, 1)

        def softmax_max(dve, n, j, link):
            for b in range(2):
                dve.wait_ge(s_s, 2 * (TPS * n + j) + b + 1)
                last = nc.vector.tensor_reduce(out=d_mx[:, 8 * b:8 * b + 8],
                                               in_=bank[2 + b][:, :].rearrange("p (h k) -> p h k", h=8), op=ALU.max, axis=AXX)
            link(last)
            if not (isinstance(n, int) and n == 0):
                dve.wait_ge(s_tp, slot_of(n - 1, PT[j]) + 2)
            for b in range(2):
                last = nc.vector.tensor_tensor(d_e[j][:, 8 * b:8 * b + 8, :], bank[2 + b][:, :].rearrange("p (h k) -> p h k", h=8),
                                               d_mx[:, 8 * b:8 * b + 8].unsqueeze(2).to_broadcast([P, 8, 2 * WIN]), ALU.subtract)
            last.then_inc(s_sub, 1)

        def softmax_prob(dve, n, j, link):
            dve.wait_ge(s_exp, TPS * n + j + 1)
            link(nc.vector.tensor_reduce(out=d_sum, in_=d_e[j], op=ALU.add, axis=AXX))
            link(nc.vector.reciprocal(d_inv, d_sum))
            nc.vector.tensor_tensor(d_e[j], d_e[j], d_inv.unsqueeze(2).to_broadcast([P, H, 2 * WIN]), ALU.mult).then_inc(s_prob, 1)

        def split_weights(dve, layer_next, link):
            par = layer_next & 1
            dve.wait_ge(loaded_qk, 16 * (layer_next + 1))
            hi = wqk_split[:, bass.ds(par, 1), 0, :].rearrange("p a n -> p (a n)")
            lo = wqk_split[:, bass.ds(par, 1), 1, :].rearrange("p a n -> p (a n)")
            link(nc.vector.tensor_copy(hi, wqk_stage[:, :]))
            nc.vector.tensor_tensor(lo, wqk_stage[:, :], hi.bitcast(F32), ALU.subtract).then_inc(s_wsplit, 1)

        def residual(dve, n, j):
            dve.wait_ge(s_acc, TPS * n + j + 2)
            dve.wait_ge(s_tp, slot_of(n, X2) + 1)
            xs = x_all[:, bass.ds(sequence(n) * TPS + j, 1), :].rearrange("p a c -> p (a c)")
            nc.vector.tensor_tensor(d_x2[:, j, :], xs, bank[j][:, 0:C], ALU.add)
            nc.vector.tensor_tensor(xs, xs, bank[j][:, 0:C], ALU.add).then_inc(s_x2, 1)

        def ffn_centre(dve, n, link):
            dve.wait_ge(s_mean, n + 1)
            link(nc.vector.tensor_tensor(d_xc, d_xf, bank[2][:, 0:T], ALU.subtract))
            nc.vector.tensor_tensor(d_v, d_xc, d_xc, ALU.mult).then_inc(s_xsq, 1)

        def ffn_variance(dve, n):
            dve.wait_ge(s_varp, n + 1)
            nc.vector.tensor_scalar(d_v, bank[3][:, 0:T], EPS, None, ALU.add).then_inc(s_var, 1)

        def ffn_norm(dve, n, link, weights_loaded):
            dve.wait_ge(s_y2, n + 1)
            rsqrt_step(link, d_v, d_r, d_wf)
            link(nc.vector.tensor_tensor(d_xc, d_xc, d_r, ALU.mult))
            dve.wait_ge(loaded_ff, weights_loaded)
            nc.vector.tensor_scalar(d_xn, d_xc, cols_d[:, 0:1], cols_d[:, 1:2], ALU.mult, ALU.add).then_inc(s_xn, 1)

        def ffn_gate(dve, n, c):
            m = FBLK[c]
            dve.wait_ge(s_gl, NF * n + c + 1)
            nc.vector.scalar_tensor_tensor(d_h[0:m, c, :], bank[2 + c % 2][0:m, T:2 * T], cols_d[0:m, 2 + c:3 + c],
                                           d_gl[0:m, c % 2, :], ALU.add, ALU.mult).then_inc(s_h, 1)

        def ffn_residual(dve, n, tile):
            dve.wait_ge(s_ffo, n + 1)
            dve.wait_ge(s_x2, TPS * n + 2)
            xs = x_all[:, bass.ds(tile, TPS), :]
            nc.vector.tensor_tensor(xs, xs, bank[6][:, 0:T].rearrange("p (t c) -> p t c", t=TPS), ALU.add).then_inc(s_x_done, 1)

        def ffn_tile(n):
            return (sequence(n + SEQS - 1) + before_first(n)) * TPS

        def ffn_loaded(n):
            return ((n + SEQS - 1) >> 4) * (16 * LOADS_FF) + 1

        D_LINKS = 20

        def phase_d_vector(dve):
            for v in (d_xt, d_k, d_xw[0], d_xw[1], d_xf, d_yt, x_all[:, NT:, :]):
                nc.vector.memset(v, 0.0).then_inc(d_zero, 1)
            for j in range(TPS):
                nc.vector.memset(d_x2[:, j, :], 0.0).then_inc(s_x2, 1)
            for q, s in enumerate((s_sub, s_py, s_yev, s_yev, s_acc, s_x_done, loaded_ff)):
                nc.vector.memset(d_w[:, q:q + 1], 0.0).then_inc(s, 1)
            link = Chain(dve, d_chain, 0, 0)
            split_weights(dve, 0, link)
            for t in range(NT):
                ins = nc.vector.bn_stats(d_st[:, t, :], x_all[:, t, :])
            link(ins)
            for t in range(NT):
                ins = nc.vector.bn_aggr(d_mv[:, t, :], d_st[:, t, :])
            link(ins)
            nc.vector.tensor_scalar(d_var, d_mv[:, :, 1], EPS, None, ALU.add).then_inc(d_stats, 1)
            dve.wait_ge(d_stats, 3)
            rsqrt_step(link, d_var, d_rstd, d_wn)
            dve.wait_ge(kept, 16 * (NT // KEEP))
            for t in range(NT):
                ins = nc.vector.tensor_scalar(x_all[:, t, :], x_all[:, t, :], d_mv[:, t, 0:1], d_rstd[:, t:t + 1],
                                              ALU.subtract, ALU.mult)
            link(ins)
            front_tokens(dve, 0)
            front_split(dve, 0, link)
            dve.wait_ge(loaded_ff, 16 * LOADS_FF + 1)
            for j in range(TPS):
                front_sums(dve, 0, j, link)
                front_norm(dve, 0, j, link)
                front_cos(dve, 0, j)
            front_tokens(dve, 1)
            front_split(dve, 1, link)
            front_keys(dve, 0, 0)
            softmax_max(dve, 0, 0, link)
            front_keys(dve, 0, 1)
            softmax_prob(dve, 0, 0, link)
            before = link.n
            with dve.Fori(0, LAYERS) as layer:
                link = Chain(dve, d_chain, 1 + SEQS * D_LINKS, layer)
                link.base = link.base + before
                split_weights(dve, layer + 1, link)
                with dve.Fori(0, SEQS) as b:
                    n = layer * SEQS + b
                    link = Chain(dve, d_chain, D_LINKS, n)
                    link.base = link.base + (layer + 1 + before)
                    front_tokens(dve, n + 2)
                    softmax_max(dve, n, 1, link)
                    front_sums(dve, n + 1, 0, link, (0,))
                    softmax_prob(dve, n, 1, link)
                    front_sums(dve, n + 1, 0, link, (1,))
                    ffn_centre(dve, n, link)
                    front_norm(dve, n + 1, 0, link)
                    front_cos(dve, n + 1, 0)
                    ffn_variance(dve, n)
                    front_sums(dve, n + 1, 1, link)
                    ffn_norm(dve, n, link, ffn_loaded(n))
                    front_norm(dve, n + 1, 1, link)
                    residual(dve, n, 0)
                    front_cos(dve, n + 1, 1, (0,))
                    ffn_gate(dve, n, 0)
                    ffn_gate(dve, n, 1)
                    residual(dve, n, 1)
                    front_split(dve, n + 2, link)
                    front_cos(dve, n + 1, 1, (1,))
                    ffn_gate(dve, n, 2)
                    front_keys(dve, n + 1, 0)
                    ffn_residual(dve, n, ffn_tile(n))
                    softmax_max(dve, n + 1, 0, link)
                    front_keys(dve, n + 1, 1)
                    softmax_prob(dve, n + 1, 0, link)
                    link.end()
            link = Chain(dve, d_chain, 0, 0)
            link.base = before + LAYERS + (LAST + 1) * D_LINKS
            ffn_centre(dve, LAST + 1, link)
            ffn_variance(dve, LAST + 1)
            ffn_norm(dve, LAST + 1, link, 16 * LOADS_FF * LAYERS + 1)
            for c in range(NF):
                ffn_gate(dve, LAST + 1, c)
            ffn_residual(dve, LAST + 1, (SEQS - 1) * TPS)
            dve.wait_ge(s_x_done, LAST + 3)

        def add_kept(dve):
            for g in range(NT // KEEP):
                dve.wait_ge(back[g], 16)
                s = slice(g * KEEP, (g + 1) * KEEP)
                nc.vector.tensor_tensor(x_all[:, s, :], x_all[:, s, :], x_kept[:, s, :], ALU.add).then_inc(s_x_done, 1)

        def phase_d_scalar(act):
            def front_xt(f, s):
                act.wait_ge(s_tp, slot_xt(f) + 1)
                at_least(act, s_split, f)
                src = slot_bank(s)
                nc.scalar.activation(d_xt[0:C // 2, XT0:], src[0:C // 2, 0:T], ACT.Copy)
                nc.scalar.activation(d_xt[C // 2:C, XT0 + 1:], src[C // 2:C, 0:T - 1], ACT.Copy).then_inc(s_tev, 1)

            def front_raw(f, j, chunks):
                i = TPS * f + j
                for c in chunks:
                    act.wait_ge(s_proj, 4 * i + c + 1)
                    if c == 0:
                        at_least(act, s_rope, i - 1)
                    nc.scalar.activation(d_raw[j][:, 8 * c:8 * c + 8, :], bank[c % 2][:, :].rearrange("p (h d) -> p h d", h=8),
                                         ACT.Copy).then_inc(s_raw, 1)

            def front_sq(f, j):
                i = TPS * f + j
                act.wait_ge(s_raw, 4 * i + 4)
                at_least(act, s_ss, i)
                nc.scalar.activation(d_sq, d_raw[j], ACT.Square).then_inc(s_sq, 1)

            def front_rsqrt(f, j):
                i = TPS * f + j
                act.wait_ge(s_ss, i + 1)
                nc.scalar.activation(d_y, d_ss, ACT.Ln).then_inc(d_act_chain, 1)
                act.wait_ge(d_act_chain, i + 1)
                nc.scalar.activation(d_y, d_y, ACT.Exp, scale=-0.5).then_inc(s_y, 1)

            def front_queries(f, j):
                at_least(act, s_s, 2 * TPS * f)
                for q in range(2):
                    act.wait_ge(s_tp, slot_of(f - 1, QK[j] + q) + 1)
                    nc.scalar.activation(d_q[:, 4 * q:4 * q + 4, j * P:(j + 1) * P],
                                         slot_bank(QK[j] + q)[:, :].rearrange("p (a t) -> p a t", a=4), ACT.Copy).then_inc(s_tev, 1)

            def softmax_exp(n, j):
                act.wait_ge(s_sub, TPS * n + j + 2)
                nc.scalar.activation(d_e[j], d_e[j], ACT.Exp, scale=8.0).then_inc(s_exp, 1)

            def window_tokens(n):
                act.wait_ge(s_py, NW * n + 1)
                for s, hd, first, lo, hi in ((0, 0, 2, 0, 2), (0, 1, 0, 0, 4), (1, 0, 0, 2, 6), (1, 1, 0, 4, 8), (2, 0, 2, 6, 8)):
                    if hd == 0:
                        act.wait_ge(s_tp, slot_of(n - 1, WINDOWS + s) + 1)
                    rows = slice(hd * DH, (hd + 1) * DH)
                    last = nc.scalar.activation(
                        d_xw[hd][rows, lo:hi, :],
                        slot_bank(WINDOWS + s)[rows, first * P:(first + hi - lo) * P].rearrange("p (w c) -> p w c", c=P), ACT.Copy)
                    if hd == 1:
                        last.then_inc(s_tev, 1)

            def probabilities(n, j):
                for q in range(2):
                    act.wait_ge(s_tp, slot_of(n, PT[j] + q) + 1)
                    act.wait_ge(s_py, NW * n + WPT * j + 1)
                    nc.scalar.activation(d_pt[:, 4 * q:4 * q + 4, :],
                                         slot_bank(PT[j] + q)[:, :].rearrange("p (a q) -> p a q", a=4), ACT.Copy).then_inc(s_tev, 1)

            def weighted_tokens(n, j, windows):
                act.wait_ge(s_acc, TPS * n + j + 1)
                for w in windows:
                    act.wait_ge(s_py, NW * n + WPT * j + w + 2)
                    nc.scalar.activation(d_yt[:, :, w * WIN:(w + 1) * WIN],
                                         bank[6 + w % 2][:, :].rearrange("p (h q) -> p h q", h=H), ACT.Copy).then_inc(s_yev, 1)

            def ffn_tokens(n):
                act.wait_ge(s_tp, slot_of(n, x2_slot(n)) + 1)
                src = slot_bank(X2)
                nc.scalar.activation(d_xf[0:C // 2, :], src[0:C // 2, 0:T], ACT.Copy)
                nc.scalar.activation(d_xf[C // 2:C, 1:], src[C // 2:C, 0:T - 1], ACT.Copy).then_inc(s_tev, 1)

            def ffn_rsqrt(n):
                act.wait_ge(s_var, n + 1)
                nc.scalar.activation(d_r, d_v, ACT.Ln).then_inc(s_ln, 1)
                act.wait_ge(s_ln, n + 1)
                nc.scalar.activation(d_r, d_r, ACT.Exp, scale=-0.5).then_inc(s_y2, 1)

            def ffn_gelu(n, c):
                m = FBLK[c]
                act.wait_ge(s_up, NF * n + c + 1)
                if c >= 2:
                    act.wait_ge(s_h, NF * n + c - 1)
                nc.scalar.activation(d_gl[0:m, c % 2, :], bank[2 + c % 2][0:m, 0:T], ACT.Gelu,
                                     bias=cols_d[0:m, 2 + NF + c:3 + NF + c]).then_inc(s_gl, 1)

            act.wait_ge(d_zero, ZEROS)
            act.wait_ge(d_stats, 1)
            nc.scalar.activation(d_rstd, d_var, ACT.Ln).then_inc(d_stats, 1)
            act.wait_ge(d_stats, 2)
            nc.scalar.activation(d_rstd, d_rstd, ACT.Exp, scale=-0.5).then_inc(d_stats, 1)
            front_xt(0, 0)
            for j in range(TPS):
                front_raw(0, j, range(4))
                front_sq(0, j)
                front_rsqrt(0, j)
            window_tokens(0)
            front_xt(1, XT)
            front_queries(0, 0)
            front_raw(1, 0, range(2))
            front_queries(0, 1)
            softmax_exp(0, 0)
            front_raw(1, 0, range(2, 4))
            front_sq(1, 0)
            front_raw(1, 1, range(2))
            with act.Fori(0, LAYERS) as layer:
                for g in range(4):
                    act.wait_ge(s_m, 4 * layer + g + 1)
                    nc.scalar.activation(wv_wo_slots(g), bank[6 + g % 2][:, :].rearrange("p (h c) -> p h c", h=4),
                                         ACT.Copy).then_inc(s_m_ready, 1)
                with act.Fori(0, SEQS) as b:
                    n = layer * SEQS + b
                    probabilities(n, 0)
                    softmax_exp(n, 1)
                    weighted_tokens(n, 0, (0, 1))
                    ffn_tokens(n)
                    front_raw(n + 1, 1, range(2, 4))
                    weighted_tokens(n, 0, (2, 3))
                    front_rsqrt(n + 1, 0)
                    front_sq(n + 1, 1)
                    probabilities(n, 1)
                    weighted_tokens(n, 1, (0, 1))
                    ffn_rsqrt(n)
                    weighted_tokens(n, 1, (2, 3))
                    front_rsqrt(n + 1, 1)
                    nc.scalar.preload_act_table(ACT.Gelu)
                    window_tokens(n + 1)
                    front_xt(n + 2, XT)
                    ffn_gelu(n, 0)
                    ffn_gelu(n, 1)
                    front_queries(n + 1, 0)
                    ffn_gelu(n, 2)
                    nc.scalar.preload_act_table_set(EXP_SET)
                    front_raw(n + 2, 0, range(2))
                    front_queries(n + 1, 1)
                    softmax_exp(n + 1, 0)
                    front_raw(n + 2, 0, range(2, 4))
                    front_sq(n + 2, 0)
                    front_raw(n + 2, 1, range(2))
            ffn_tokens(LAST + 1)
            ffn_rsqrt(LAST + 1)
            nc.scalar.preload_act_table(ACT.Gelu)
            for c in range(NF):
                ffn_gelu(LAST + 1, c)

        def phase_d_gpsimd(pool):
            def tables(layer_next):
                par = layer_next & 1
                pool.wait_ge(loaded_sc, 16 * (layer_next + 1))
                half = DH // 2
                for m in range(2):
                    sc = qk_scale[:, m * DH:(m + 1) * DH]
                    nc.gpsimd.tensor_tensor(rope_d[:, bass.ds(par, 1), :, m, :].rearrange("p a t d -> p (a t) d"),
                                            rope[:, :, m, :], sc.unsqueeze(1).to_broadcast([P, TPS, DH]), ALU.mult)
                    for a, z in ((0, half), (half, 0)):
                        last = nc.gpsimd.tensor_tensor(
                            rope_d[:, bass.ds(par, 1), :, 2 + m, a:a + half].rearrange("p a t d -> p (a t) d"),
                            rope[:, :, 2 + m, a:a + half], sc[:, z:z + half].unsqueeze(1).to_broadcast([P, TPS, half]), ALU.mult)
                last.then_inc(s_tab, 1)

            def rotate(f, j):
                i = TPS * f + j
                par = layer_of(f) & 1
                half = DH // 2
                pool.wait_ge(s_tab, layer_of(f) + 1)
                at_least(pool, s_rope, i)
                pool.wait_ge(s_norm, i + 1)
                for m in range(2):
                    for a, z in ((0, half), (half, 0)):
                        last = nc.gpsimd.tensor_tensor(
                            d_t2[:, m * H:(m + 1) * H, a:a + half], d_raw[j][:, m * H:(m + 1) * H, z:z + half],
                            rope_d[:, bass.ds(par, 1), j, 2 + m, a:a + half].to_broadcast([P, H, half]), ALU.mult)
                last.then_inc(d_pool_chain, 1)
                pool.wait_ge(d_pool_chain, i + 1)
                pool.wait_ge(s_t1, 2 * i + 2)
                nc.gpsimd.tensor_tensor(d_rot[j], d_rot[j], d_t2, ALU.add).then_inc(s_rope, 1)

            tables(0)
            for j in range(TPS):
                rotate(0, j)
            with pool.Fori(0, LAYERS) as layer:
                tables(layer + 1)
                with pool.Fori(0, SEQS) as b:
                    n = layer * SEQS + b
                    for j in range(TPS):
                        rotate(n + 1, j)

        def phase_d_tensor(pe):
            def slot_free(n, s):
                if not (isinstance(n, int) and SLOTS0 + SLOTS * n + s < 3):
                    read(pe, n - 1 if s < 2 else n, (s - 2) % SLOTS)

            def front_xt(f, s):
                pe.wait_ge(s_xs, f + 1)
                if s:
                    slot_free(f - 2, XT)
                for t in range(TPS):
                    last = nc.tensor.transpose(slot_bank(s)[:, t * P:(t + 1) * P], d_xs[:, t, :], ident[:, :])
                if s:
                    for q in range(2):
                        at = (NW + q) * WIN
                        last = nc.tensor.transpose(slot_bank(s)[0:DH, T + q * P:T + (q + 1) * P], d_xt[:, at:at + 2 * WIN],
                                                   ident[:, :])
                last.then_inc(s_tp, 1)

            def front_project(f, j, chunks=range(4)):
                i = TPS * f + j
                par = layer_of(f) & 1
                pe.wait_ge(s_split, f + 1)
                pe.wait_ge(s_wsplit, layer_of(f) + 1)
                for c in chunks:
                    at_least(pe, s_raw, 4 * i + c - 1)
                    if j == 0 and c < 2 and not isinstance(f, int):
                        pe.wait_ge(s_x2, TPS * f + c - 1)
                    for q, (xp, wp) in enumerate(((0, 0), (1, 0), (0, 1))):
                        w = wqk_split[:, bass.ds(par, 1), wp, c * 512:(c + 1) * 512].rearrange("p a n -> p (a n)")
                        last = nc.tensor.matmul(bank[c % 2][:, :], x_split[:, xp, j * P:(j + 1) * P], w,
                                                start=(q == 0), stop=(q == 2))
                    last.then_inc(s_proj, 1)

            def front_transpose(f, j):
                pe.wait_ge(s_rope, TPS * f + j + 1)
                for q in range(4):
                    slot_free(f - 1, QK[j] + q)
                    for a in range(4):
                        h = 2 * (4 * q + a)
                        last = nc.tensor.transpose(slot_bank(QK[j] + q)[:, a * P:(a + 1) * P],
                                                   d_rot[j][:, h:h + 2, :].rearrange("p h d -> p (h d)"), ident[:, :])
                    last.then_inc(s_tp, 1)

            def scores(n, j):
                pe.wait_ge(s_sub, TPS * n + j + 1)
                read(pe, n - 1, QK[j] + 1)
                read(pe, n - 1, QK[j] + 3)
                for b in range(2):
                    nc.tensor.matmul(bank[2 + b][:, :], ident_bf[:, :], mask_bf[:, j, :, :].rearrange("p h k -> p (h k)"),
                                     start=True, stop=True)
                    for a in range(4):
                        for w in range(WPT):
                            at = j * P + w * WIN
                            last = nc.tensor.matmul(bank[2 + b][w * WIN:(w + 1) * WIN, a * P:(a + 1) * P],
                                                    d_q[:, 4 * b + a, at:at + WIN], d_k[:, 4 * b + a, :, at:at + 2 * WIN],
                                                    start=False, stop=True, skip_group_check=True, tile_position=(0, w * WIN))
                    last.then_inc(s_s, 1)

            def window_tokens(n):
                for s in range(2):
                    slot_free(n - 1, WINDOWS + s)
                    for q in range(4):
                        at = (4 * s + q) * WIN
                        last = nc.tensor.transpose(slot_bank(WINDOWS + s)[:, q * P:(q + 1) * P], d_xt[:, at:at + P], ident[:, :])
                    last.then_inc(s_tp, 1)

            def probabilities(n, j):
                pe.wait_ge(s_prob, TPS * n + j + 1)
                for q in range(2):
                    slot_free(n, PT[j] + q)
                    for a in range(4):
                        h = 2 * (4 * q + a)
                        last = nc.tensor.transpose(slot_bank(PT[j] + q)[:, a * P:(a + 1) * P],
                                                   d_e[j][:, h:h + 2, :].rearrange("p h k -> p (h k)"), ident[:, :])
                    last.then_inc(s_tp, 1)

            def weight_tokens(n, j):
                read(pe, n, PT[j] + 1)
                if j == 0:
                    pe.wait_ge(s_x_done, n + 1)
                for w in range(WPT):
                    pe.wait_ge(s_yev, NW * n + WPT * j + w + 1)
                    for hd in range(2):
                        last = nc.tensor.matmul(bank[6 + w % 2][:, hd * T:(hd + 1) * T], d_xw[hd][:, WPT * j + w, :],
                                                d_pt[:, :, w * WIN:(w + 1) * WIN], start=True, stop=True)
                    last.then_inc(s_py, 1)

            def sum_heads(n, j):
                pe.wait_ge(s_yev, NW * n + WPT * (j + 1) + 2)
                pe.wait_ge(s_raw, 8 * n + 15 + j)
                for r in range(H):
                    last = nc.tensor.matmul(bank[j][:, 0:C], d_yt[:, r, :], m_vo[:, r, :], start=(r == 0), stop=(r == H - 1))
                last.then_inc(s_acc, 1)

            def ffn_tokens(n):
                pe.wait_ge(s_x2, TPS * n + 2)
                slot_free(n, x2_slot(n))
                for t in range(TPS):
                    last = nc.tensor.transpose(slot_bank(X2)[:, t * P:(t + 1) * P], d_x2[:, t, :], ident[:, :])
                last.then_inc(s_tp, 1)

            def ffn_mean(n):
                pe.wait_ge(s_sub, TPS * n + 3 if not isinstance(n, int) else TPS * n + 2)
                read(pe, n, x2_slot(n))
                nc.tensor.matmul(bank[2][:, 0:T], mean_mat[:, :], d_xf, start=True, stop=True).then_inc(s_mean, 1)

            def ffn_var(n):
                pe.wait_ge(s_xsq, n + 1)
                nc.tensor.matmul(bank[3][:, 0:T], mean_mat[:, :], d_v, start=True, stop=True).then_inc(s_varp, 1)

            def ffn_up(n, c):
                m = FBLK[c]
                if c == 0:
                    pe.wait_ge(s_xn, n + 1)
                else:
                    at_least(pe, s_h, NF * n + c - 1 if c >= 2 else 0)
                for half, first in ((0, FF), (1, 0)):
                    last = nc.tensor.matmul(bank[2 + c % 2][0:m, half * T:(half + 1) * T],
                                            w1[:, first + c * P:first + c * P + m], d_xn, start=True, stop=True)
                last.then_inc(s_up, 1)

            def ffn_down(n):
                pe.wait_ge(s_h, NF * n + NF)
                for t in range(TPS):
                    for c, m in enumerate(FBLK):
                        nc.tensor.matmul(bank[6][:, t * C:(t + 1) * C], d_h[0:m, c, t * P:(t + 1) * P], w2[0:m, c, :],
                                         start=(c == 0), stop=False)
                    last = nc.tensor.matmul(bank[6][:, t * C:(t + 1) * C], ones_row[:, :], b2[:, :], start=False, stop=True)
                last.then_inc(s_ffo, 1)

            pe.wait_ge(d_zero, ZEROS)
            pe.wait_ge(loaded_ff, 16 * LOADS_FF + 1)
            front_xt(0, 0)
            for j in range(TPS):
                front_project(0, j)
            window_tokens(0)
            front_xt(1, XT)
            front_transpose(0, 0)
            front_project(1, 0, range(2))
            scores(0, 0)
            front_transpose(0, 1)
            front_project(1, 0, range(2, 4))
            front_project(1, 1, range(2))
            scores(0, 1)
            with pe.Fori(0, LAYERS) as layer:
                pe.wait_ge(loaded_vo, 32 * (layer + 1))
                wv_wo(pe, s_m, s_m_ready, 4 * layer, 6)
                with pe.Fori(0, SEQS) as b:
                    n = layer * SEQS + b
                    pe.wait_ge(s_m_ready, 4 * layer + 4)
                    probabilities(n, 0)
                    front_project(n + 1, 1, range(2, 4))
                    ffn_tokens(n)
                    weight_tokens(n, 0)
                    ffn_mean(n)
                    probabilities(n, 1)
                    sum_heads(n, 0)
                    ffn_var(n)
                    weight_tokens(n, 1)
                    window_tokens(n + 1)
                    sum_heads(n, 1)
                    front_xt(n + 2, XT)
                    pe.wait_ge(loaded_ff, ffn_loaded(n))
                    ffn_up(n, 0)
                    ffn_up(n, 1)
                    front_transpose(n + 1, 0)
                    ffn_up(n, 2)
                    front_project(n + 2, 0, range(2))
                    ffn_down(n)
                    scores(n + 1, 0)
                    front_transpose(n + 1, 1)
                    front_project(n + 2, 0, range(2, 4))
                    front_project(n + 2, 1, range(2))
                    scores(n + 1, 1)
            ffn_tokens(LAST + 1)
            ffn_mean(LAST + 1)
            ffn_var(LAST + 1)
            pe.wait_ge(loaded_ff, 16 * LOADS_FF * LAYERS + 1)
            for c in range(NF):
                ffn_up(LAST + 1, c)
            ffn_down(LAST + 1)

        def weights_of(name, layer):
            return dram[name][bass.ds(layer % LAYERS, 1)].rearrange("a p n -> (a p) n")

        def load_qk(sp, layer):
            at_least(sp, s_wsplit, layer)
            sp.dma_start(wqk_stage[:, :], weights_of("wqk", layer)).then_inc(loaded_qk, 16)
            at_least(sp, s_tab, layer)
            sp.dma_start(qk_scale[:, :], weights_of("qk_scale", layer).to_broadcast([P, 2 * DH])).then_inc(loaded_sc, 16)

        def load_vo(sp, layer):
            at_least(sp, s_m, 4 * layer)
            sp.dma_start(wvt[:, :, :], weights_of("wvt", layer).rearrange("(a p) c -> p a c", p=P)).then_inc(loaded_vo, 16)
            sp.dma_start(wo[:, :, :], weights_of("wo", layer).rearrange("(a p) c -> p a c", p=P)).then_inc(loaded_vo, 16)

        def load_ff(sp, layer):
            if not isinstance(layer, int):
                sp.wait_ge(s_ffo, SEQS * layer + 1)
            sp.dma_start(w1[:, :], weights_of("w1", layer)).then_inc(loaded_ff, 16)
            full = FF // P
            sp.dma_start(w2[:, 0:full, :], weights_of("w2", layer)[0:full * P, :].rearrange("(b p) c -> p b c", p=P))\
                .then_inc(loaded_ff, 16)
            sp.dma_start(w2[0:FBLK[-1], full, :], weights_of("w2", layer)[full * P:FF, :]).then_inc(loaded_ff, 16)
            sp.dma_start(cols_d[:, :], weights_of("cols_d", layer)).then_inc(loaded_ff, 16)
            sp.dma_start(b2[:, :], weights_of("b2", layer)).then_inc(loaded_ff, 16)

        block = ctx.enter_context(nc.Block())

        @block.sync
        def _(sp):
            sp.dma_start(x_all[:, 0:NT, :], dram["x"].rearrange("n p c -> p n c")).then_inc(loaded_x, 16)
            sp.dma_start(cols_a, dram["cols_a"]).then_inc(loaded_a, 16)
            sp.dma_start(ident[:, :], dram["ident"]).then_inc(loaded_const, 16)
            sp.dma_start(wa, dram["wa"]).then_inc(loaded_a, 16)
            sp.dma_start(wcv, dram["wcv"].rearrange("(b p) c -> p b c", p=P)).then_inc(loaded_a, 16)
            sp.dma_start(mask_stage, dram["mask"].rearrange("t p k -> p t k")).then_inc(loaded_const, 16)
            for k in range(4):
                sp.dma_start(rope[:, :, k, :], dram["rope"][k].rearrange("(t p) d -> p t d", p=P)).then_inc(loaded_const, 16)
            sp.dma_start(cols_b, dram["cols_b"]).then_inc(loaded_b, 16)
            sp.dma_start(wb1, dram["wb1"]).then_inc(loaded_b, 16)
            sp.dma_start(wbh, dram["wbh"].rearrange("l (b p) n -> p l b n", p=P)).then_inc(loaded_b, 16)
            sp.dma_start(wb3, dram["wb3"].rearrange("(b p) c -> p b c", p=P)).then_inc(loaded_b, 16)
            sp.dma_start(wqk_c, dram["wqk_c"]).then_inc(loaded_c, 16)
            sp.dma_start(wvt[:, :, :], dram["wvt_c"].rearrange("(a p) c -> p a c", p=P)).then_inc(loaded_c, 16)
            sp.dma_start(wo[:, :, :], dram["wo_c"].rearrange("(a p) c -> p a c", p=P)).then_inc(loaded_c, 16)
            sp.dma_start(bo[:, :], dram["bo"]).then_inc(loaded_c, 16)
            sp.wait_ge(const_ready, CONSTS)
            sp.wait_ge(loaded_c, LOADS_C * 16)
            sp.wait_ge(c_m, H // 4)
            load_qk(sp, 0)
            load_vo(sp, 0)
            load_ff(sp, 0)
            sp.wait_ge(phase_end, 4 * 3)
            for g in range(NT // KEEP):
                s = slice(g * KEEP, (g + 1) * KEEP)
                sp.dma_start(out[s].rearrange("n p c -> p n c"), x_all[:, s, :]).then_inc(kept, 16)
            load_qk(sp, 1)
            with sp.Fori(0, LAYERS) as layer:
                load_vo(sp, layer + 1)
                load_qk(sp, layer + 2)
                load_ff(sp, layer + 1)
            sp.wait_ge(loaded_x, 16)
            sp.wait_ge(loaded_qk, 16 * (LAYERS + 2))
            sp.wait_ge(loaded_sc, 16 * (LAYERS + 2))
            sp.wait_ge(loaded_vo, 32 * (LAYERS + 1))
            sp.wait_ge(loaded_ff, 16 * LOADS_FF * (LAYERS + 1) + 1)
            sp.wait_ge(phase_end, 4 * PHASES)
            sp.wait_ge(kept, 16 * (NT // KEEP))
            for g in range(NT // KEEP):
                s = slice(g * KEEP, (g + 1) * KEEP)
                sp.dma_start(x_kept[:, s, :], out[s].rearrange("n p c -> p n c")).then_inc(back[g], 16)
            for g in range(NT // KEEP):
                s = slice(g * KEEP, (g + 1) * KEEP)
                sp.wait_ge(s_x_done, LAST + 4 + g)
                sp.dma_start(out[s].rearrange("n p c -> p n c"), x_all[:, s, :]).then_inc(stored, 16)
            sp.wait_ge(stored, 16 * (NT // KEEP))
            sp.wait_ge(loaded_a, LOADS_A * 16)
            sp.wait_ge(loaded_b, LOADS_B * 16)
            sp.wait_ge(loaded_c, LOADS_C * 16)

        @block.vector
        def _(dve):
            dve.wait_ge(loaded_const, LOADS_CONST * 16)
            nc.vector.tensor_copy(ident_bf[:, :], ident[:, :]).then_inc(const_ready, 1)
            for t in range(TPS):
                nc.vector.tensor_copy(mask_bf[:, t, :, :], mask_stage[:, t, :].unsqueeze(1).to_broadcast([P, 8, 2 * WIN]))\
                    .then_inc(const_ready, 1)
            nc.vector.memset(ones_row[:, :], 1.0).then_inc(const_ready, 1)
            nc.vector.memset(mean_mat[:, :], 1.0 / C).then_inc(const_ready, 1)
            dve.wait_ge(loaded_x, 16)
            phase_a_vector_start(dve)
            with dve.Fori(0, SA) as step:
                phase_a_vector_steps(dve, step)
            end_phase(dve, 1)
            nc.vector.memset(b_w[:, :NT // 2], 0.0).then_inc(b_x_done, 1)
            nc.vector.memset(b_w[:, NT // 2:], 0.0).then_inc(b_down, 1)
            phase_b_vector(dve)
            end_phase(dve, 2)
            phase_c_vector(dve)
            end_phase(dve, 3)
            phase_d_vector(dve)
            end_phase(dve, 4)
            add_kept(dve)

        @block.scalar
        def _(act):
            nc.scalar.preload_act_table_set(EXP_SET)
            act.wait_ge(const_ready, CONSTS)
            act.wait_ge(loaded_a, LOADS_A * 16)
            with act.Fori(0, SA) as step:
                phase_a_scalar_steps(act, step)
            end_phase(act, 1)
            phase_b_scalar(act)
            end_phase(act, 2)
            nc.scalar.preload_act_table_set(EXP_SET)
            phase_c_scalar(act)
            end_phase(act, 3)
            nc.scalar.preload_act_table_set(EXP_SET)
            phase_d_scalar(act)
            end_phase(act, 4)

        @block.gpsimd
        def _(pool):
            with pool.Fori(0, SA) as step:
                phase_a_gpsimd_steps(pool, step)
            end_phase(pool, 1)
            end_phase(pool, 2)
            end_phase(pool, 3)
            phase_d_gpsimd(pool)
            end_phase(pool, 4)

        @block.tensor
        def _(pe):
            pe.wait_ge(const_ready, CONSTS)
            pe.wait_ge(loaded_const, LOADS_CONST * 16)
            pe.wait_ge(loaded_a, LOADS_A * 16)
            with pe.Fori(0, SA) as step:
                phase_a_tensor_steps(pe, step)
            end_phase(pe, 1)
            phase_b_tensor(pe)
            end_phase(pe, 2)
            phase_c_tensor(pe)
            end_phase(pe, 3)
            phase_d_tensor(pe)
            end_phase(pe, 4)


def rope_tables():
    import numpy as np

    half = np.arange(0, DH, 2, dtype=np.float32)
    inv_freq = (np.float32(1.0) / np.float32(10000.0) ** (half / np.float32(DH))).astype(np.float32)
    t = np.arange(T, dtype=np.float32)
    freqs = (t[:, None] * inv_freq[None, :]).astype(np.float32)
    freqs = np.concatenate([freqs, freqs], -1)
    base = ((half + np.float32(0.4 * DH)) / np.float32(1.4 * DH)).astype(np.float32)
    power = ((t - T // 2) / np.float32(WIN // 2)).astype(np.float32)
    scale = (base[None, :] ** power[:, None]).astype(np.float32)
    scale = np.concatenate([scale, scale], -1)
    sign = np.concatenate([-np.ones(DH // 2), np.ones(DH // 2)]).astype(np.float32)
    cos, sin = np.cos(freqs), np.sin(freqs) * sign
    inv = np.float32(1.0) / scale
    return np.stack([cos * scale, cos * inv, sin * scale, sin * inv]).astype(np.float32)


def window_masks():
    import numpy as np

    out = np.zeros((TPS, P, 2 * WIN), np.float32)
    r, k = np.arange(P) % WIN, np.arange(2 * WIN)
    banned = (k[None, :] - WIN > r[:, None]) | (r[:, None] > k[None, :])
    out[:] = np.where(banned, np.float32(MASKED), np.float32(0.0))
    out[0, :WIN, :WIN] = np.float32(MASKED)
    return out


def laid_out(inp):
    import numpy as np

    a = {k: np.asarray(v) for k, v in inp.items()}
    f = np.float32

    def block_cols(v):
        n = -(-v.shape[-1] // P)
        z = np.zeros(v.shape[:-1] + (n * P,), f)
        z[..., : v.shape[-1]] = v
        return np.swapaxes(z.reshape(v.shape[:-1] + (n, P)), -1, -2)

    d = {}
    d["x"] = a["L0_attn_x"].reshape(NT, P, C)
    d["ident"] = np.eye(P, dtype=f)
    d["mask"] = window_masks()
    d["rope"] = rope_tables()
    d["wa"] = np.concatenate([a["L0_attn_" + n].T for n in ("Wk", "Wv", "Wr", "Wcr", "Wck")], 1)
    d["wcv"] = a["L0_attn_Wcv"].T
    d["cols_a"] = np.stack([a["L0_attn_" + n].reshape(C) for n in
                            ("time_shift", "time_first", "ln1_w", "ln1_b", "ln2_w", "ln2_b")], 1)
    d["wb1"] = np.concatenate([a["L0_ffn_w1_w"].T, a["L0_ffn_w2_w"].T], 1)
    d["wbh"] = np.stack([a["L0_ffn_h1_w"].T, a["L0_ffn_h2_w"].T])
    d["wb3"] = a["L0_ffn_w3_w"].T
    d["cols_b"] = np.concatenate([block_cols(a["L0_ffn_" + n]) for n in ("w1_s", "w2_s", "h1_s", "h2_s", "w3_s")], 1)
    d["wqk_c"] = np.concatenate([a["L1_attn_Wq"], a["L1_attn_Wk"]], 1)
    d["wvt_c"] = a["L1_attn_Wv"].T
    d["wo_c"] = a["L1_attn_Wo"]
    d["bo"] = a["L1_attn_bo"].reshape(1, C)
    w = a["L1_ffn_Wqkv"]
    d["wqk"] = w[:, :, : 2 * INNER]
    d["wvt"] = np.swapaxes(w[:, :, 2 * INNER:], 1, 2)
    d["wo"] = a["L1_ffn_Wo"]
    d["qk_scale"] = np.concatenate([a["L1_ffn_q_scale"], a["L1_ffn_k_scale"]], 1).reshape(LAYERS, 1, 2 * DH)
    d["w1"] = a["L1_ffn_W1"]
    d["w2"] = a["L1_ffn_W2"]
    b1 = a["L1_ffn_b1"]
    d["cols_d"] = np.concatenate([a["L1_ffn_ln_g"][..., None], a["L1_ffn_ln_b"][..., None],
                                  block_cols(b1[:, :FF]), block_cols(b1[:, FF:])], 2)
    d["b2"] = a["L1_ffn_b2"].reshape(LAYERS, 1, C)
    return {k: np.ascontiguousarray(v) for k, v in d.items()}


def kernel(**inputs):
    import concourse.bacc as bacc
    from concourse.bass_utils import run_bass_kernel_spmd

    nc = bacc.Bacc("TRN2", target_bir_lowering=False, num_devices=1)
    arrays, dram = {}, {}
    for name, a in laid_out(inputs).items():
        arrays[f"in_{name}"] = a
        dram[name] = nc.dram_tensor(f"in_{name}", a.shape, mybir.dt.from_np(a.dtype), kind="ExternalInput").ap()
    out = nc.dram_tensor("out_x", (NT, P, C), F32, kind="ExternalOutput").ap()
    build(nc, dram, out)
    r = run_bass_kernel_spmd(nc, [arrays], core_ids=[0])
    return r.results[0]["out_x"].reshape(SEQS, T, C)
```

```python
import concourse.bass as bass
from concourse import mybir
from contextlib import ExitStack

F32 = mybir.dt.float32
F32R = mybir.dt.float32r
BF16 = mybir.dt.bfloat16
ACT = mybir.ActivationFunctionType
ALU = mybir.AluOpType
AXX = mybir.AxisListType.X

P = 128
C = 128
SEQS, T = 16, 256
NT = SEQS * T // P
TPS = T // P
H, DH = 16, 64
PAIRS = H // 2
INNER = H * DH
HID = 512
HB = HID // P
LAYERS = 6
WIN = 32
NW = T // WIN
WPT = P // WIN
FF = int(C * 4 * 2 / 3)
FBLK = [min(P, FF - c * P) for c in range(-(-FF // P))]
EPS = 1e-5
MASKED = -1.0e30
EXP_SET = "natural_log_exp_and_others"


class Chain:

    def __init__(self, eng, sem, per_step, step):
        self.eng, self.sem, self.base, self.per_step, self.n = eng, sem, step * per_step, per_step, 0

    def __call__(self, ins):
        self.n += 1
        ins.then_inc(self.sem, 1)
        self.eng.wait_ge(self.sem, self.base + self.n)

    def end(self):
        assert self.n == self.per_step, (self.n, self.per_step)
LOADS_A, LOADS_B, LOADS_C, LOADS_CONST, CONSTS = 3, 4, 5, 6, 5
PHASES = 4


def build(nc, dram, out):
    ctx = ExitStack()
    with ctx:
        def sb(name, shape, dt=F32):
            return ctx.enter_context(nc.sbuf_tensor(name, shape, dt))

        def sem(name):
            return ctx.enter_context(nc.semaphore(name))

        bank = [ctx.enter_context(nc.psum_tensor(f"bank{i}", [P, 512], F32)) for i in range(8)]

        x_all = sb("x_all", [P, NT + TPS, C])
        ident = sb("ident", [P, P])
        ident_bf = sb("ident_bf", [P, P], BF16)
        mask_bf = sb("mask_bf", [P, TPS, 8, 2 * WIN], BF16)
        ones_row = sb("ones_row", [1, P])
        mean_mat = sb("mean_mat", [P, P])
        rope = sb("rope", [P, TPS, 4, DH])
        rope_d = sb("rope_d", [P, 2, TPS, 4, DH])
        m_vo = sb("m_vo", [P, H, C])
        wvt = sb("wvt", [P, PAIRS, C])
        wo = sb("wo", [P, PAIRS, C])
        wqk_stage = sb("wqk_stage", [P, 2 * INNER])
        wqk_split = sb("wqk_split", [P, 2, 2, 2 * INNER], F32R)
        x_split = sb("x_split", [P, 2, T], F32R)
        w1 = sb("w1", [P, 2 * FF])
        w2 = sb("w2", [P, len(FBLK), C])
        cols_d = sb("cols_d", [P, 2 + 2 * len(FBLK)])
        b2 = sb("b2", [1, C])
        qk_scale = sb("qk_scale", [P, 2 * DH])

        ARENA = 30176
        arena = sb("arena", [P, ARENA])

        class Local:
            def __init__(self):
                self.at = 0

            def __call__(self, *shape):
                n = 1
                for s in shape:
                    n *= s
                v = arena[:, self.at:self.at + n]
                self.at += n
                assert self.at <= ARENA, self.at
                names = " ".join("abcd"[i] for i in range(len(shape)))
                if len(shape) > 1:
                    v = v.rearrange(f"p ({names}) -> p {names}", **{"abcd"[i]: s for i, s in enumerate(shape)})
                return v

        weights_c = Local()
        wqt_c = weights_c(PAIRS, C)
        wkt_c = weights_c(PAIRS, C)
        bo = weights_c(C)[0:1]
        weights = Local()
        weights.at = weights_c.at
        wa = weights(8 * C)
        wcv = weights(HB, C)
        cols_a = weights(6)
        wb1 = weights(2 * HID)
        wbh = weights(2, HB, HID)
        wb3 = weights(HB, C)
        cols_b = weights(4 * HB + 1)

        phase_end = sem("phase_end")

        def end_phase(eng, k):
            eng.drain().then_inc(phase_end, 1)
            eng.wait_ge(phase_end, 4 * k)

        loaded_x = sem("loaded_x")
        loaded_const = sem("loaded_const")
        loaded_a = sem("loaded_a")
        loaded_b = sem("loaded_b")
        loaded_c = sem("loaded_c")
        stored = sem("stored")
        const_ready = sem("const_ready")
        mask_stage = wqk_stage[:, 0:TPS * 2 * WIN].rearrange("p (t k) -> p t k", t=TPS)

        def rsqrt_step(link, v, y, w):
            link(nc.vector.tensor_tensor(w, y, y, ALU.mult))
            link(nc.vector.scalar_tensor_tensor(w, w, -0.5, v, ALU.mult, ALU.mult))
            link(nc.vector.scalar_tensor_tensor(y, w, 1.5, y, ALU.add, ALU.mult))

        LANES, UT = 2, 4
        UN = UT * P
        SA = NT // (UT * LANES)
        la = Local()
        la.at = weights.at

        def lanes(*shape):
            return [la(*shape) for _ in range(LANES)]

        a_st, a_mv, a_var, a_y, a_w = lanes(UT, 6), lanes(UT, 2), lanes(UT), lanes(UT), lanes(UT)
        a_x1, a_hn = lanes(UT, C), lanes(UT, C)
        a_x1t = lanes(2, T)
        a_h = lanes(2, T + 1)
        a_d, a_xxx = lanes(2, T), lanes(2, T)
        a_k, a_v, a_er = lanes(2, T), lanes(2, T), lanes(2, T)
        a_m, a_bs, a_aa = lanes(2, T + 1), lanes(2, T + 1), lanes(2, T + 1)
        a_g = [v.rearrange("p a c -> p (a c)").rearrange("p (s t) -> p s t", s=2) for v in a_x1]
        a_ek = [v.rearrange("p a c -> p (a c)").rearrange("p (s t) -> p s t", s=2) for v in a_hn]
        a_e1b, a_e2b, a_e1, a_e2 = lanes(2, T), lanes(2, T), lanes(2, T), lanes(2, T)
        a_rk = [[v.rearrange("p s t -> p (s t)") for v in (a_k[i], a_v[i], a_e1b[i], a_e2b[i])] for i in range(LANES)]
        TS, TF, G1, B1, G2, B2 = (cols_a[:, i:i + 1] for i in range(6))

        def flat(v):
            return v.rearrange("p a b -> p (a b)")

        def seqs(v):
            return v.rearrange("p (s t) -> p s t", s=2)

        bT0, bT1, bK, bV = ([bank[4 * i + j] for i in range(LANES)] for j in range(4))
        (a_var1, a_y1, a_var2, a_y2, a_hn_ready, a_tr1, a_h_ready, a_xxx_ready, a_kvr, a_kv_ready, a_ge_in,
         a_ge, a_bs_ready, a_bb, a_e_in, a_e, a_er_plus, a_den, a_xr, a_tr2, a_var3, a_y3, a_h2n, a_tr3, a_h2_ready,
         a_xxx2, a_cr, a_ck, a_relu, a_rk_ready, a_cv, a_er2, a_out, a_tr4, a_x_done) = (sem("a_" + s) for s in (
             "var1 rstd1 var2 rstd2 hn transposed1 h xxx kvr kv ge_in ge cum lncum e_in e er_plus den xr transposed2 var3 rstd3 "
             "h2n transposed3 h2 xxx2 cr ck relu relu2 cv er2 out transposed4 x_done").split())
        a_fixed = sem("a_fixed")
        a_chain = sem("a_chain")
        a_act_chain = sem("a_act_chain")
        a_pool_chain = sem("a_pool_chain")

        def phase_a_vector_start(dve):
            dve.wait_ge(loaded_a, LOADS_A * 16)
            for i in range(LANES):
                nc.vector.tensor_copy(a_h[i][:, :, 0], cols_a[:, 0:1].to_broadcast([P, 2])).then_inc(a_fixed, 1)
                nc.vector.memset(a_m[i][:, :, 0], 0.0).then_inc(a_fixed, 1)
                nc.vector.memset(a_bs[i][:, :, 0], 1.0).then_inc(a_fixed, 1)
                nc.vector.memset(a_aa[i][:, :, 0], 0.0).then_inc(a_fixed, 1)
                nc.vector.memset(a_w[i], 0.0).then_inc(a_x_done, 1)
            dve.wait_ge(a_fixed, 4 * LANES)
            dve.wait_ge(a_x_done, LANES)

        def phase_a_vector_steps(dve, step):
            link = Chain(dve, a_chain, LANES * A_LINKS, step)
            n = LANES * step + 1

            def tiles(i, t):
                return x_all[:, bass.ds((LANES * step + i) * UT + t, 1), :].rearrange("p a c -> p (a c)")

            def stats(src, i):
                for t in range(UT):
                    ins = nc.vector.bn_stats(a_st[i][:, t, :], src(t))
                link(ins)
                nc.vector.memset(a_w[i], 0.0)
                for t in range(UT):
                    ins = nc.vector.bn_aggr(a_mv[i][:, t, :], a_st[i][:, t, :])
                link(ins)

            def normalise(dst, src, i):
                rsqrt_step(link, a_var[i], a_y[i], a_w[i])
                for t in range(UT):
                    last = nc.vector.tensor_scalar(dst[:, t, :], src(t), a_mv[i][:, t, 0:1], a_y[i][:, t:t + 1],
                                                   ALU.subtract, ALU.mult)
                return last

            for i in range(LANES):
                stats(lambda t: tiles(i, t), i)
                nc.vector.tensor_scalar(a_var[i], a_mv[i][:, :, 1], EPS, None, ALU.add).then_inc(a_var1, 1)
            for i in range(LANES):
                dve.wait_ge(a_y1, n + i)
                link(normalise(a_x1[i], lambda t: tiles(i, t), i))
                stats(lambda t: a_x1[i][:, t, :], i)
                nc.vector.tensor_scalar(a_var[i], a_mv[i][:, :, 1], EPS, None, ALU.add).then_inc(a_var2, 1)
            for i in range(LANES):
                dve.wait_ge(a_y2, n + i)
                normalise(a_hn[i], lambda t: a_x1[i][:, t, :], i).then_inc(a_hn_ready, 1)
            for i in range(LANES):
                dve.wait_ge(a_h_ready, n + i)
                link(nc.vector.tensor_tensor(a_d[i], a_h[i][:, :, 1:], a_h[i][:, :, :T], ALU.subtract))
                nc.vector.scalar_tensor_tensor(a_xxx[i], a_d[i], TS, a_h[i][:, :, 1:], ALU.mult, ALU.add)\
                    .then_inc(a_xxx_ready, 1)
            for i in range(LANES):
                dve.wait_ge(a_kv_ready, n + i)
                for s in range(2):
                    link(nc.vector.tensor_tensor_scan(a_m[i][:, s, 1:], a_k[i][:, s, :], a_k[i][:, s, :], 0.0,
                                                      ALU.max, ALU.max))
                nc.vector.tensor_tensor(a_g[i], a_m[i][:, :, :T], a_m[i][:, :, 1:], ALU.subtract).then_inc(a_ge_in, 1)
                nc.vector.tensor_tensor(a_ek[i], a_k[i], a_m[i][:, :, 1:], ALU.subtract).then_inc(a_ge_in, 1)
            for i in range(LANES):
                dve.wait_ge(a_ge, n + i)
                for s in range(2):
                    nc.vector.tensor_tensor_scan(a_bs[i][:, s, 1:], a_g[i][:, s, :], a_ek[i][:, s, :], 1.0,
                                                 ALU.mult, ALU.add).then_inc(a_bs_ready, 1)
            for i in range(LANES):
                dve.wait_ge(a_bb, n + i)
                link(nc.vector.tensor_tensor(a_d[i], a_d[i], a_m[i][:, :, :T], ALU.add))
                link(nc.vector.tensor_tensor(a_d[i], a_d[i], a_k[i], ALU.subtract))
                nc.vector.tensor_scalar(a_e1b[i], a_d[i], 0.0, None, ALU.min).then_inc(a_e_in, 1)
                nc.vector.tensor_scalar(a_e2b[i], a_d[i], 0.0, None, ALU.max).then_inc(a_e_in, 1)
                nc.vector.tensor_scalar(a_e1[i], a_d[i], TF, 0.0, ALU.subtract, ALU.min).then_inc(a_e_in, 1)
                nc.vector.tensor_scalar(a_e2[i], a_d[i], TF, 0.0, ALU.subtract, ALU.max).then_inc(a_e_in, 1)
            for i in range(LANES):
                dve.wait_ge(a_e, n + i)
                link(nc.vector.tensor_tensor(a_e2b[i], a_e2b[i], a_v[i], ALU.mult))
                for s in range(2):
                    link(nc.vector.tensor_tensor_scan(a_aa[i][:, s, 1:], a_e1b[i][:, s, :], a_e2b[i][:, s, :], 0.0,
                                                      ALU.mult, ALU.add))
                dve.wait_ge(a_den, n + i)
                link(nc.vector.tensor_tensor(a_d[i], a_e1[i], a_aa[i][:, :, :T], ALU.mult))
                link(nc.vector.tensor_tensor(a_d[i], a_d[i], a_e2[i], ALU.add))
                link(nc.vector.reciprocal(a_er[i], a_er[i]))
                link(nc.vector.tensor_tensor(a_d[i], a_d[i], a_er[i], ALU.mult))
                nc.vector.tensor_tensor(a_x1t[i], a_d[i], a_x1t[i], ALU.add).then_inc(a_xr, 1)
            for i in range(LANES):
                dve.wait_ge(a_tr2, n + i)
                stats(lambda t: bT1[i][:, t * C:(t + 1) * C], i)
                nc.vector.tensor_scalar(a_var[i], a_mv[i][:, :, 1], EPS, None, ALU.add).then_inc(a_var3, 1)
            for i in range(LANES):
                dve.wait_ge(a_y3, n + i)
                normalise(a_hn[i], lambda t: bT1[i][:, t * C:(t + 1) * C], i).then_inc(a_h2n, 1)
            for i in range(LANES):
                dve.wait_ge(a_h2_ready, n + i)
                link(nc.vector.tensor_tensor(a_d[i], a_h[i][:, :, :T], a_h[i][:, :, 1:], ALU.subtract))
                link(nc.vector.scalar_tensor_tensor(a_xxx[i], a_d[i], TS, a_h[i][:, :, 1:], ALU.mult, ALU.add))
                nc.vector.tensor_copy(a_h[i][:, :, 0], cols_a[:, 0:1].to_broadcast([P, 2])).then_inc(a_xxx2, 1)
            for i in range(LANES):
                dve.wait_ge(a_er2, n + i)
                link(nc.vector.reciprocal(a_er[i], a_er[i]))
                dve.wait_ge(a_cv, n + i)
                link(nc.vector.tensor_tensor(flat(a_d[i]), flat(a_er[i]), bK[i][:, :], ALU.mult))
                nc.vector.tensor_tensor(a_x1t[i], a_x1t[i], a_d[i], ALU.add).then_inc(a_out, 1)
            for i in range(LANES):
                dve.wait_ge(a_tr4, n + i)
                xs = x_all[:, bass.ds((LANES * step + i) * UT, UT), :]
                nc.vector.tensor_tensor(xs, xs, bT0[i][:, :].rearrange("p (t c) -> p t c", t=UT), ALU.add)\
                    .then_inc(a_x_done, 1)
            dve.wait_ge(a_x_done, n + 2 * LANES - 1)
            link.end()

        A_LINKS = 32

        def phase_a_scalar_steps(act, step):
            n = LANES * step + 1
            link = Chain(act, a_act_chain, 9 * LANES, step)

            def rstd(i):
                link(nc.scalar.activation(a_y[i], a_var[i], ACT.Ln))
                return nc.scalar.activation(a_y[i], a_y[i], ACT.Exp, scale=-0.5)

            for i in range(LANES):
                act.wait_ge(a_var1, n + i)
                rstd(i).then_inc(a_y1, 1)
            for i in range(LANES):
                act.wait_ge(a_var2, n + i)
                rstd(i).then_inc(a_y2, 1)
            for i in range(LANES):
                act.wait_ge(a_tr1, n + i)
                nc.scalar.activation(flat(a_x1t[i]), bT0[i][:, :], ACT.Copy)
                nc.scalar.activation(a_h[i][:, :, 1:], seqs(bT1[i][:, :]), ACT.Identity, bias=B1, scale=G1)\
                    .then_inc(a_h_ready, 1)
            for i in range(LANES):
                act.wait_ge(a_kvr, n + i)
                nc.scalar.activation(flat(a_k[i]), bK[i][:, :], ACT.Copy)
                nc.scalar.activation(flat(a_v[i]), bV[i][:, :], ACT.Copy)
                nc.scalar.activation(flat(a_er[i]), bT0[i][:, :], ACT.Exp, scale=-1.0).then_inc(a_kv_ready, 1)
            for i in range(LANES):
                act.wait_ge(a_ge_in, 2 * (n + i))
                nc.scalar.activation(a_g[i], a_g[i], ACT.Exp)
                nc.scalar.activation(a_ek[i], a_ek[i], ACT.Exp).then_inc(a_ge, 1)
                act.wait_ge(a_kv_ready, n + i)
                nc.scalar.activation(a_er[i], a_er[i], ACT.Identity, bias=1.0).then_inc(a_er_plus, 1)
            for i in range(LANES):
                act.wait_ge(a_bs_ready, 2 * (n + i))
                nc.scalar.activation(a_d[i], a_bs[i][:, :, :T], ACT.Ln).then_inc(a_bb, 1)
            for i in range(LANES):
                act.wait_ge(a_e_in, 4 * (n + i))
                nc.scalar.activation(a_e1[i], a_e1[i], ACT.Exp)
                nc.scalar.activation(a_e2[i], a_e2[i], ACT.Exp, scale=-1.0)
                nc.scalar.activation(a_e1b[i], a_e1b[i], ACT.Exp)
                nc.scalar.activation(a_e2b[i], a_e2b[i], ACT.Exp, scale=-1.0).then_inc(a_e, 1)
            for i in range(LANES):
                act.wait_ge(a_var3, n + i)
                rstd(i).then_inc(a_y3, 1)
            for i in range(LANES):
                act.wait_ge(a_tr3, n + i)
                link(nc.scalar.activation(a_h[i][:, :, 1:], seqs(bT1[i][:, :]), ACT.Identity, bias=B2, scale=G2))
                nc.scalar.activation(a_h[i][:, :, 0], a_h[i][:, :, T], ACT.Copy).then_inc(a_h2_ready, 1)
            for i in range(LANES):
                act.wait_ge(a_cr, n + i)
                link(nc.scalar.activation(flat(a_er[i]), bT0[i][:, :], ACT.Exp, scale=-1.0))
                nc.scalar.activation(a_er[i], a_er[i], ACT.Identity, bias=1.0).then_inc(a_er2, 1)
            for c in range(HB):
                for i in range(LANES):
                    act.wait_ge(a_ck, HB * LANES * step + c * LANES + i + 1)
                    src = (bV, bT1)[c % 2][i]
                    link(nc.scalar.activation(a_rk[i][c], src[:, :], ACT.Relu))
                    nc.scalar.activation(a_rk[i][c], a_rk[i][c], ACT.Square).then_inc(a_rk_ready, 1)
            link.end()

        def phase_a_gpsimd_steps(pool, step):
            n = LANES * step + 1
            link = Chain(pool, a_pool_chain, 2 * LANES, step)
            for i in range(LANES):
                pool.wait_ge(a_er_plus, n + i)
                pool.wait_ge(a_e, n + i)
                link(nc.gpsimd.tensor_tensor(a_g[i], a_e1[i], a_e2[i], ALU.add))
                link(nc.gpsimd.tensor_tensor(a_er[i], a_er[i], a_g[i], ALU.mult))
                nc.gpsimd.tensor_tensor(a_e2[i], a_e2[i], a_v[i], ALU.mult).then_inc(a_den, 1)
            link.end()

        def phase_a_tensor_steps(pe, step):
            n = LANES * step + 1

            def transposes(dst, src):
                for t in range(UT):
                    last = nc.tensor.transpose(dst[:, t * P:(t + 1) * P], src(t), ident[:, :])
                return last

            for i in range(LANES):
                pe.wait_ge(a_hn_ready, n + i)
                pe.wait_ge(a_x_done, n + i)
                transposes(bT0[i], lambda t: a_x1[i][:, t, :])
                transposes(bT1[i], lambda t: a_hn[i][:, t, :]).then_inc(a_tr1, 1)
            for i in range(LANES):
                pe.wait_ge(a_xxx_ready, n + i)
                for j, dst in enumerate((bK, bV, bT0)):
                    last = nc.tensor.matmul(dst[i][:, :], wa[:, j * C:(j + 1) * C], flat(a_xxx[i]), start=True, stop=True)
                last.then_inc(a_kvr, 1)
            for i in range(LANES):
                pe.wait_ge(a_xr, n + i)
                transposes(bT1[i], lambda t: flat(a_x1t[i])[:, t * P:(t + 1) * P]).then_inc(a_tr2, 1)
            for i in range(LANES):
                pe.wait_ge(a_h2n, n + i)
                transposes(bT1[i], lambda t: a_hn[i][:, t, :]).then_inc(a_tr3, 1)
            for i in range(LANES):
                pe.wait_ge(a_xxx2, n + i)
                nc.tensor.matmul(bT0[i][:, :], wa[:, 3 * C:4 * C], flat(a_xxx[i]), start=True, stop=True).then_inc(a_cr, 1)
            for c in range(HB):
                for i in range(LANES):
                    if c >= 2:
                        pe.wait_ge(a_rk_ready, HB * LANES * step + (c - 2) * LANES + i + 1)
                    dst = (bV, bT1)[c % 2][i]
                    nc.tensor.matmul(dst[:, :], wa[:, (4 + c) * C:(5 + c) * C], flat(a_xxx[i]), start=True, stop=True)\
                        .then_inc(a_ck, 1)
            for c in range(HB):
                for i in range(LANES):
                    pe.wait_ge(a_rk_ready, HB * LANES * step + c * LANES + i + 1)
                    last = nc.tensor.matmul(bK[i][:, :], wcv[:, c, :], a_rk[i][c], start=(c == 0), stop=(c == HB - 1))
                    if c == HB - 1:
                        last.then_inc(a_cv, 1)
            for i in range(LANES):
                pe.wait_ge(a_out, n + i)
                transposes(bT0[i], lambda t: flat(a_x1t[i])[:, t * P:(t + 1) * P]).then_inc(a_tr4, 1)

        SB_ = NT // UT
        lb = Local()
        lb.at = weights.at
        b_st, b_mv = lb(NT, 6), lb(NT, 2)
        b_var, b_y, b_w = lb(NT), lb(NT), lb(NT)
        b_xn = lb(UT, C)
        b_xt = lb(UN)
        b_sl = lb(2, UN)
        b_h = lb(HB, UN)
        b_g = lb(2, HB, UN)
        b_o = lb(UN)
        b_fixed, b_chain, b_rstd, b_xn_ready, b_xtp, b_xt_ready = (sem("b_" + s) for s in "fixed chain rstd xn xtp xt".split())
        b_up, b_silu, b_h_ready, b_hid, b_gelu, b_down, b_o_ready, b_ot, b_x_done = (
            sem("b_" + s) for s in "up silu h hid gelu down o ot x_done".split())

        def scale_b(layer, c):
            return cols_b[:, layer * HB + c:layer * HB + c + 1]

        def normalise_b(u):
            for t in range(UT):
                last = nc.vector.tensor_scalar(
                    b_xn[:, t, :], x_all[:, bass.ds(u * UT + t, 1), :].rearrange("p a c -> p (a c)"),
                    b_mv[:, bass.ds(u * UT + t, 1), 0], b_y[:, bass.ds(u * UT + t, 1)], ALU.subtract, ALU.mult)
            last.then_inc(b_xn_ready, 1)

        def phase_b_vector(dve):
            link = Chain(dve, b_chain, 5, 0)
            for t in range(NT):
                ins = nc.vector.bn_stats(b_st[:, t, :], x_all[:, t, :])
            link(ins)
            for t in range(NT):
                ins = nc.vector.bn_aggr(b_mv[:, t, :], b_st[:, t, :])
            link(ins)
            nc.vector.tensor_scalar(b_var, b_mv[:, :, 1], EPS, None, ALU.add).then_inc(b_fixed, 1)
            dve.wait_ge(b_rstd, 1)
            rsqrt_step(link, b_var, b_y, b_w)
            link.end()
            dve.wait_ge(loaded_b, LOADS_B * 16)
            normalise_b(0)
            with dve.Fori(0, SB_) as u:
                for c in range(HB):
                    dve.wait_ge(b_silu, HB * u + c + 1)
                    if c == 0:
                        dve.wait_ge(b_down, u + 1)
                    nc.vector.scalar_tensor_tensor(b_h[:, c, :], bank[2 + c % 2][:, :], scale_b(1, c), b_sl[:, c % 2, :],
                                                   ALU.mult, ALU.mult).then_inc(b_h_ready, 1)
                dve.wait_ge(b_xtp, u + 1)
                normalise_b((u + 1) & (SB_ - 1))
                dve.wait_ge(b_ot, u + 1)
                xs = x_all[:, bass.ds(u * UT, UT), :]
                nc.vector.tensor_tensor(xs, xs, bank[5][:, :].rearrange("p (t c) -> p t c", t=UT), ALU.add)\
                    .then_inc(b_x_done, 1)
            dve.wait_ge(b_x_done, SB_ + 1)

        def phase_b_scalar(act):
            act.wait_ge(b_fixed, 1)
            nc.scalar.activation(b_y, b_var, ACT.Ln).then_inc(b_fixed, 1)
            act.wait_ge(b_fixed, 2)
            nc.scalar.activation(b_y, b_y, ACT.Exp, scale=-0.5).then_inc(b_rstd, 1)
            act.wait_ge(loaded_b, LOADS_B * 16)
            act.wait_ge(b_xtp, 1)
            nc.scalar.activation(b_xt, bank[6][:, :], ACT.Copy).then_inc(b_xt_ready, 1)
            with act.Fori(0, SB_) as u:
                for c in range(HB):
                    act.wait_ge(b_up, HB * u + c + 1)
                    if c >= 2:
                        act.wait_ge(b_h_ready, HB * u + c - 1)
                    nc.scalar.activation(b_sl[:, c % 2, :], bank[c % 2][:, :], ACT.Silu, scale=scale_b(0, c))\
                        .then_inc(b_silu, 1)
                for layer in range(2):
                    for c in range(HB):
                        act.wait_ge(b_hid, 2 * HB * u + HB * layer + c + 1)
                        nc.scalar.activation(b_g[:, layer, c, :], bank[(4 if layer == 0 else 0) + c][:, :], ACT.Gelu,
                                             scale=scale_b(2 + layer, c)).then_inc(b_gelu, 1)
                act.wait_ge(b_xtp, u + 2)
                nc.scalar.activation(b_xt, bank[6][:, :], ACT.Copy).then_inc(b_xt_ready, 1)
                act.wait_ge(b_down, u + 2)
                nc.scalar.activation(b_o, bank[4][:, :], ACT.Copy, scale=scale_b(4, 0)).then_inc(b_o_ready, 1)

        def phase_b_tensor(pe):
            def transpose_tokens():
                for t in range(UT):
                    last = nc.tensor.transpose(bank[6][:, t * P:(t + 1) * P], b_xn[:, t, :], ident[:, :])
                last.then_inc(b_xtp, 1)

            pe.wait_ge(loaded_b, LOADS_B * 16)
            pe.wait_ge(b_xn_ready, 1)
            transpose_tokens()
            with pe.Fori(0, SB_) as u:
                pe.wait_ge(b_xt_ready, u + 1)
                for c in range(HB):
                    if c >= 2:
                        pe.wait_ge(b_h_ready, HB * u + c - 1)
                    nc.tensor.matmul(bank[c % 2][:, :], wb1[:, c * P:(c + 1) * P], b_xt, start=True, stop=True)
                    nc.tensor.matmul(bank[2 + c % 2][:, :], wb1[:, HID + c * P:HID + (c + 1) * P], b_xt,
                                     start=True, stop=True).then_inc(b_up, 1)
                for layer in range(2):
                    if layer == 0:
                        pe.wait_ge(b_x_done, u + 1)
                    for c in range(HB):
                        for k in range(HB):
                            if c == 0 and layer == 0:
                                pe.wait_ge(b_h_ready, HB * u + k + 1)
                            if c == 0 and layer == 1:
                                pe.wait_ge(b_gelu, 2 * HB * u + k + 1)
                            src = b_h[:, k, :] if layer == 0 else b_g[:, 0, k, :]
                            last = nc.tensor.matmul(bank[(4 if layer == 0 else 0) + c][:, :],
                                                    wbh[:, layer, k, c * P:(c + 1) * P], src,
                                                    start=(k == 0), stop=(k == HB - 1))
                        last.then_inc(b_hid, 1)
                pe.wait_ge(b_xn_ready, u + 2)
                transpose_tokens()
                for k in range(HB):
                    pe.wait_ge(b_gelu, 2 * HB * u + HB + k + 1)
                    last = nc.tensor.matmul(bank[4][:, :], wb3[:, k, :], b_g[:, 1, k, :], start=(k == 0), stop=(k == HB - 1))
                last.then_inc(b_down, 1)
                pe.wait_ge(b_o_ready, u + 1)
                for t in range(UT):
                    last = nc.tensor.transpose(bank[5][:, t * P:(t + 1) * P], b_o[:, t * P:(t + 1) * P], ident[:, :])
                last.then_inc(b_ot, 1)

        TURNS = TPS * PAIRS
        HALF = TURNS // 2
        RING = 4
        lc = Local()
        lc.at = weights_c.at
        c_st, c_mv = lc(NT, 6), lc(NT, 2)
        c_var, c_y, c_w = lc(NT), lc(NT), lc(NT)
        c_xn = lc(TPS, C)
        c_xt = lc(2, T)
        c_a = lc(H, C)
        c_z = [lc(H, T) for _ in range(2)]
        c_u = [lc(TPS, H, C) for _ in range(2)]
        c_e = lc(RING, 2, T)
        c_pt = lc(2, 2 * TPS, P)
        c_nm, c_sum, c_inv = lc(RING, 2), lc(RING, 2), lc(RING, 2)
        (c_fixed, c_chain, c_rstd, c_xn_ready, c_xtp, c_xt_ready, c_unit, c_z_ready, c_u_ready, c_s, c_max,
         c_exp, c_prob, c_ptp, c_pt_ready, c_po, c_acc, c_x_done, c_m, c_m_ready, c_recip) = (
            sem("c_" + s) for s in ("fixed chain rstd xn xtp xt unit z u s max exp prob ptp pt po acc x_done m m_ready "
                                    "recip").split())
        QSCALE = float(DH) ** -0.5
        U_GROUPS = [(hg, k) for hg in (0, 2, 1, 3) for k in range(TPS)]

        def head_slot(h):
            return h % 2 * PAIRS + h // 2

        def head_products(pe, left, right, ready, done, base, first_bank=5):
            for g in range(4):
                if g >= 2:
                    pe.wait_ge(done, base + g - 1)
                d = g % 2 * DH
                for j in range(4):
                    a = 4 * (g // 2) + j
                    last = nc.tensor.matmul(bank[first_bank + g % 2][:, j * P:(j + 1) * P], left[d:d + DH, a, :],
                                            right[d:d + DH, a, :], start=True, stop=True)
                last.then_inc(ready, 1)

        def product_slots(products, g):
            first = g % 2 * PAIRS + 4 * (g // 2)
            return products[:, first:first + 4, :]

        def acc_bank(j):
            return bank[2] if j == 0 else bank[7]

        def phase_c_vector(dve):
            for q in range(2):
                nc.vector.memset(c_nm[:, q, :], 0.0).then_inc(c_pt_ready, 1)
                nc.vector.memset(c_sum[:, q, :], 0.0).then_inc(c_po, 1)
                nc.vector.memset(c_inv[:, q, :], 0.0).then_inc(c_x_done, 1)
            link = Chain(dve, c_chain, 5, 0)
            for t in range(NT):
                ins = nc.vector.bn_stats(c_st[:, t, :], x_all[:, t, :])
            link(ins)
            for t in range(NT):
                ins = nc.vector.bn_aggr(c_mv[:, t, :], c_st[:, t, :])
            link(ins)
            nc.vector.tensor_scalar(c_var, c_mv[:, :, 1], EPS, None, ALU.add).then_inc(c_fixed, 1)
            dve.wait_ge(c_rstd, 1)
            rsqrt_step(link, c_var, c_y, c_w)
            link.end()

            def normalise(m):
                if not (isinstance(m, int) and m == 0):
                    dve.wait_ge(c_xtp, m)
                tile = (m & (SEQS - 1)) * TPS
                for t in range(TPS):
                    last = nc.vector.tensor_scalar(
                        c_xn[:, t, :], x_all[:, bass.ds(tile + t, 1), :].rearrange("p a c -> p (a c)"),
                        c_mv[:, bass.ds(tile + t, 1), 0], c_y[:, bass.ds(tile + t, 1)], ALU.subtract, ALU.mult)
                last.then_inc(c_xn_ready, 1)

            def maximum(g, r):
                dve.wait_ge(c_s, g + 1)
                nc.vector.tensor_reduce(out=c_nm[:, r, :], in_=bank[r % 2][:, :].rearrange("p (h k) -> p h k", h=2),
                                        op=ALU.max, axis=AXX, negate=True).then_inc(c_max, 1)

            def probabilities(g, r):
                dve.wait_ge(c_exp, g + 1)
                nc.vector.reciprocal(c_inv[:, r, :], c_sum[:, r, :]).then_inc(c_recip, 1)
                dve.wait_ge(c_recip, g + 1)
                for hd in range(2):
                    last = nc.vector.tensor_scalar(c_e[:, r, hd, :], c_e[:, r, hd, :], c_inv[:, r, hd:hd + 1], None, ALU.mult)
                last.then_inc(c_prob, 1)

            def read_u(m, par, q):
                hg, k = U_GROUPS[q]
                dve.wait_ge(c_unit, TURNS * m + HALF + q + 1)
                nc.vector.tensor_copy(c_u[par][:, k, 4 * hg:4 * hg + 4, :],
                                      bank[5 + q % 2][:, :].rearrange("p (h c) -> p h c", h=4)).then_inc(c_u_ready, 1)

            normalise(0)
            normalise(1)
            for q in range(HALF):
                read_u(0, 0, q)
            maximum(0, 0)
            maximum(1, 1)
            probabilities(0, 0)
            with dve.Fori(0, SEQS // 2) as two:
                for s in range(2):
                    n = two * 2 + s
                    for t in range(TURNS):
                        g = n * TURNS + t
                        probabilities(g + 1, (t + 1) % RING)
                        maximum(g + 2, (t + 2) % RING)
                        if t >= HALF:
                            read_u(n + 1, 1 - s, t - HALF)
                        if t == HALF + 2:
                            normalise(n + 2)
                        if t in (HALF + 1, TURNS - 1):
                            j = 0 if t < TURNS - 1 else 1
                            dve.wait_ge(c_acc, TPS * n + j + 1)
                            xs = x_all[:, bass.ds(n * TPS + j, 1), :].rearrange("p a c -> p (a c)")
                            nc.vector.tensor_tensor(xs, xs, acc_bank(j)[:, 0:C], ALU.add).then_inc(c_x_done, 1)
            dve.wait_ge(c_x_done, TPS * SEQS + 2)

        def phase_c_scalar(act):
            for products, base, scale in ((m_vo, 0, 1.0), (c_a, 4, QSCALE)):
                for g in range(4):
                    act.wait_ge(c_m, base + g + 1)
                    nc.scalar.activation(product_slots(products, g), bank[5 + g % 2][:, :].rearrange("p (h c) -> p h c", h=4),
                                         ACT.Copy, scale=scale).then_inc(c_m_ready, 1)
            act.wait_ge(c_fixed, 1)
            nc.scalar.activation(c_y, c_var, ACT.Ln).then_inc(c_fixed, 1)
            act.wait_ge(c_fixed, 2)
            nc.scalar.activation(c_y, c_y, ACT.Exp, scale=-0.5).then_inc(c_rstd, 1)

            def read_xt(m, par):
                act.wait_ge(c_xtp, m + 1)
                nc.scalar.activation(c_xt[:, par, :], bank[2][:, 0:T], ACT.Copy).then_inc(c_xt_ready, 1)

            def read_z(m, par, a):
                act.wait_ge(c_unit, TURNS * m + a + 1)
                nc.scalar.activation(c_z[par][:, 2 * a:2 * a + 2, :], bank[5 + a % 2][:, :].rearrange("p (h t) -> p h t", h=2),
                                     ACT.Copy).then_inc(c_z_ready, 1)

            def exponentials(g, r):
                act.wait_ge(c_max, g + 1)
                for hd in range(2):
                    last = nc.scalar.activation(c_e[:, r, hd, :], bank[r % 2][:, hd * T:(hd + 1) * T], ACT.Exp,
                                                bias=c_nm[:, r, hd:hd + 1], accum_out=c_sum[:, r, hd:hd + 1])
                last.then_inc(c_exp, 1)

            read_xt(0, 0)
            read_xt(1, 1)
            for a in range(PAIRS):
                read_z(0, 0, a)
            exponentials(0, 0)
            exponentials(1, 1)
            with act.Fori(0, SEQS // 2) as two:
                for s in range(2):
                    n = two * 2 + s
                    for t in range(TURNS):
                        g = n * TURNS + t
                        act.wait_ge(c_ptp, g + 1)
                        act.wait_ge(c_po, g + 1)
                        nc.scalar.activation(c_pt[:, t % 2, :, :], bank[3 + t % 2][:, :].rearrange("p (a q) -> p a q", a=2 * TPS),
                                             ACT.Copy).then_inc(c_pt_ready, 1)
                        exponentials(g + 2, (t + 2) % RING)
                        if t < HALF:
                            read_z(n + 1, 1 - s, t)
                        if t == TURNS - 1:
                            read_xt(n + 2, s)

        def phase_c_tensor(pe):
            pe.wait_ge(loaded_c, LOADS_C * 16)
            head_products(pe, wvt, wo, c_m, c_m_ready, 0)
            pe.wait_ge(c_m_ready, 4)
            head_products(pe, wqt_c, wkt_c, c_m, c_m_ready, 4)
            pe.wait_ge(c_m_ready, 8)

            def transpose_tokens(m):
                pe.wait_ge(c_xn_ready, m + 1)
                for t in range(TPS):
                    last = nc.tensor.transpose(bank[2][:, t * P:(t + 1) * P], c_xn[:, t, :], ident[:, :])
                last.then_inc(c_xtp, 1)

            def unit(m, par, t, first):
                into = bank[5 + t % 2]
                if t < 2:
                    if not first:
                        pe.wait_ge(c_u_ready, HALF * m - 1 + t)
                elif t < HALF + 2:
                    pe.wait_ge(c_z_ready, HALF * m + t - 1)
                else:
                    pe.wait_ge(c_u_ready, HALF * m + t - HALF - 1)
                if t < HALF:
                    if t == 0:
                        pe.wait_ge(c_xt_ready, m + 1)
                    for hd in range(2):
                        last = nc.tensor.matmul(into[:, hd * T:(hd + 1) * T], c_a[:, head_slot(2 * t + hd), :], c_xt[:, par, :],
                                                start=True, stop=True)
                else:
                    hg, k = U_GROUPS[t - HALF]
                    last = nc.tensor.matmul(into[:, :], c_xt[:, par, k * P:(k + 1) * P],
                                            m_vo[:, 4 * hg:4 * hg + 4, :].rearrange("p h c -> p (h c)"), start=True, stop=True)
                last.then_inc(c_unit, 1)

            def scores(m, par, t):
                j, a = t // PAIRS, t % PAIRS
                pe.wait_ge(c_z_ready, HALF * m + a + 1)
                for hd in range(2):
                    last = nc.tensor.matmul(bank[t % 2][:, hd * T:(hd + 1) * T], c_z[par][:, 2 * a + hd, j * P:(j + 1) * P],
                                            c_xt[:, par, :], start=True, stop=True)
                last.then_inc(c_s, 1)

            transpose_tokens(0)
            pe.wait_ge(c_xt_ready, 1)
            transpose_tokens(1)
            for t in range(TURNS):
                unit(0, 0, t, True)
            scores(0, 0, 0)
            scores(0, 0, 1)
            with pe.Fori(0, SEQS // 2) as two:
                for s in range(2):
                    n = two * 2 + s
                    for t in range(TURNS):
                        g = n * TURNS + t
                        j, a = t // PAIRS, t % PAIRS
                        pe.wait_ge(c_prob, g + 1)
                        pe.wait_ge(c_pt_ready, g + 1)
                        for hd in range(2):
                            for k in range(TPS):
                                last = nc.tensor.transpose(bank[3 + t % 2][:, (hd * TPS + k) * P:(hd * TPS + k + 1) * P],
                                                           c_e[:, t % RING, hd, k * P:(k + 1) * P], ident[:, :])
                        last.then_inc(c_ptp, 1)
                        if t + 2 < TURNS:
                            scores(n, s, t + 2)
                        else:
                            scores(n + 1, 1 - s, t + 2 - TURNS)
                        unit(n + 1, 1 - s, t, False)
                        if t == 0:
                            pe.wait_ge(c_u_ready, HALF * n + HALF)
                        if a == 0:
                            pe.wait_ge(c_x_done, TPS * n + j + 1)
                        pe.wait_ge(c_pt_ready, g + 3)
                        for hd in range(2):
                            for k in range(TPS):
                                last = nc.tensor.matmul(acc_bank(j)[:, 0:C], c_pt[:, t % 2, hd * TPS + k, :],
                                                        c_u[s][:, k, head_slot(2 * a + hd), :],
                                                        start=(a == 0 and hd == 0 and k == 0), stop=False)
                        last.then_inc(c_po, 1)
                        if a == PAIRS - 1:
                            nc.tensor.matmul(acc_bank(j)[:, 0:C], ones_row[:, :], bo[:, :], start=False, stop=True).then_inc(c_acc, 1)
                        if t == TURNS - 2:
                            pe.wait_ge(c_x_done, TPS * n + 3)
                            transpose_tokens(n + 2)

        ld = Local()
        LAST = LAYERS * SEQS - 1
        QUADS = H // 4
        d_xs = ld(TPS, C)
        d_xt, d_xv = ld(T), ld(T)
        d_raw = [ld(2 * H, DH) for _ in range(TPS)]
        d_rot = [ld(2 * H, DH) for _ in range(TPS)]
        d_sq, d_t2 = ld(2 * H, DH), ld(2 * H, DH)
        d_ss, d_y, d_w = ld(2 * H), ld(2 * H), ld(2 * H)
        d_q = ld(PAIRS, T)
        d_k = ld(PAIRS, 2, WIN + T)
        d_e = [ld(2, H, WIN) for _ in range(TPS)]
        d_mx, d_sum, d_inv = ld(H), ld(H), ld(H)
        d_pt = ld(2, QUADS, P)
        d_u = ld(1 + NW, QUADS, C)
        d_x2 = ld(TPS, C)
        d_xf, d_xc, d_v, d_r = ld(T), ld(T), ld(T), ld(T)
        d_xn = d_xc
        d_gl = ld(2, T)
        d_wf = d_gl[:, 0, :]
        stats = Local()
        stats.at = ld.at
        d_h = ld(len(FBLK), T)
        d_st, d_mv = stats(NT, 6), stats(NT, 2)
        d_var, d_rstd, d_wn = stats(NT), stats(NT), stats(NT)
        NF = len(FBLK)
        SLOTS, SLOTS0 = 14, 10
        (s_xs, s_split, s_ss, s_y, s_norm, s_t1, s_rope, s_tab, s_wsplit, s_proj, s_raw, s_sq, s_tp, s_tev,
         s_s, s_sub, s_exp, s_prob, s_xv, s_u, s_uev, s_acc, s_x2, s_mean, s_xsq, s_varp, s_var, s_ln, s_y2, s_xn, s_up, s_gl, s_h,
         s_ffo, s_x_done, s_m, s_m_ready, d_zero, d_chain, d_pool_chain, d_act_chain,
         kept, d_stats, loaded_qk, loaded_sc, loaded_vo, loaded_ff) = (
            sem("d_" + s) for s in (
                "xs split ss rsq norm t1 rope tab wsplit proj raw sq tp tev s sub exp prob xv u uev acc x2 mean xsq varp "
                "var ln rsq2 xn up gl h ffo x_done m m_ready zero chain pool_chain act_chain "
                "kept stats loaded_qk loaded_sc loaded_vo loaded_ff").split())
        LOADS_FF = 5
        back = [sem(f"d_back{g}") for g in range(4)]
        KEEP = NT // len(back)
        x_kept = Local()(NT, C)
        ZEROS = 5

        def at_least(eng, s, count):
            if not (isinstance(count, int) and count < 1):
                eng.wait_ge(s, count)

        def slot_of(n, s):
            return SLOTS0 + SLOTS * n + s

        def read(eng, n, s):
            eng.wait_ge(s_tev, slot_of(n, s) + 1)

        PT, X2, XT, QK = (0, 3), 2, 5, (6, 10)

        def x2_slot(n):
            return 0 if isinstance(n, int) else X2

        def slot_xt(f):
            return slot_of(f - 2, XT) if not (isinstance(f, int) and f == 0) else 0

        def slot_bank(s):
            return bank[4 + s % 2]

        def layer_of(f):
            return f >> 4

        def sequence(n):
            return n & (SEQS - 1)

        def before_first(n):
            return (LAST - n) // LAST

        def front_tokens(dve, f):
            at_least(dve, s_tp, slot_xt(f - 1) + 1 if not (isinstance(f, int) and f == 0) else 0)
            if not isinstance(f, int):
                dve.wait_ge(s_x_done, f - 1)
            nc.vector.tensor_copy(d_xs, x_all[:, bass.ds(sequence(f) * TPS, TPS), :]).then_inc(s_xs, 1)

        def front_split(dve, f, link):
            if isinstance(f, int) and f == 0:
                dve.wait_ge(s_tev, 1)
            else:
                read(dve, f - 2, XT)
            at_least(dve, s_proj, 8 * f)
            link(nc.vector.tensor_copy(x_split[:, 0, :], d_xt))
            nc.vector.tensor_tensor(x_split[:, 1, :], d_xt, x_split[:, 0, :].bitcast(F32), ALU.subtract)\
                .then_inc(s_split, 1)

        def front_sums(dve, f, j, link, halves=(0, 1)):
            dve.wait_ge(s_sq, TPS * f + j + 1)
            for m in halves:
                last = nc.vector.tensor_reduce(out=d_ss[:, m * H:(m + 1) * H], in_=d_sq[:, m * H:(m + 1) * H, :], op=ALU.add, axis=AXX)
            if 1 not in halves:
                return
            link(last)
            nc.vector.tensor_scalar(d_ss, d_ss, 1e-24, None, ALU.max).then_inc(s_ss, 1)

        def front_norm(dve, f, j, link):
            dve.wait_ge(s_y, TPS * f + j + 1)
            rsqrt_step(link, d_ss, d_y, d_w)
            nc.vector.tensor_tensor(d_raw[j], d_raw[j], d_y.unsqueeze(2).to_broadcast([P, 2 * H, DH]), ALU.mult)\
                .then_inc(s_norm, 1)

        def front_cos(dve, f, j, halves=(0, 1)):
            par = layer_of(f) & 1
            dve.wait_ge(s_norm, TPS * f + j + 1)
            dve.wait_ge(s_tab, layer_of(f) + 1)
            if not (isinstance(f, int) and f == 0):
                dve.wait_ge(s_tp, slot_of(f - 2, QK[j]) + 4)
            for m in halves:
                tab = rope_d[:, bass.ds(par, 1), j, m, :].to_broadcast([P, H, DH])
                nc.vector.tensor_tensor(d_rot[j][:, m * H:(m + 1) * H, :], d_raw[j][:, m * H:(m + 1) * H, :], tab, ALU.mult)\
                    .then_inc(s_t1, 1)

        def softmax_max(dve, n, j, link):
            for b in range(2):
                dve.wait_ge(s_s, 2 * (TPS * n + j) + b + 1)
                last = nc.vector.tensor_reduce(out=d_mx[:, 8 * b:8 * b + 8],
                                               in_=bank[2 + b][:, :].rearrange("p (h k) -> p h k", h=8), op=ALU.max, axis=AXX)
            link(last)
            if not (isinstance(n, int) and n == 0):
                dve.wait_ge(s_tp, slot_of(n - 1, PT[j]) + 2)
            for b in range(2):
                last = nc.vector.tensor_tensor(
                    d_e[j][:, :, 8 * b:8 * b + 8, :].rearrange("p s h k -> p h s k"),
                    bank[2 + b][:, :].rearrange("p (h s k) -> p h s k", h=8, s=2),
                    d_mx[:, 8 * b:8 * b + 8].unsqueeze(2).unsqueeze(3).to_broadcast([P, 8, 2, WIN]), ALU.subtract)
            last.then_inc(s_sub, 1)

        def softmax_prob(dve, n, j, link):
            dve.wait_ge(s_exp, TPS * n + j + 1)
            link(nc.vector.tensor_reduce(out=d_sum, in_=d_e[j].rearrange("p s h k -> p h s k"), op=ALU.add, axis=mybir.AxisListType.XY))
            link(nc.vector.reciprocal(d_inv, d_sum))
            nc.vector.tensor_tensor(d_e[j], d_e[j], d_inv.unsqueeze(1).unsqueeze(3).to_broadcast([P, 2, H, WIN]), ALU.mult).then_inc(s_prob, 1)

        def split_weights(dve, layer_next, link):
            par = layer_next & 1
            dve.wait_ge(loaded_qk, 16 * (layer_next + 1))
            hi = wqk_split[:, bass.ds(par, 1), 0, :].rearrange("p a n -> p (a n)")
            lo = wqk_split[:, bass.ds(par, 1), 1, :].rearrange("p a n -> p (a n)")
            link(nc.vector.tensor_copy(hi, wqk_stage[:, :]))
            nc.vector.tensor_tensor(lo, wqk_stage[:, :], hi.bitcast(F32), ALU.subtract).then_inc(s_wsplit, 1)

        def residual(dve, n, j):
            dve.wait_ge(s_acc, TPS * n + j + 2)
            dve.wait_ge(s_tp, slot_of(n, X2) + 1)
            xs = x_all[:, bass.ds(sequence(n) * TPS + j, 1), :].rearrange("p a c -> p (a c)")
            nc.vector.tensor_tensor(d_x2[:, j, :], xs, bank[j][:, 0:C], ALU.add)
            nc.vector.tensor_tensor(xs, xs, bank[j][:, 0:C], ALU.add).then_inc(s_x2, 1)

        def ffn_centre(dve, n, link):
            dve.wait_ge(s_mean, n + 1)
            link(nc.vector.tensor_tensor(d_xc, d_xf, bank[2][:, 0:T], ALU.subtract))
            nc.vector.tensor_tensor(d_v, d_xc, d_xc, ALU.mult).then_inc(s_xsq, 1)

        def ffn_variance(dve, n):
            dve.wait_ge(s_varp, n + 1)
            nc.vector.tensor_scalar(d_v, bank[3][:, 0:T], EPS, None, ALU.add).then_inc(s_var, 1)

        def ffn_norm(dve, n, link, weights_loaded):
            dve.wait_ge(s_y2, n + 1)
            rsqrt_step(link, d_v, d_r, d_wf)
            link(nc.vector.tensor_tensor(d_xc, d_xc, d_r, ALU.mult))
            dve.wait_ge(loaded_ff, weights_loaded)
            nc.vector.tensor_scalar(d_xn, d_xc, cols_d[:, 0:1], cols_d[:, 1:2], ALU.mult, ALU.add).then_inc(s_xn, 1)

        def ffn_gate(dve, n, c):
            m = FBLK[c]
            dve.wait_ge(s_gl, NF * n + c + 1)
            nc.vector.scalar_tensor_tensor(d_h[0:m, c, :], bank[2 + c % 2][0:m, T:2 * T], cols_d[0:m, 2 + c:3 + c],
                                           d_gl[0:m, c % 2, :], ALU.add, ALU.mult).then_inc(s_h, 1)

        def ffn_residual(dve, n, tile):
            dve.wait_ge(s_ffo, n + 1)
            dve.wait_ge(s_x2, TPS * n + 2)
            xs = x_all[:, bass.ds(tile, TPS), :]
            nc.vector.tensor_tensor(xs, xs, bank[6][:, 0:T].rearrange("p (t c) -> p t c", t=TPS), ALU.add).then_inc(s_x_done, 1)

        def ffn_tile(n):
            return (sequence(n + SEQS - 1) + before_first(n)) * TPS

        def ffn_loaded(n):
            return ((n + SEQS - 1) >> 4) * (16 * LOADS_FF) + 1

        D_LINKS = 20

        def phase_d_vector(dve):
            for v in (d_xt, d_k, d_u[:, 0], d_xf, x_all[:, NT:, :]):
                nc.vector.memset(v, 0.0).then_inc(d_zero, 1)
            for j in range(TPS):
                nc.vector.memset(d_x2[:, j, :], 0.0).then_inc(s_x2, 1)
            for q, s in enumerate((s_sub, s_uev, s_uev, s_acc, s_x_done, loaded_ff)):
                nc.vector.memset(d_w[:, q:q + 1], 0.0).then_inc(s, 1)
            link = Chain(dve, d_chain, 0, 0)
            split_weights(dve, 0, link)
            for t in range(NT):
                ins = nc.vector.bn_stats(d_st[:, t, :], x_all[:, t, :])
            link(ins)
            for t in range(NT):
                ins = nc.vector.bn_aggr(d_mv[:, t, :], d_st[:, t, :])
            link(ins)
            nc.vector.tensor_scalar(d_var, d_mv[:, :, 1], EPS, None, ALU.add).then_inc(d_stats, 1)
            dve.wait_ge(d_stats, 3)
            rsqrt_step(link, d_var, d_rstd, d_wn)
            dve.wait_ge(kept, 16 * (NT // KEEP))
            for t in range(NT):
                ins = nc.vector.tensor_scalar(x_all[:, t, :], x_all[:, t, :], d_mv[:, t, 0:1], d_rstd[:, t:t + 1],
                                              ALU.subtract, ALU.mult)
            link(ins)
            front_tokens(dve, 0)
            front_split(dve, 0, link)
            dve.wait_ge(loaded_ff, 16 * LOADS_FF + 1)
            for j in range(TPS):
                front_sums(dve, 0, j, link)
                front_norm(dve, 0, j, link)
                front_cos(dve, 0, j)
            front_tokens(dve, 1)
            front_split(dve, 1, link)
            softmax_max(dve, 0, 0, link)
            softmax_prob(dve, 0, 0, link)
            front_sums(dve, 1, 0, link)
            front_norm(dve, 1, 0, link)
            front_cos(dve, 1, 0)
            before = link.n
            with dve.Fori(0, LAYERS) as layer:
                link = Chain(dve, d_chain, 1 + SEQS * D_LINKS, layer)
                link.base = link.base + before
                split_weights(dve, layer + 1, link)
                with dve.Fori(0, SEQS) as b:
                    n = layer * SEQS + b
                    link = Chain(dve, d_chain, D_LINKS, n)
                    link.base = link.base + (layer + 1 + before)
                    softmax_max(dve, n, 1, link)
                    front_sums(dve, n + 1, 1, link)
                    softmax_prob(dve, n, 1, link)
                    front_norm(dve, n + 1, 1, link)
                    front_tokens(dve, n + 2)
                    ffn_centre(dve, n, link)
                    ffn_variance(dve, n)
                    residual(dve, n, 0)
                    front_cos(dve, n + 1, 1, (0,))
                    ffn_norm(dve, n, link, ffn_loaded(n))
                    front_split(dve, n + 2, link)
                    residual(dve, n, 1)
                    ffn_gate(dve, n, 0)
                    front_cos(dve, n + 1, 1, (1,))
                    ffn_gate(dve, n, 1)
                    ffn_gate(dve, n, 2)
                    softmax_max(dve, n + 1, 0, link)
                    front_sums(dve, n + 2, 0, link, (0,))
                    front_sums(dve, n + 2, 0, link, (1,))
                    softmax_prob(dve, n + 1, 0, link)
                    front_norm(dve, n + 2, 0, link)
                    ffn_residual(dve, n, ffn_tile(n))
                    front_cos(dve, n + 2, 0, (0,))
                    front_cos(dve, n + 2, 0, (1,))
                    link.end()
            link = Chain(dve, d_chain, 0, 0)
            link.base = before + LAYERS + (LAST + 1) * D_LINKS
            ffn_centre(dve, LAST + 1, link)
            ffn_variance(dve, LAST + 1)
            ffn_norm(dve, LAST + 1, link, 16 * LOADS_FF * LAYERS + 1)
            for c in range(NF):
                ffn_gate(dve, LAST + 1, c)
            ffn_residual(dve, LAST + 1, (SEQS - 1) * TPS)
            dve.wait_ge(s_x_done, LAST + 3)

        def add_kept(dve):
            for g in range(NT // KEEP):
                dve.wait_ge(back[g], 16)
                s = slice(g * KEEP, (g + 1) * KEEP)
                nc.vector.tensor_tensor(x_all[:, s, :], x_all[:, s, :], x_kept[:, s, :], ALU.add).then_inc(s_x_done, 1)

        def phase_d_scalar(act):
            def front_xt(f, s):
                act.wait_ge(s_tp, slot_xt(f) + 1)
                at_least(act, s_split, f)
                at_least(act, s_xv, f)
                src = slot_bank(s)
                nc.scalar.activation(d_xt[0:C // 2, :], src[0:C // 2, 0:T], ACT.Copy)
                nc.scalar.activation(d_xt[C // 2:C, 1:], src[C // 2:C, 0:T - 1], ACT.Copy).then_inc(s_tev, 1)

            def front_raw(f, j, chunks):
                i = TPS * f + j
                for c in chunks:
                    act.wait_ge(s_proj, 4 * i + c + 1)
                    if c == 0:
                        at_least(act, s_rope, i - 1)
                    nc.scalar.activation(d_raw[j][:, 8 * c:8 * c + 8, :], bank[c % 2][:, :].rearrange("p (h d) -> p h d", h=8),
                                         ACT.Copy).then_inc(s_raw, 1)

            def front_sq(f, j):
                i = TPS * f + j
                act.wait_ge(s_raw, 4 * i + 4)
                at_least(act, s_ss, i)
                nc.scalar.activation(d_sq, d_raw[j], ACT.Square).then_inc(s_sq, 1)

            def front_rsqrt(f, j):
                i = TPS * f + j
                act.wait_ge(s_ss, i + 1)
                nc.scalar.activation(d_y, d_ss, ACT.Ln).then_inc(d_act_chain, 1)
                act.wait_ge(d_act_chain, i + 1)
                nc.scalar.activation(d_y, d_y, ACT.Exp, scale=-0.5).then_inc(s_y, 1)

            def front_queries(f, j):
                at_least(act, s_s, 2 * TPS * f)
                for q in range(2):
                    act.wait_ge(s_tp, slot_of(f - 1, QK[j] + q) + 1)
                    nc.scalar.activation(d_q[:, 4 * q:4 * q + 4, j * P:(j + 1) * P],
                                         slot_bank(QK[j] + q)[:, :].rearrange("p (a t) -> p a t", a=4), ACT.Copy).then_inc(s_tev, 1)

            def front_keys(f, j):
                at_least(act, s_s, 2 * TPS * f)
                at = WIN + j * P
                for q in range(2):
                    act.wait_ge(s_tp, slot_of(f - 1, QK[j] + 2 + q) + 1)
                    src = slot_bank(QK[j] + 2 + q)[:, :].rearrange("p (a t) -> p a t", a=4)
                    nc.scalar.activation(d_k[0:DH, 4 * q:4 * q + 4, 0, at:at + P], src[0:DH], ACT.Copy)
                    nc.scalar.activation(d_k[DH:P, 4 * q:4 * q + 4, 1, at:at + P], src[DH:P], ACT.Copy).then_inc(s_tev, 1)

            def softmax_exp(n, j):
                act.wait_ge(s_sub, TPS * n + j + 2)
                nc.scalar.activation(d_e[j], d_e[j], ACT.Exp, scale=8.0).then_inc(s_exp, 1)

            def probabilities(n, j):
                for q in range(2):
                    act.wait_ge(s_tp, slot_of(n, PT[j] + q) + 1)
                    act.wait_ge(s_acc, TPS * n + j + 1)
                    nc.scalar.activation(d_pt[:, q, :, :], slot_bank(PT[j] + q)[:, :].rearrange("p (a q) -> p a q", a=QUADS),
                                         ACT.Copy).then_inc(s_tev, 1)

            def token_products(n, windows):
                act.wait_ge(s_acc, TPS * n + 1)
                for w in windows:
                    act.wait_ge(s_u, NW * n + w + 1)
                    nc.scalar.activation(d_u[:, 1 + w, :, :], bank[6 + w % 2][:, :].rearrange("p (a c) -> p a c", a=QUADS),
                                         ACT.Copy).then_inc(s_uev, 1)

            def ffn_tokens(n):
                act.wait_ge(s_tp, slot_of(n, x2_slot(n)) + 1)
                src = slot_bank(X2)
                nc.scalar.activation(d_xf[0:C // 2, :], src[0:C // 2, 0:T], ACT.Copy)
                nc.scalar.activation(d_xf[C // 2:C, 1:], src[C // 2:C, 0:T - 1], ACT.Copy).then_inc(s_tev, 1)

            def ffn_rsqrt(n):
                act.wait_ge(s_var, n + 1)
                nc.scalar.activation(d_r, d_v, ACT.Ln).then_inc(s_ln, 1)
                act.wait_ge(s_ln, n + 1)
                nc.scalar.activation(d_r, d_r, ACT.Exp, scale=-0.5).then_inc(s_y2, 1)

            def ffn_gelu(n, c):
                m = FBLK[c]
                act.wait_ge(s_up, NF * n + c + 1)
                if c >= 2:
                    act.wait_ge(s_h, NF * n + c - 1)
                nc.scalar.activation(d_gl[0:m, c % 2, :], bank[2 + c % 2][0:m, 0:T], ACT.Gelu,
                                     bias=cols_d[0:m, 2 + NF + c:3 + NF + c]).then_inc(s_gl, 1)

            act.wait_ge(d_zero, ZEROS)
            act.wait_ge(d_stats, 1)
            nc.scalar.activation(d_rstd, d_var, ACT.Ln).then_inc(d_stats, 1)
            act.wait_ge(d_stats, 2)
            nc.scalar.activation(d_rstd, d_rstd, ACT.Exp, scale=-0.5).then_inc(d_stats, 1)
            front_xt(0, 0)
            for j in range(TPS):
                front_raw(0, j, range(4))
                front_sq(0, j)
                front_rsqrt(0, j)
            front_xt(1, XT)
            front_queries(0, 0)
            front_keys(0, 0)
            front_raw(1, 0, range(2))
            front_raw(1, 0, range(2, 4))
            front_sq(1, 0)
            front_queries(0, 1)
            softmax_exp(0, 0)
            front_keys(0, 1)
            front_rsqrt(1, 0)
            front_raw(1, 1, range(4))
            front_sq(1, 1)
            with act.Fori(0, LAYERS) as layer:
                for g in range(4):
                    act.wait_ge(s_m, 4 * layer + g + 1)
                    into = m_vo[:, :, :].rearrange("p (b odd g a) c -> p odd g a b c", b=2, odd=2, g=2)
                    src = bank[6 + g % 2][:, :].rearrange("p (a b c) -> p a b c", a=2, b=2)
                    nc.scalar.activation(into[:, g % 2, g // 2], src, ACT.Copy).then_inc(s_m_ready, 1)
                with act.Fori(0, SEQS) as b:
                    n = layer * SEQS + b
                    token_products(n, range(0, 2))
                    probabilities(n, 0)
                    token_products(n, range(2, 4))
                    softmax_exp(n, 1)
                    front_rsqrt(n + 1, 1)
                    ffn_tokens(n)
                    token_products(n, range(4, 6))
                    probabilities(n, 1)
                    token_products(n, range(6, 8))
                    front_xt(n + 2, XT)
                    ffn_rsqrt(n)
                    nc.scalar.preload_act_table(ACT.Gelu)
                    front_queries(n + 1, 0)
                    front_keys(n + 1, 0)
                    ffn_gelu(n, 0)
                    ffn_gelu(n, 1)
                    front_raw(n + 2, 0, range(2))
                    ffn_gelu(n, 2)
                    front_raw(n + 2, 0, range(2, 4))
                    nc.scalar.preload_act_table_set(EXP_SET)
                    front_sq(n + 2, 0)
                    front_queries(n + 1, 1)
                    softmax_exp(n + 1, 0)
                    front_keys(n + 1, 1)
                    front_rsqrt(n + 2, 0)
                    front_raw(n + 2, 1, range(2))
                    front_raw(n + 2, 1, range(2, 4))
                    front_sq(n + 2, 1)
            ffn_tokens(LAST + 1)
            ffn_rsqrt(LAST + 1)
            nc.scalar.preload_act_table(ACT.Gelu)
            for c in range(NF):
                ffn_gelu(LAST + 1, c)

        def phase_d_gpsimd(pool):
            def tables(layer_next):
                par = layer_next & 1
                pool.wait_ge(loaded_sc, 16 * (layer_next + 1))
                half = DH // 2
                for m in range(2):
                    sc = qk_scale[:, m * DH:(m + 1) * DH]
                    nc.gpsimd.tensor_tensor(rope_d[:, bass.ds(par, 1), :, m, :].rearrange("p a t d -> p (a t) d"),
                                            rope[:, :, m, :], sc.unsqueeze(1).to_broadcast([P, TPS, DH]), ALU.mult)
                    for a, z in ((0, half), (half, 0)):
                        last = nc.gpsimd.tensor_tensor(
                            rope_d[:, bass.ds(par, 1), :, 2 + m, a:a + half].rearrange("p a t d -> p (a t) d"),
                            rope[:, :, 2 + m, a:a + half], sc[:, z:z + half].unsqueeze(1).to_broadcast([P, TPS, half]), ALU.mult)
                last.then_inc(s_tab, 1)

            def rotate(f, j):
                i = TPS * f + j
                par = layer_of(f) & 1
                half = DH // 2
                pool.wait_ge(s_tab, layer_of(f) + 1)
                at_least(pool, s_rope, i)
                pool.wait_ge(s_norm, i + 1)
                for m in range(2):
                    for a, z in ((0, half), (half, 0)):
                        last = nc.gpsimd.tensor_tensor(
                            d_t2[:, m * H:(m + 1) * H, a:a + half], d_raw[j][:, m * H:(m + 1) * H, z:z + half],
                            rope_d[:, bass.ds(par, 1), j, 2 + m, a:a + half].to_broadcast([P, H, half]), ALU.mult)
                last.then_inc(d_pool_chain, 1)
                pool.wait_ge(d_pool_chain, i + 1)
                pool.wait_ge(s_t1, 2 * i + 2)
                nc.gpsimd.tensor_tensor(d_rot[j], d_rot[j], d_t2, ALU.add).then_inc(s_rope, 1)

            def keep_tokens(f):
                if isinstance(f, int):
                    pool.wait_ge(s_tev, 1)
                else:
                    read(pool, f - 2, XT)
                    pool.wait_ge(s_u, NW * f)
                zeros = d_u[:, 0].rearrange("p a c -> p (a c)")[:, 0:T]
                nc.gpsimd.tensor_tensor(d_xv, d_xt, zeros, ALU.add).then_inc(s_xv, 1)

            pool.wait_ge(d_zero, ZEROS)
            tables(0)
            keep_tokens(0)
            for j in range(TPS):
                rotate(0, j)
            rotate(1, 0)
            with pool.Fori(0, LAYERS) as layer:
                tables(layer + 1)
                with pool.Fori(0, SEQS) as b:
                    n = layer * SEQS + b
                    keep_tokens(n + 1)
                    rotate(n + 1, 1)
                    rotate(n + 2, 0)
        def phase_d_tensor(pe):
            def slot_free(n, s):
                if not (isinstance(n, int) and SLOTS0 + SLOTS * n + s < 3):
                    read(pe, n - 1 if s < 2 else n, (s - 2) % SLOTS)

            def front_xt(f, s):
                pe.wait_ge(s_xs, f + 1)
                if s:
                    slot_free(f - 2, XT)
                for t in range(TPS):
                    last = nc.tensor.transpose(slot_bank(s)[:, t * P:(t + 1) * P], d_xs[:, t, :], ident[:, :])
                last.then_inc(s_tp, 1)

            def front_project(f, j, chunks=range(4)):
                i = TPS * f + j
                par = layer_of(f) & 1
                pe.wait_ge(s_split, f + 1)
                pe.wait_ge(s_wsplit, layer_of(f) + 1)
                for c in chunks:
                    at_least(pe, s_raw, 4 * i + c - 1)
                    if j == 0 and c < 2 and not isinstance(f, int):
                        pe.wait_ge(s_x2, TPS * f + c - 1)
                    for q, (xp, wp) in enumerate(((0, 0), (1, 0), (0, 1))):
                        w = wqk_split[:, bass.ds(par, 1), wp, c * 512:(c + 1) * 512].rearrange("p a n -> p (a n)")
                        last = nc.tensor.matmul(bank[c % 2][:, :], x_split[:, xp, j * P:(j + 1) * P], w,
                                                start=(q == 0), stop=(q == 2))
                    last.then_inc(s_proj, 1)

            def front_transpose(f, j):
                pe.wait_ge(s_rope, TPS * f + j + 1)
                for q in range(4):
                    slot_free(f - 1, QK[j] + q)
                    for a in range(4):
                        h = 2 * (4 * q + a)
                        last = nc.tensor.transpose(slot_bank(QK[j] + q)[:, a * P:(a + 1) * P],
                                                   d_rot[j][:, h:h + 2, :].rearrange("p h d -> p (h d)"), ident[:, :])
                    last.then_inc(s_tp, 1)

            def scores(n, j):
                pe.wait_ge(s_sub, TPS * n + j + 1)
                at_least(pe, s_h, NF * n)
                read(pe, n - 1, QK[j] + 1)
                read(pe, n - 1, QK[j] + 3)
                for b in range(2):
                    nc.tensor.matmul(bank[2 + b][:, :], ident_bf[:, :], mask_bf[:, j, :, :].rearrange("p h k -> p (h k)"),
                                     start=True, stop=True)
                    for a in range(4):
                        for w in range(WPT):
                            at = j * P + w * WIN
                            last = nc.tensor.matmul(bank[2 + b][w * WIN:(w + 1) * WIN, a * P:(a + 1) * P],
                                                    d_q[:, 4 * b + a, at:at + WIN], d_k[:, 4 * b + a, :, at:at + 2 * WIN],
                                                    start=False, stop=True, skip_group_check=True, tile_position=(0, w * WIN))
                    last.then_inc(s_s, 1)

            def probabilities(n, j):
                pe.wait_ge(s_prob, TPS * n + j + 1)
                for q in range(2):
                    slot_free(n, PT[j] + q)
                    for a in range(QUADS):
                        last = nc.tensor.transpose(slot_bank(PT[j] + q)[:, a * P:(a + 1) * P],
                                                   d_e[j][:, q, 4 * a:4 * a + 4, :].rearrange("p h k -> p (h k)"), ident[:, :])
                    last.then_inc(s_tp, 1)

            def token_products(n, windows):
                pe.wait_ge(s_xv, n + 1)
                for w in windows:
                    pe.wait_ge(s_uev, NW * n + w + 1)
                    if w == 0:
                        pe.wait_ge(s_x_done, n + 1)
                    for q in range(4):
                        last = nc.tensor.matmul(bank[6 + w % 2][q * WIN:(q + 1) * WIN, :], d_xv[:, w * WIN:(w + 1) * WIN],
                                                m_vo[:, 4 * q:4 * q + 4, :].rearrange("p a c -> p (a c)"), start=True, stop=True,
                                                tile_position=(0, q * WIN))
                    last.then_inc(s_u, 1)

            def attention(n, j):
                pe.wait_ge(s_uev, NW * n + WPT * (j + 1) + 2)
                read(pe, n, PT[j] + 1)
                pe.wait_ge(s_raw, 8 * n + 15 + j)
                for q in range(2):
                    for a in range(QUADS):
                        for w in range(WPT):
                            last = nc.tensor.matmul(bank[j][w * WIN:(w + 1) * WIN, 0:C], d_pt[:, q, a, w * WIN:(w + 1) * WIN],
                                                    d_u[:, WPT * j + w + q, a, :], start=(q == 0 and a == 0),
                                                    stop=(q == 1 and a == QUADS - 1), skip_group_check=True,
                                                    tile_position=(0, w * WIN))
                last.then_inc(s_acc, 1)

            def ffn_tokens(n):
                pe.wait_ge(s_x2, TPS * n + 2)
                slot_free(n, x2_slot(n))
                for t in range(TPS):
                    last = nc.tensor.transpose(slot_bank(X2)[:, t * P:(t + 1) * P], d_x2[:, t, :], ident[:, :])
                last.then_inc(s_tp, 1)

            def ffn_mean(n):
                pe.wait_ge(s_sub, TPS * n + 3 if not isinstance(n, int) else TPS * n + 2)
                read(pe, n, x2_slot(n))
                nc.tensor.matmul(bank[2][:, 0:T], mean_mat[:, :], d_xf, start=True, stop=True).then_inc(s_mean, 1)

            def ffn_var(n):
                pe.wait_ge(s_xsq, n + 1)
                nc.tensor.matmul(bank[3][:, 0:T], mean_mat[:, :], d_v, start=True, stop=True).then_inc(s_varp, 1)

            def ffn_up(n, c):
                m = FBLK[c]
                if c == 0:
                    pe.wait_ge(s_xn, n + 1)
                else:
                    at_least(pe, s_h, NF * n + c - 1 if c >= 2 else 0)
                for half, first in ((0, FF), (1, 0)):
                    last = nc.tensor.matmul(bank[2 + c % 2][0:m, half * T:(half + 1) * T],
                                            w1[:, first + c * P:first + c * P + m], d_xn, start=True, stop=True)
                last.then_inc(s_up, 1)

            def ffn_down(n):
                pe.wait_ge(s_h, NF * n + NF)
                for t in range(TPS):
                    for c, m in enumerate(FBLK):
                        nc.tensor.matmul(bank[6][:, t * C:(t + 1) * C], d_h[0:m, c, t * P:(t + 1) * P], w2[0:m, c, :],
                                         start=(c == 0), stop=False)
                    last = nc.tensor.matmul(bank[6][:, t * C:(t + 1) * C], ones_row[:, :], b2[:, :], start=False, stop=True)
                last.then_inc(s_ffo, 1)

            pe.wait_ge(d_zero, ZEROS)
            pe.wait_ge(loaded_ff, 16 * LOADS_FF + 1)
            front_xt(0, 0)
            for j in range(TPS):
                front_project(0, j)
            front_xt(1, XT)
            front_transpose(0, 0)
            front_project(1, 0, range(2))
            front_project(1, 0, range(2, 4))
            scores(0, 0)
            front_transpose(0, 1)
            front_project(1, 1)
            scores(0, 1)
            with pe.Fori(0, LAYERS) as layer:
                pe.wait_ge(loaded_vo, 32 * (layer + 1))
                pe.wait_ge(s_x_done, SEQS * layer + 1)
                head_products(pe, wvt, wo, s_m, s_m_ready, 4 * layer, 6)
                with pe.Fori(0, SEQS) as b:
                    n = layer * SEQS + b
                    pe.wait_ge(s_m_ready, 4 * layer + 4)
                    probabilities(n, 0)
                    token_products(n, range(0, 2))
                    token_products(n, range(2, 4))
                    token_products(n, range(4, 6))
                    ffn_tokens(n)
                    attention(n, 0)
                    token_products(n, range(6, 8))
                    ffn_mean(n)
                    probabilities(n, 1)
                    front_xt(n + 2, XT)
                    ffn_var(n)
                    attention(n, 1)
                    front_transpose(n + 1, 0)
                    pe.wait_ge(loaded_ff, ffn_loaded(n))
                    ffn_up(n, 0)
                    ffn_up(n, 1)
                    front_project(n + 2, 0, range(2))
                    ffn_up(n, 2)
                    front_project(n + 2, 0, range(2, 4))
                    scores(n + 1, 0)
                    front_transpose(n + 1, 1)
                    ffn_down(n)
                    front_project(n + 2, 1, range(2))
                    scores(n + 1, 1)
                    front_project(n + 2, 1, range(2, 4))
            ffn_tokens(LAST + 1)
            ffn_mean(LAST + 1)
            ffn_var(LAST + 1)
            pe.wait_ge(loaded_ff, 16 * LOADS_FF * LAYERS + 1)
            for c in range(NF):
                ffn_up(LAST + 1, c)
            ffn_down(LAST + 1)

        def weights_of(name, layer):
            return dram[name][bass.ds(layer % LAYERS, 1)].rearrange("a p n -> (a p) n")

        def load_qk(sp, layer):
            at_least(sp, s_wsplit, layer)
            sp.dma_start(wqk_stage[:, :], weights_of("wqk", layer)).then_inc(loaded_qk, 16)
            at_least(sp, s_tab, layer)
            sp.dma_start(qk_scale[:, :], weights_of("qk_scale", layer).to_broadcast([P, 2 * DH])).then_inc(loaded_sc, 16)

        def load_vo(sp, layer):
            at_least(sp, s_m, 4 * layer)
            sp.dma_start(wvt[:, :, :], weights_of("wvt", layer).rearrange("(a p) c -> p a c", p=P)).then_inc(loaded_vo, 16)
            sp.dma_start(wo[:, :, :], weights_of("wo", layer).rearrange("(a p) c -> p a c", p=P)).then_inc(loaded_vo, 16)

        def load_ff(sp, layer):
            if not isinstance(layer, int):
                sp.wait_ge(s_ffo, SEQS * layer + 1)
            sp.dma_start(w1[:, :], weights_of("w1", layer)).then_inc(loaded_ff, 16)
            full = FF // P
            sp.dma_start(w2[:, 0:full, :], weights_of("w2", layer)[0:full * P, :].rearrange("(b p) c -> p b c", p=P))\
                .then_inc(loaded_ff, 16)
            sp.dma_start(w2[0:FBLK[-1], full, :], weights_of("w2", layer)[full * P:FF, :]).then_inc(loaded_ff, 16)
            sp.dma_start(cols_d[:, :], weights_of("cols_d", layer)).then_inc(loaded_ff, 16)
            sp.dma_start(b2[:, :], weights_of("b2", layer)).then_inc(loaded_ff, 16)

        block = ctx.enter_context(nc.Block())

        @block.sync
        def _(sp):
            sp.dma_start(x_all[:, 0:NT, :], dram["x"].rearrange("n p c -> p n c")).then_inc(loaded_x, 16)
            sp.dma_start(cols_a, dram["cols_a"]).then_inc(loaded_a, 16)
            sp.dma_start(ident[:, :], dram["ident"]).then_inc(loaded_const, 16)
            sp.dma_start(wa, dram["wa"]).then_inc(loaded_a, 16)
            sp.dma_start(wcv, dram["wcv"].rearrange("(b p) c -> p b c", p=P)).then_inc(loaded_a, 16)
            sp.dma_start(mask_stage, dram["mask"].rearrange("t p k -> p t k")).then_inc(loaded_const, 16)
            for k in range(4):
                sp.dma_start(rope[:, :, k, :], dram["rope"][k].rearrange("(t p) d -> p t d", p=P)).then_inc(loaded_const, 16)
            sp.dma_start(cols_b, dram["cols_b"]).then_inc(loaded_b, 16)
            sp.dma_start(wb1, dram["wb1"]).then_inc(loaded_b, 16)
            sp.dma_start(wbh, dram["wbh"].rearrange("l (b p) n -> p l b n", p=P)).then_inc(loaded_b, 16)
            sp.dma_start(wb3, dram["wb3"].rearrange("(b p) c -> p b c", p=P)).then_inc(loaded_b, 16)
            sp.dma_start(wqt_c, dram["wqt_c"].rearrange("(a p) c -> p a c", p=P)).then_inc(loaded_c, 16)
            sp.dma_start(wkt_c, dram["wkt_c"].rearrange("(a p) c -> p a c", p=P)).then_inc(loaded_c, 16)
            sp.dma_start(wvt[:, :, :], dram["wvt_c"].rearrange("(a p) c -> p a c", p=P)).then_inc(loaded_c, 16)
            sp.dma_start(wo[:, :, :], dram["wo_c"].rearrange("(a p) c -> p a c", p=P)).then_inc(loaded_c, 16)
            sp.dma_start(bo[:, :], dram["bo"]).then_inc(loaded_c, 16)
            sp.wait_ge(const_ready, CONSTS)
            sp.wait_ge(loaded_c, LOADS_C * 16)
            sp.wait_ge(c_m, 4)
            load_qk(sp, 0)
            load_vo(sp, 0)
            load_ff(sp, 0)
            sp.wait_ge(phase_end, 4 * 3)
            for g in range(NT // KEEP):
                s = slice(g * KEEP, (g + 1) * KEEP)
                sp.dma_start(out[s].rearrange("n p c -> p n c"), x_all[:, s, :]).then_inc(kept, 16)
            load_qk(sp, 1)
            with sp.Fori(0, LAYERS) as layer:
                load_vo(sp, layer + 1)
                load_qk(sp, layer + 2)
                load_ff(sp, layer + 1)
            sp.wait_ge(loaded_x, 16)
            sp.wait_ge(loaded_qk, 16 * (LAYERS + 2))
            sp.wait_ge(loaded_sc, 16 * (LAYERS + 2))
            sp.wait_ge(loaded_vo, 32 * (LAYERS + 1))
            sp.wait_ge(loaded_ff, 16 * LOADS_FF * (LAYERS + 1) + 1)
            sp.wait_ge(phase_end, 4 * PHASES)
            sp.wait_ge(kept, 16 * (NT // KEEP))
            for g in range(NT // KEEP):
                s = slice(g * KEEP, (g + 1) * KEEP)
                sp.dma_start(x_kept[:, s, :], out[s].rearrange("n p c -> p n c")).then_inc(back[g], 16)
            for g in range(NT // KEEP):
                s = slice(g * KEEP, (g + 1) * KEEP)
                sp.wait_ge(s_x_done, LAST + 4 + g)
                sp.dma_start(out[s].rearrange("n p c -> p n c"), x_all[:, s, :]).then_inc(stored, 16)
            sp.wait_ge(stored, 16 * (NT // KEEP))
            sp.wait_ge(loaded_a, LOADS_A * 16)
            sp.wait_ge(loaded_b, LOADS_B * 16)
            sp.wait_ge(loaded_c, LOADS_C * 16)

        @block.vector
        def _(dve):
            dve.wait_ge(loaded_const, LOADS_CONST * 16)
            nc.vector.tensor_copy(ident_bf[:, :], ident[:, :]).then_inc(const_ready, 1)
            for t in range(TPS):
                nc.vector.tensor_copy(mask_bf[:, t, :, :], mask_stage[:, t, :].unsqueeze(1).to_broadcast([P, 8, 2 * WIN]))\
                    .then_inc(const_ready, 1)
            nc.vector.memset(ones_row[:, :], 1.0).then_inc(const_ready, 1)
            nc.vector.memset(mean_mat[:, :], 1.0 / C).then_inc(const_ready, 1)
            dve.wait_ge(loaded_x, 16)
            phase_a_vector_start(dve)
            with dve.Fori(0, SA) as step:
                phase_a_vector_steps(dve, step)
            end_phase(dve, 1)
            nc.vector.memset(b_w[:, :NT // 2], 0.0).then_inc(b_x_done, 1)
            nc.vector.memset(b_w[:, NT // 2:], 0.0).then_inc(b_down, 1)
            phase_b_vector(dve)
            end_phase(dve, 2)
            phase_c_vector(dve)
            end_phase(dve, 3)
            phase_d_vector(dve)
            end_phase(dve, 4)
            add_kept(dve)

        @block.scalar
        def _(act):
            nc.scalar.preload_act_table_set(EXP_SET)
            act.wait_ge(const_ready, CONSTS)
            act.wait_ge(loaded_a, LOADS_A * 16)
            with act.Fori(0, SA) as step:
                phase_a_scalar_steps(act, step)
            end_phase(act, 1)
            phase_b_scalar(act)
            end_phase(act, 2)
            nc.scalar.preload_act_table_set(EXP_SET)
            phase_c_scalar(act)
            end_phase(act, 3)
            nc.scalar.preload_act_table_set(EXP_SET)
            phase_d_scalar(act)
            end_phase(act, 4)

        @block.gpsimd
        def _(pool):
            with pool.Fori(0, SA) as step:
                phase_a_gpsimd_steps(pool, step)
            end_phase(pool, 1)
            end_phase(pool, 2)
            end_phase(pool, 3)
            phase_d_gpsimd(pool)
            end_phase(pool, 4)

        @block.tensor
        def _(pe):
            pe.wait_ge(const_ready, CONSTS)
            pe.wait_ge(loaded_const, LOADS_CONST * 16)
            pe.wait_ge(loaded_a, LOADS_A * 16)
            with pe.Fori(0, SA) as step:
                phase_a_tensor_steps(pe, step)
            end_phase(pe, 1)
            phase_b_tensor(pe)
            end_phase(pe, 2)
            phase_c_tensor(pe)
            end_phase(pe, 3)
            phase_d_tensor(pe)
            end_phase(pe, 4)


def rope_tables():
    import numpy as np

    half = np.arange(0, DH, 2, dtype=np.float32)
    inv_freq = (np.float32(1.0) / np.float32(10000.0) ** (half / np.float32(DH))).astype(np.float32)
    t = np.arange(T, dtype=np.float32)
    freqs = (t[:, None] * inv_freq[None, :]).astype(np.float32)
    freqs = np.concatenate([freqs, freqs], -1)
    base = ((half + np.float32(0.4 * DH)) / np.float32(1.4 * DH)).astype(np.float32)
    power = ((t - T // 2) / np.float32(WIN // 2)).astype(np.float32)
    scale = (base[None, :] ** power[:, None]).astype(np.float32)
    scale = np.concatenate([scale, scale], -1)
    sign = np.concatenate([-np.ones(DH // 2), np.ones(DH // 2)]).astype(np.float32)
    cos, sin = np.cos(freqs), np.sin(freqs) * sign
    inv = np.float32(1.0) / scale
    return np.stack([cos * scale, cos * inv, sin * scale, sin * inv]).astype(np.float32)


def window_masks():
    import numpy as np

    out = np.zeros((TPS, P, 2 * WIN), np.float32)
    r, k = np.arange(P) % WIN, np.arange(2 * WIN)
    banned = (k[None, :] - WIN > r[:, None]) | (r[:, None] > k[None, :])
    out[:] = np.where(banned, np.float32(MASKED), np.float32(0.0))
    out[0, :WIN, :WIN] = np.float32(MASKED)
    return out


def laid_out(inp):
    import numpy as np

    a = {k: np.asarray(v) for k, v in inp.items()}
    f = np.float32

    def block_cols(v):
        n = -(-v.shape[-1] // P)
        z = np.zeros(v.shape[:-1] + (n * P,), f)
        z[..., : v.shape[-1]] = v
        return np.swapaxes(z.reshape(v.shape[:-1] + (n, P)), -1, -2)

    d = {}
    d["x"] = a["L0_attn_x"].reshape(NT, P, C)
    d["ident"] = np.eye(P, dtype=f)
    d["mask"] = window_masks()
    d["rope"] = rope_tables()
    d["wa"] = np.concatenate([a["L0_attn_" + n].T for n in ("Wk", "Wv", "Wr", "Wcr", "Wck")], 1)
    d["wcv"] = a["L0_attn_Wcv"].T
    d["cols_a"] = np.stack([a["L0_attn_" + n].reshape(C) for n in
                            ("time_shift", "time_first", "ln1_w", "ln1_b", "ln2_w", "ln2_b")], 1)
    d["wb1"] = np.concatenate([a["L0_ffn_w1_w"].T, a["L0_ffn_w2_w"].T], 1)
    d["wbh"] = np.stack([a["L0_ffn_h1_w"].T, a["L0_ffn_h2_w"].T])
    d["wb3"] = a["L0_ffn_w3_w"].T
    d["cols_b"] = np.concatenate([block_cols(a["L0_ffn_" + n]) for n in ("w1_s", "w2_s", "h1_s", "h2_s", "w3_s")], 1)
    d["wqt_c"] = a["L1_attn_Wq"].T
    d["wkt_c"] = a["L1_attn_Wk"].T
    d["wvt_c"] = a["L1_attn_Wv"].T
    d["wo_c"] = a["L1_attn_Wo"]
    d["bo"] = a["L1_attn_bo"].reshape(1, C)
    w = a["L1_ffn_Wqkv"]
    d["wqk"] = w[:, :, : 2 * INNER]
    d["wvt"] = np.swapaxes(w[:, :, 2 * INNER:], 1, 2)
    d["wo"] = a["L1_ffn_Wo"]
    d["qk_scale"] = np.concatenate([a["L1_ffn_q_scale"], a["L1_ffn_k_scale"]], 1).reshape(LAYERS, 1, 2 * DH)
    d["w1"] = a["L1_ffn_W1"]
    d["w2"] = a["L1_ffn_W2"]
    b1 = a["L1_ffn_b1"]
    d["cols_d"] = np.concatenate([a["L1_ffn_ln_g"][..., None], a["L1_ffn_ln_b"][..., None],
                                  block_cols(b1[:, :FF]), block_cols(b1[:, FF:])], 2)
    d["b2"] = a["L1_ffn_b2"].reshape(LAYERS, 1, C)
    return {k: np.ascontiguousarray(v) for k, v in d.items()}


def kernel(**inputs):
    import concourse.bacc as bacc
    from concourse.bass_utils import run_bass_kernel_spmd

    nc = bacc.Bacc("TRN2", target_bir_lowering=False, num_devices=1)
    arrays, dram = {}, {}
    for name, a in laid_out(inputs).items():
        arrays[f"in_{name}"] = a
        dram[name] = nc.dram_tensor(f"in_{name}", a.shape, mybir.dt.from_np(a.dtype), kind="ExternalInput").ap()
    out = nc.dram_tensor("out_x", (NT, P, C), F32, kind="ExternalOutput").ap()
    build(nc, dram, out)
    r = run_bass_kernel_spmd(nc, [arrays], core_ids=[0])
    return r.results[0]["out_x"].reshape(SEQS, T, C)
```
